# Optimizing a Trainium2 kernel written in Bass

```python
import numpy as np
import jax
import jax.numpy as jnp

def _softmax(x, axis=-1):
    return jax.nn.softmax(x, axis=axis)

def _gelu(x):
    return jax.nn.gelu(x, approximate=True)

def _silu(x):
    return jax.nn.silu(x)

def _sigmoid(x):
    return jax.nn.sigmoid(x)

def _layernorm(x, axis=-1, eps=1e-05):
    m = jnp.mean(x, axis=axis, keepdims=True)
    v = jnp.var(x, axis=axis, keepdims=True)
    return (x - m) / jnp.sqrt(v + eps)

def _scatter_add(tgt, idx, src, axis=0):
    return tgt.at[idx].add(src)

def _segment_sum(src, seg, n):
    return jax.ops.segment_sum(src, seg, n)
kernel_name = 'mk_prb_d2_jaxref_r4_2d0a06'

def setup_inputs(seed: int=0):
    np.random.seed(seed)
    _w = jnp.asarray

    def _L0_attn_setup():
        import jax, jax.numpy as jnp
        import numpy as np
        from jax import lax
        D_MODEL = 256
        D_INNER = 512
        D_STATE = 16
        D_CONV = 4
        DT_RANK = 64
        N_LAYERS = 1
        EPS = 1e-05

        def _selective_scan(u, delta, A, B, C, Dp):

            def step(h, xs):
                d_t, B_t, C_t, u_t = xs
                dA = jnp.exp(d_t[..., None] * A)
                dBu = d_t[..., None] * B_t[:, None, :] * u_t[..., None]
                h = dA * h + dBu
                y_t = jnp.einsum('bdn,bn->bd', h, C_t)
                return (h, y_t)
            b = u.shape[0]
            h0 = jnp.zeros((b, D_INNER, D_STATE), u.dtype)
            xs = (delta.transpose(1, 0, 2), B.transpose(1, 0, 2), C.transpose(1, 0, 2), u.transpose(1, 0, 2))
            _, ys = lax.scan(step, h0, xs)
            y = ys.transpose(1, 0, 2)
            return y + u * Dp

        def _mamba_block(x, in_proj_w, conv_w, conv_b, x_proj_w, dt_proj_w, dt_proj_b, A_log, Dp, out_proj_w):
            b, l, _ = x.shape
            xz = x @ in_proj_w.T
            xm, res = jnp.split(xz, 2, axis=-1)
            xm_bdl = xm.transpose(0, 2, 1)
            conv = lax.conv_general_dilated(xm_bdl, conv_w, window_strides=(1,), padding=[(D_CONV - 1, 0)], feature_group_count=D_INNER, dimension_numbers=('NCH', 'OIH', 'NCH'))
            xm = jax.nn.silu((conv + conv_b[None, :, None]).transpose(0, 2, 1))
            x_dbl = xm @ x_proj_w.T
            dt, Bm, Cm = jnp.split(x_dbl, [DT_RANK, DT_RANK + D_STATE], axis=-1)
            delta = jax.nn.softplus(dt @ dt_proj_w.T + dt_proj_b)
            A = -jnp.exp(A_log)
            y = _selective_scan(xm, delta, A, Bm, Cm, Dp)
            y = y * jax.nn.silu(res)
            return y @ out_proj_w.T
        key = jax.random.key(seed)
        ks = jax.random.split(key, 16)
        s = lambda fan_in: 1.0 / np.sqrt(fan_in)
        inp = {'seq_embeddings': jax.random.normal(ks[0], (8, 256, D_MODEL), jnp.float32), 'in_proj_w': jax.random.normal(ks[1], (2 * D_INNER, D_MODEL), jnp.float32) * s(D_MODEL), 'conv_w': jax.random.normal(ks[2], (D_INNER, 1, D_CONV), jnp.float32) * s(D_CONV), 'conv_b': jax.random.normal(ks[3], (D_INNER,), jnp.float32) * 0.01, 'x_proj_w': jax.random.normal(ks[4], (DT_RANK + 2 * D_STATE, D_INNER), jnp.float32) * s(D_INNER), 'dt_proj_w': jax.random.normal(ks[5], (D_INNER, DT_RANK), jnp.float32) * s(DT_RANK), 'dt_proj_b': jax.random.normal(ks[6], (D_INNER,), jnp.float32) * 0.01, 'A_log': jnp.log(jnp.tile(jnp.arange(1.0, D_STATE + 1.0, dtype=jnp.float32), (D_INNER, 1))), 'D': jnp.ones((D_INNER,), jnp.float32), 'out_proj_w': jax.random.normal(ks[7], (D_MODEL, D_INNER), jnp.float32) * s(D_INNER), 'ffn_w1': jax.random.normal(ks[8], (4 * D_MODEL, D_MODEL), jnp.float32) * s(D_MODEL), 'ffn_b1': jnp.zeros((4 * D_MODEL,), jnp.float32), 'ffn_w2': jax.random.normal(ks[9], (D_MODEL, 4 * D_MODEL), jnp.float32) * s(4 * D_MODEL), 'ffn_b2': jnp.zeros((D_MODEL,), jnp.float32)}
        return inp
    _L0_attn_in = _L0_attn_setup()

    def _L0_ffn_setup():
        import jax, jax.numpy as jnp
        import numpy as np
        NUM_EXPERTS = 8
        TOP_K = 2
        HIDDEN = 256
        INTER_TOTAL = 2048
        B, S = (2, 512)
        key = jax.random.key(seed)
        k1, k2, k3, k4, k5, k6 = jax.random.split(key, 6)
        T = B * S
        x = jax.random.normal(k1, (B, S, HIDDEN), dtype=jnp.float32)
        scores = jax.random.uniform(k2, (T, NUM_EXPERTS), dtype=jnp.float32)
        expert_weights = jax.random.uniform(k3, (T, TOP_K), dtype=jnp.float32)
        top_experts = jax.random.randint(k4, (T, TOP_K), 0, NUM_EXPERTS, dtype=jnp.int32)
        w1 = jax.random.normal(k5, (HIDDEN, INTER_TOTAL), dtype=jnp.float32) * 0.02
        w2 = jax.random.normal(k6, (INTER_TOTAL, HIDDEN), dtype=jnp.float32) * 0.02
        return {'x': x, 'scores': scores, 'expert_weights': expert_weights, 'top_experts': top_experts, 'w1': w1, 'w2': w2}
    _L0_ffn_in = _L0_ffn_setup()

    def _L1_attn_setup():
        import jax, jax.numpy as jnp
        import numpy as np
        from itertools import combinations
        B, T, D = (2, 512, 256)
        H, PD = (16, 4)
        DH = D // H
        PAIRS = list(combinations(range(PD), 2))
        _J6 = jnp.array([[0, 0, 0, 0, 0, 1], [0, 0, 0, 0, -1, 0], [0, 0, 0, 1, 0, 0], [0, 0, 1, 0, 0, 0], [0, -1, 0, 0, 0, 0], [1, 0, 0, 0, 0, 0]], dtype=jnp.float32)

        def exterior(p1, p2):
            parts = [p1[..., i] * p2[..., j] - p1[..., j] * p2[..., i] for i, j in PAIRS]
            L = jnp.stack(parts, axis=-1)
            n = jnp.maximum(jnp.linalg.norm(L, axis=-1, keepdims=True), 1e-12)
            return L / n
        key = jax.random.key(seed)
        ks = jax.random.split(key, 16)
        s = 0.02
        inp = {'x': jax.random.normal(ks[0], (B, T, D), jnp.float32), 'qkv_w': jax.random.normal(ks[1], (D, 3 * D), jnp.float32) * s, 'qkv_b': jnp.zeros((3 * D,), jnp.float32), 'w1_write': jax.random.normal(ks[2], (D, PD * H), jnp.float32) * s, 'w2_write': jax.random.normal(ks[3], (D, PD * H), jnp.float32) * s, 'w1_read': jax.random.normal(ks[4], (D, PD * H), jnp.float32) * s, 'w2_read': jax.random.normal(ks[5], (D, PD * H), jnp.float32) * s, 'memv_w': jax.random.normal(ks[6], (D, D), jnp.float32) * s, 'memv_b': jnp.zeros((D,), jnp.float32), 'memg_w': jax.random.normal(ks[7], (D, H), jnp.float32) * s, 'memg_b': jnp.zeros((H,), jnp.float32), 'mem_scale': jnp.full((H,), 0.1, jnp.float32), 'out_w': jax.random.normal(ks[8], (D, D), jnp.float32) * s, 'out_b': jnp.zeros((D,), jnp.float32), 'J': _J6, 'decays': jnp.array([0.95] * (H // 2) + [0.999] * (H - H // 2), jnp.float32)}
        return inp
    _L1_attn_in = _L1_attn_setup()

    def _L1_ffn_setup():
        import jax, jax.numpy as jnp
        import numpy as np
        LORA_DIM = 16
        LORA_TOKEN_INDEX = 1
        B, S, D, H = (4, 512, 256, 1024)
        key = jax.random.key(seed)
        ks = jax.random.split(key, 6)
        x = jax.random.normal(ks[0], (B, S, D), dtype=jnp.float32)
        W1 = jax.random.normal(ks[1], (H, D), dtype=jnp.float32) * 0.02
        b1 = jnp.zeros((H,), dtype=jnp.float32)
        W2 = jax.random.normal(ks[2], (D, H), dtype=jnp.float32) * 0.02
        b2 = jnp.zeros((D,), dtype=jnp.float32)
        scale = jnp.asarray(0.001, dtype=jnp.float32)
        return {'x': x, 'W1': W1, 'b1': b1, 'W2': W2, 'b2': b2, 'scale': scale}
    _L1_ffn_in = _L1_ffn_setup()
    _d = {'L0_attn_seq_embeddings': _L0_attn_in['seq_embeddings'], 'L0_attn_in_proj_w': _L0_attn_in['in_proj_w'], 'L0_attn_conv_w': _L0_attn_in['conv_w'], 'L0_attn_conv_b': _L0_attn_in['conv_b'], 'L0_attn_x_proj_w': _L0_attn_in['x_proj_w'], 'L0_attn_dt_proj_w': _L0_attn_in['dt_proj_w'], 'L0_attn_dt_proj_b': _L0_attn_in['dt_proj_b'], 'L0_attn_A_log': _L0_attn_in['A_log'], 'L0_attn_D': _L0_attn_in['D'], 'L0_attn_out_proj_w': _L0_attn_in['out_proj_w'], 'L0_attn_ffn_w1': _L0_attn_in['ffn_w1'], 'L0_attn_ffn_b1': _L0_attn_in['ffn_b1'], 'L0_attn_ffn_w2': _L0_attn_in['ffn_w2'], 'L0_attn_ffn_b2': _L0_attn_in['ffn_b2'], 'L0_ffn_scores': _L0_ffn_in['scores'], 'L0_ffn_expert_weights': _L0_ffn_in['expert_weights'], 'L0_ffn_top_experts': _L0_ffn_in['top_experts'], 'L0_ffn_w1': _L0_ffn_in['w1'], 'L0_ffn_w2': _L0_ffn_in['w2'], 'L1_attn_qkv_w': _L1_attn_in['qkv_w'], 'L1_attn_qkv_b': _L1_attn_in['qkv_b'], 'L1_attn_w1_write': _L1_attn_in['w1_write'], 'L1_attn_w2_write': _L1_attn_in['w2_write'], 'L1_attn_w1_read': _L1_attn_in['w1_read'], 'L1_attn_w2_read': _L1_attn_in['w2_read'], 'L1_attn_memv_w': _L1_attn_in['memv_w'], 'L1_attn_memv_b': _L1_attn_in['memv_b'], 'L1_attn_memg_w': _L1_attn_in['memg_w'], 'L1_attn_memg_b': _L1_attn_in['memg_b'], 'L1_attn_mem_scale': _L1_attn_in['mem_scale'], 'L1_attn_out_w': _L1_attn_in['out_w'], 'L1_attn_out_b': _L1_attn_in['out_b'], 'L1_attn_J': _L1_attn_in['J'], 'L1_attn_decays': _L1_attn_in['decays'], 'L1_ffn_W1': _L1_ffn_in['W1'], 'L1_ffn_b1': _L1_ffn_in['b1'], 'L1_ffn_W2': _L1_ffn_in['W2'], 'L1_ffn_b2': _L1_ffn_in['b2'], 'L1_ffn_scale': _L1_ffn_in['scale']}
    _x0 = _d['L0_attn_seq_embeddings']
    _d['L0_attn_seq_embeddings'] = jax.random.normal(jax.random.fold_in(jax.random.key(seed), 1), (8, 1024, 256), dtype=_x0.dtype)
    del _x0
    return _d

def reference(L0_attn_seq_embeddings, L0_attn_in_proj_w, L0_attn_conv_w, L0_attn_conv_b, L0_attn_x_proj_w, L0_attn_dt_proj_w, L0_attn_dt_proj_b, L0_attn_A_log, L0_attn_D, L0_attn_out_proj_w, L0_attn_ffn_w1, L0_attn_ffn_b1, L0_attn_ffn_w2, L0_attn_ffn_b2, L0_ffn_scores, L0_ffn_expert_weights, L0_ffn_top_experts, L0_ffn_w1, L0_ffn_w2, L1_attn_qkv_w, L1_attn_qkv_b, L1_attn_w1_write, L1_attn_w2_write, L1_attn_w1_read, L1_attn_w2_read, L1_attn_memv_w, L1_attn_memv_b, L1_attn_memg_w, L1_attn_memg_b, L1_attn_mem_scale, L1_attn_out_w, L1_attn_out_b, L1_attn_J, L1_attn_decays, L1_ffn_W1, L1_ffn_b1, L1_ffn_W2, L1_ffn_b2, L1_ffn_scale):

    def _L0_attn_ref(seq_embeddings, in_proj_w, conv_w, conv_b, x_proj_w, dt_proj_w, dt_proj_b, A_log, D, out_proj_w, ffn_w1, ffn_b1, ffn_w2, ffn_b2):
        import jax, jax.numpy as jnp
        import numpy as np
        from jax import lax
        D_MODEL = 256
        D_INNER = 512
        D_STATE = 16
        D_CONV = 4
        DT_RANK = 64
        N_LAYERS = 1
        EPS = 1e-05

        def _selective_scan(u, delta, A, B, C, Dp):

            def step(h, xs):
                d_t, B_t, C_t, u_t = xs
                dA = jnp.exp(d_t[..., None] * A)
                dBu = d_t[..., None] * B_t[:, None, :] * u_t[..., None]
                h = dA * h + dBu
                y_t = jnp.einsum('bdn,bn->bd', h, C_t)
                return (h, y_t)
            b = u.shape[0]
            h0 = jnp.zeros((b, D_INNER, D_STATE), u.dtype)
            xs = (delta.transpose(1, 0, 2), B.transpose(1, 0, 2), C.transpose(1, 0, 2), u.transpose(1, 0, 2))
            _, ys = lax.scan(step, h0, xs)
            y = ys.transpose(1, 0, 2)
            return y + u * Dp

        def _mamba_block(x, in_proj_w, conv_w, conv_b, x_proj_w, dt_proj_w, dt_proj_b, A_log, Dp, out_proj_w):
            b, l, _ = x.shape
            xz = x @ in_proj_w.T
            xm, res = jnp.split(xz, 2, axis=-1)
            xm_bdl = xm.transpose(0, 2, 1)
            conv = lax.conv_general_dilated(xm_bdl, conv_w, window_strides=(1,), padding=[(D_CONV - 1, 0)], feature_group_count=D_INNER, dimension_numbers=('NCH', 'OIH', 'NCH'))
            xm = jax.nn.silu((conv + conv_b[None, :, None]).transpose(0, 2, 1))
            x_dbl = xm @ x_proj_w.T
            dt, Bm, Cm = jnp.split(x_dbl, [DT_RANK, DT_RANK + D_STATE], axis=-1)
            delta = jax.nn.softplus(dt @ dt_proj_w.T + dt_proj_b)
            A = -jnp.exp(A_log)
            y = _selective_scan(xm, delta, A, Bm, Cm, Dp)
            y = y * jax.nn.silu(res)
            return y @ out_proj_w.T
        x = seq_embeddings
        for _ in range(N_LAYERS):
            m = _mamba_block(x, in_proj_w, conv_w, conv_b, x_proj_w, dt_proj_w, dt_proj_b, A_log, D, out_proj_w)
            f = jax.nn.gelu(m @ ffn_w1.T + ffn_b1, approximate=False) @ ffn_w2.T + ffn_b2
            c = m + f
            mu = jnp.mean(c, axis=(1, 2), keepdims=True)
            var = jnp.var(c, axis=(1, 2), keepdims=True)
            x = (c - mu) / jnp.sqrt(var + EPS)
        return x

    def _L0_ffn_ref(x, scores, expert_weights, top_experts, w1, w2):
        import jax, jax.numpy as jnp
        import numpy as np
        NUM_EXPERTS = 8
        TOP_K = 2
        HIDDEN = 256
        INTER_TOTAL = 2048
        B, S = (2, 512)
        in_shape = x.shape
        T = in_shape[0] * in_shape[1]
        H = in_shape[-1]
        x_flat = x.reshape(T, H)
        flat_experts = top_experts.reshape(-1)
        flat_weights = expert_weights.reshape(-1)
        order = jnp.argsort(flat_experts, stable=True)
        token_idx = order // TOP_K
        xg = x_flat[token_idx]
        h = jax.nn.gelu(xg @ w1, approximate=True)
        y = h @ w2
        w_sorted = flat_weights[order]
        out = jnp.zeros((T, H), dtype=x.dtype).at[token_idx].add(w_sorted[:, None] * y)
        return out.reshape(in_shape)

    def _L1_attn_ref(x, qkv_w, qkv_b, w1_write, w2_write, w1_read, w2_read, memv_w, memv_b, memg_w, memg_b, mem_scale, out_w, out_b, J, decays):
        import jax, jax.numpy as jnp
        import numpy as np
        from itertools import combinations
        B, T, D = (2, 512, 256)
        H, PD = (16, 4)
        DH = D // H
        PAIRS = list(combinations(range(PD), 2))
        _J6 = jnp.array([[0, 0, 0, 0, 0, 1], [0, 0, 0, 0, -1, 0], [0, 0, 0, 1, 0, 0], [0, 0, 1, 0, 0, 0], [0, -1, 0, 0, 0, 0], [1, 0, 0, 0, 0, 0]], dtype=jnp.float32)

        def exterior(p1, p2):
            parts = [p1[..., i] * p2[..., j] - p1[..., j] * p2[..., i] for i, j in PAIRS]
            L = jnp.stack(parts, axis=-1)
            n = jnp.maximum(jnp.linalg.norm(L, axis=-1, keepdims=True), 1e-12)
            return L / n
        Bx, Tx, Dx = x.shape
        scale = DH ** (-0.5)
        qkv = (x @ qkv_w + qkv_b).reshape(Bx, Tx, 3, H, DH)
        q, k, v = (qkv[:, :, 0], qkv[:, :, 1], qkv[:, :, 2])
        scores = jnp.einsum('bihd,bjhd->bhij', q, k) * scale
        i = jnp.arange(Tx)
        causal = i[:, None] >= i[None, :]
        scores = jnp.where(causal[None, None], scores, -jnp.inf)
        attn = jax.nn.softmax(scores, axis=-1)
        seq_out = jnp.einsum('bhij,bjhd->bihd', attn, v).reshape(Bx, Tx, Dx)
        x_prev = jnp.concatenate([jnp.zeros((Bx, 1, Dx), x.dtype), x[:, :-1]], axis=1)
        w1 = (x_prev @ w1_write).reshape(Bx, Tx, H, PD)
        w2 = (x @ w2_write).reshape(Bx, Tx, H, PD)
        write_lines = exterior(w1, w2)
        r1 = (x @ w1_read).reshape(Bx, Tx, H, PD)
        r2 = (x @ w2_read).reshape(Bx, Tx, H, PD)
        read_lines = exterior(r1, r2)
        Jw = jnp.einsum('bthi,ij->bthj', write_lines, J)
        incidence = jnp.einsum('bihp,bjhp->bhij', read_lines, Jw)
        inc_sq = incidence ** 2
        diffs = i[:, None] - i[None, :]
        lower = diffs > 0
        dsafe = jnp.where(lower, diffs, 0).astype(x.dtype)
        weights = jnp.where(lower[None], decays[:, None, None] ** dsafe[None], 0.0)
        mem_score = jnp.sum(inc_sq * weights[None], axis=-1)
        mem_val = x @ memv_w + memv_b
        gate = jax.nn.sigmoid(x @ memg_w + memg_b)
        gated = jax.nn.sigmoid(mem_score.transpose(0, 2, 1) * mem_scale[None, None]) * gate
        gated = jnp.mean(gated, axis=-1, keepdims=True)
        return (seq_out + gated * mem_val) @ out_w + out_b

    def _L1_ffn_ref(x, W1, b1, W2, b2, scale):
        import jax, jax.numpy as jnp
        import numpy as np
        LORA_DIM = 16
        LORA_TOKEN_INDEX = 1
        B, S, D, H = (4, 512, 256, 1024)
        Bx, Sx, Dx = x.shape
        Hx = W1.shape[0]
        lt = jax.lax.dynamic_slice_in_dim(x, LORA_TOKEN_INDEX, LORA_DIM, axis=1)
        even = lt[:, ::2, :]
        odd = lt[:, 1::2, :]
        m1 = (even[:, :4, :, None] * odd[:, :4, None, :]).reshape(Bx, Hx, Dx)
        m2 = (even[:, 4:, :, None] * odd[:, 4:, None, :]).reshape(Bx, Dx, Hx)
        h = jnp.einsum('bsd,hd->bsh', x, W1) + scale * jnp.einsum('bsd,bhd->bsh', x, m1) + b1
        h = jax.nn.gelu(h, approximate=False)
        out = jnp.einsum('bsh,oh->bso', h, W2) + scale * jnp.einsum('bsh,boh->bso', h, m2) + b2
        return out
    x = L0_attn_seq_embeddings
    xn = _layernorm(x, axis=-1)
    x = x + _L0_attn_ref(xn, L0_attn_in_proj_w, L0_attn_conv_w, L0_attn_conv_b, L0_attn_x_proj_w, L0_attn_dt_proj_w, L0_attn_dt_proj_b, L0_attn_A_log, L0_attn_D, L0_attn_out_proj_w, L0_attn_ffn_w1, L0_attn_ffn_b1, L0_attn_ffn_w2, L0_attn_ffn_b2) + _L0_ffn_ref(xn, L0_ffn_scores, L0_ffn_expert_weights, L0_ffn_top_experts, L0_ffn_w1, L0_ffn_w2)
    xn = _layernorm(x, axis=-1)
    x = x + _L1_attn_ref(xn, L1_attn_qkv_w, L1_attn_qkv_b, L1_attn_w1_write, L1_attn_w2_write, L1_attn_w1_read, L1_attn_w2_read, L1_attn_memv_w, L1_attn_memv_b, L1_attn_memg_w, L1_attn_memg_b, L1_attn_mem_scale, L1_attn_out_w, L1_attn_out_b, L1_attn_J, L1_attn_decays) + _L1_ffn_ref(xn, L1_ffn_W1, L1_ffn_b1, L1_ffn_W2, L1_ffn_b2, L1_ffn_scale)
    return x

_drawn_inputs = setup_inputs


def setup_inputs(seed=0):
    import zlib

    import numpy as np

    out = dict(_drawn_inputs(seed))
    spreads = {'L0_attn_D': (1.0, 0.2),
     'L0_attn_ffn_b1': (0.0, 0.1),
     'L0_attn_ffn_b2': (0.0, 0.1),
     'L1_attn_qkv_b': (0.0, 0.1),
     'L1_attn_memv_b': (0.0, 0.1),
     'L1_attn_memg_b': (0.0, 0.1),
     'L1_attn_mem_scale': (0.10000000149011612, 0.2),
     'L1_attn_out_b': (0.0, 0.1),
     'L1_ffn_b1': (0.0, 0.1),
     'L1_ffn_b2': (0.0, 0.1)}
    factors = {}
    for name, (base, spread) in spreads.items():
        noise = np.random.default_rng([zlib.crc32(name.encode()), seed]).standard_normal(out[name].shape)
        drawn = base * np.exp(spread * noise) if base else spread * noise
        out[name] = jnp.asarray(drawn.astype(out[name].dtype))
    for name, factor in factors.items():
        out[name] = (out[name] * factor).astype(out[name].dtype)
    return out
```

```python
from contextlib import ExitStack

import concourse.bass as bass
from concourse import mybir

F32 = mybir.dt.float32
F32R = mybir.dt.float32r
BF16 = mybir.dt.bfloat16
ALU = mybir.AluOpType
ACT = mybir.ActivationFunctionType
AX_X = mybir.AxisListType.X

P = 128
B, S, D = 8, 1024, 256
NT = S // P
KD = D // P
HALF = 512
NC = S // HALF
TC = HALF // P
DI, NS, DTR, NCONV = 512, 16, 64, 4
MI = DI // P
FF = 1024
MF = FF // P
ME = 2048 // P
H, DH, NG = 16, 16, 8
NPQ = 21
FCH = 3
FR = 7 * H
EPS = 1e-5
CAP = 30.0
LN_UNITS = [("xt", c, k) for c in range(NC) for k in range(KD)]

WEIGHTS = [("in", KD * 2 * DI), ("xproj", MI * (DTR + 2 * NS)), ("dt", DI), ("oproj", MI * D), ("f1", KD * FF),
           ("f2", MF * D), ("qk", KD * 2 * D), ("ta", KD * 464), ("tb", KD * 320), ("out", KD * D),
           ("g1", KD * FF), ("g2", MF * D)]
PARAMS = [("convw", MI * NCONV), ("convb", MI), ("dtb", MI), ("alog", MI * NS), ("dskip", MI), ("fb1", MF),
          ("qkb", 4), ("gb1", MF), ("scale", 1), ("decay", 1), ("fb2", D), ("vb", D), ("mvb", D), ("mgb", H),
          ("mscale", H), ("outb", D), ("gb2", D), ("jdiag", 6 * H), ("ident", P), ("mask", P), ("maskt", P),
          ("sumpq", FCH * H), ("pick", 2 * NS), ("mean", P), ("ew", 2 * NT)]


def columns(layout):
    at, out = 0, {}
    for name, n in layout:
        out[name] = (at, at + n)
        at += n
    return out, at


W_AT, W_COLS = columns(WEIGHTS)
P_AT, P_COLS = columns(PARAMS)


def ring_plan(units):
    plan, owner, count = {}, {}, {"a": 0, "v": 0}
    for n, (name, banks, drainers) in enumerate(units):
        need = {"a": 0, "v": 0}
        for bank in banks:
            for who, k in owner.get(bank, {}).items():
                need[who] = max(need[who], k)
        for who in drainers:
            count[who] += 1
        for bank in banks:
            owner[bank] = {who: count[who] for who in drainers}
        assert name not in plan
        plan[name] = (banks, n + 1, need, dict(owner[banks[0]]))
    return plan


def narrow(names, start=0):
    return [(name, [4 + (start + i) % 4], who) for i, (name, who) in enumerate(names)]


def moe_names():
    out = [(u, "a") for u in LN_UNITS]
    for c in range(NC):
        out += [(("h", c, m), "a") for m in range(ME)]
    return out


def layer0_names():
    out = [(u, "a") for u in LN_UNITS]
    for c in range(NC):
        out += [(("xm", c, m), "a") for m in range(MI)]
        out += [(("res", c, t), "a") for t in range(TC)]
        out += [(("xd", c), "v")]
        out += [(("dl", c, m), "v") for m in range(MI)]
        for n in range(NS):
            out += [(("B", c, n), "a"), (("C", c, n), "v")]
        out += [(("yt", c, m), "a") for m in range(MI)]
        out += [(("m", c, k), "a") for k in range(KD)]
        out += [(("h", c, m), "a") for m in range(MF)]
    return out + [(("mu",), "v"), (("var",), "v")]


def layer1_names():
    out = [(("1",) + u, "a") for u in LN_UNITS]
    for t in range(NT):
        out += [(("pa", t), "av"), (("pb", t), "av")]
    out += [(("lt", c), "a") for c in range(NC)]
    out += [(("jw", c), "a") for c in range(NC)]
    for ch in range(FCH):
        for c in range(NC):
            out += [(("fw", ch, c), "v"), (("fr", ch, c), "v")]
    out += [(("ms",), "v")]
    out += [(("qk", g, s, c), "av") for g in range(2) for s in range(2) for c in range(NC)]
    return out


def attention_events():
    ev = []

    def maxima(g):
        return [("sm", 2 * g + p, it) for p in range(2) for it in range(NT)]

    def exps(g):
        return [("st", 2 * g + p, jt) for p in range(2) for jt in range(NT)]

    for g in (0, 1):
        ev += maxima(g) + [("mt", g)]
    for g in range(NG):
        st, sm = exps(g), maxima(g + 2) if g + 2 < NG else []
        for i in range(len(st)):
            ev.append(st[i])
            if sm:
                ev.append(sm[i])
        if sm:
            ev.append(("mt", g + 2))
    out, late = [], []
    for e in ev:
        out.append(e)
        if e[0] == "st":
            late.append(("pv",) + e[1:])
            if len(late) > 2:
                out.append(late.pop(0))
    return out + late


EVENTS = attention_events()
EXPS = [e for e in EVENTS if e[0] == "st"]
PT_RING = 3
WIDE = [[4, 5], [6, 7], [0, 1]]


def wide_units():
    who = {"sm": "v", "st": "a", "mt": "av"}
    units = [e for e in EVENTS if e[0] in who]
    return [(e, WIDE[i % 3], who[e[0]]) for i, e in enumerate(units)]


def tail_names():
    out = [(("zt", k, c), "a") for c in range(NC) for k in range(KD)]
    out += [(("e1", k, c), "v") for k in range(KD) for c in range(NC)]
    out += [(("e2", q), "v") for q in range(MF // 2)]
    for c in range(NC):
        out += [(("g", c, m), "a") for m in range(MF)]
    return out


MOE_PLAN = ring_plan(narrow(moe_names()))
_units = narrow(layer0_names())
_units += narrow(layer1_names(), len(_units))
_units += wide_units()
_units += narrow(tail_names())
ROW_PLAN = ring_plan(_units)


def build(nc, x_in, w_in, p_in, moe1_in, moe2_in, out):
    ctx = ExitStack()
    with ctx:
        def sb(name, shape, dt=F32, where=ctx):
            return where.enter_context(nc.sbuf_tensor(name, shape, dt))

        def sem(name):
            return ctx.enter_context(nc.semaphore(name))

        w_all = sb("w_all", [P, W_COLS])
        p_all = sb("p_all", [P, P_COLS])
        x_row = sb("x_row", [P, NT, D])
        xT = sb("xT", [P, KD, S + 1])
        moe = sb("moe", [P, NT, D])
        neg_a = sb("neg_a", [P, MI * NS])
        ident_b = sb("ident_b", [P, P], BF16)
        mask_b = sb("mask_b", [P, 2, P], BF16)
        pick_r = sb("pick_r", [2 * 2 * NS, 2 * NS], F32R)
        out_bias = sb("out_bias", [P, D])
        ew_sum = sb("ew_sum", [P, NT])
        ln_stats = sb("ln_stats", [P, NT, 6])
        ln_mv = sb("ln_mv", [P, NT, 2])
        ln_std = sb("ln_std", [P, NT])
        ln_rstd = sb("ln_rstd", [P, NT])
        row_stats = sb("row_stats", [P, 4, 6])
        row_mv = sb("row_mv", [P, 2])
        row_q = sb("row_q", [P, 8])

        def weight(name, k=None):
            a, b = W_AT[name]
            v = w_all[:, a:b]
            return v if k is None else v.rearrange("p (k n) -> p k n", k=k)

        def param(name):
            a, b = P_AT[name]
            return p_all[:, a:b]

        ident = param("ident")

        arena_at = -(-nc.sbuf_base // 32) * 32
        arena_end = nc.sbuf_usable_end // 32 * 32
        sb("arena", [P, (arena_end - arena_at) // 4])

        def place(at, *buffers):
            views = []
            for name, shape, *dt in buffers:
                views.append(nc.alloc_sbuf_tensor_at(name, shape, dt[0] if dt else F32, offset=at))
                n = 4
                for extent in shape[1:]:
                    n *= extent
                at += -(-n // 32) * 32
            assert at <= arena_end, (at, arena_end)
            return views + [at]

        moe1, moe2, moe_xn, moe_h, _ = place(
            arena_at, ("moe1", [P, KD, ME * P]), ("moe2", [P, ME, D]), ("moe_xn", [P, NT, D]),
            ("moe_h", [P, 3, HALF]))

        (mix, raw, xm, delta, du, gate, dt_low, bc_parts, b_wide, decay, state, carry, mT, h0, _) = place(
            arena_at, ("mix", [P, NT, D]), ("raw", [P, MI, NCONV - 1 + HALF]), ("xm", [P, MI, HALF]),
            ("delta", [P, MI, HALF]), ("du", [P, MI, HALF]), ("gate", [P, TC, DI]), ("dt_low", [DTR, HALF]),
            ("bc_parts", [4 * NS, HALF], F32R), ("b_wide", [P, 3, HALF]), ("decay", [P, 2, MI, HALF]),
            ("state", [P, 3, MI, HALF]), ("carry", [P, NS, MI]), ("mT", [P, KD, HALF]), ("h0", [P, 3, HALF]))
        yT = xm

        (vals, z, even, odd, odd_hi, gate_in, mem_in, gate8, rden, seq, smax, free_at) = place(
            arena_at, ("vals", [P, NT, H, DH + 1]), ("z", [P, NT, D]), ("even", [8, 4 * D]), ("odd", [8, D]),
            ("odd_hi", [8, D]), ("gate_in", [P, NT, H]), ("mem_in", [P, NT, H]), ("gate8", [P, NT]),
            ("rden", [P, 2, NT]), ("seq", [P, 2, NT, DH]), ("smax", [P, NT, H]))
        ptab, shared_at = place(free_at, ("ptab", [P, PT_RING, S]))
        prod, _ = place(free_at, ("prod", [P, FCH, S]))
        q_hi, q_lo, _ = place(free_at, ("q_hi", [P, S], F32R), ("q_lo", [P, S], F32R))
        k_hi, k_lo, body_at = place(shared_at, ("k_hi", [P, S], F32R), ("k_lo", [P, S], F32R))
        neg_hi, neg_lo, _ = place(shared_at, ("neg_hi", [2, S], F32R), ("neg_lo", [2, S], F32R))
        (xn1, pt1, pt2, outer, lines, norm, linesT, jlines, feat_w, feat_r, gsum, _) = place(
            body_at, ("xn1", [P, NT, D]), ("pt1", [P, NT, 2 * 4 * H]), ("pt2", [P, NT, 2 * 4 * H]),
            ("outer", [P, 2, 2 * H, 4, 4]), ("lines", [P, NT, 2 * H, 6]), ("norm", [P, NT * 2 * H]),
            ("linesT", [6 * H, S]), ("jlines", [P, NT, H, 6]), ("feat_w", [P, NT, NPQ * H]),
            ("feat_r", [P, NT, NPQ * H]), ("gsum", [FR, 2, S + 1]))
        qs, ks, _ = place(body_at, ("qs", [P, NG, S], F32R), ("ks", [P, NG, S], F32R))
        zT, g1, g2, h1, done, _ = place(
            body_at, ("zT", [P, KD, S]), ("g1", [P, KD, FF]), ("g2", [P, MF, D]), ("h1", [P, 3, HALF]),
            ("done", [P, NT // 2, 2, D]))

        ps = ctx.enter_context(nc.psum_tensor("ps", [P, 8, 512], F32))
        y_acc = ps[:, 0:4, :]
        mlp_acc = [ps[:, 0:2, :], ps[:, 0:2, :]]
        pv_acc = [ps[:, 2 + i, 0:NT * (DH + 1)].rearrange("p (t d) -> p t d", d=DH + 1) for i in range(2)]

        def acc_tile(tt):
            return ps[:, tt // 2, (tt % 2) * D:(tt % 2 + 1) * D]

        params_in = sem("params_in")
        weights_in = sem("weights_in")
        moe_in = sem("moe_in")
        setup_v = sem("setup_v")
        setup_a = sem("setup_a")
        setup_p = sem("setup_p")
        round_done = sem("round_done")
        round_go = sem("round_go")
        round_seen = sem("round_seen")
        x_loaded = sem("x_loaded")
        chain_v = sem("chain_v")
        chain_a = sem("chain_a")
        chain_p = sem("chain_p")
        ring_filled = sem("ring_filled")
        drained_a = sem("drained_a")
        drained_v = sem("drained_v")
        ln_var = sem("ln_var")
        ln_sqrt = sem("ln_sqrt")
        xn_done = sem("xn_done")
        moe_added = sem("moe_added")
        pad_zero = sem("pad_zero")
        tap_done = sem("tap_done")
        conv_done = sem("conv_done")
        silu_done = sem("silu_done")
        gate_done = sem("gate_done")
        bc_hi = sem("bc_hi")
        dt_done = sem("dt_done")
        dl_clamped = sem("dl_clamped")
        dl_log = sem("dl_log")
        du_done = sem("du_done")
        skip_done = sem("skip_done")
        decay_done = sem("decay_done")
        driven = sem("driven")
        scanned = sem("scanned")
        weighed = sem("weighed")
        state_read = sem("state_read")
        y_gated = sem("y_gated")
        h_read = sem("h_read")
        acc_read = sem("acc_read")
        row_sum = sem("row_sum")
        l1_clear = sem("l1_clear")
        rows_in = sem("rows_in")
        outer_done = sem("outer_done")
        lines_read = sem("lines_read")
        lines_sq = sem("lines_sq")
        lines_sqrt = sem("lines_sqrt")
        lines_done = sem("lines_done")
        feat_w_done = sem("feat_w_done")
        feat_r_done = sem("feat_r_done")
        sig_done = sem("sig_done")
        ks_ones = sem("ks_ones")
        pt_read = sem("pt_read")
        pv_read = sem("pv_read")
        z_done = sem("z_done")
        out_sum = sem("out_sum")
        out_left = sem("out_left")
        q_in = [sem(f"q_in{g}") for g in range(NG)]
        k_in = [sem(f"k_in{g}") for g in range(NG)]
        neg_in = [sem(f"neg_in{g}") for g in range(NG)]
        per_round = [
            x_loaded, chain_v, chain_a, chain_p, ring_filled, drained_a,
            drained_v, ln_var, ln_sqrt, xn_done, moe_added, pad_zero,
            tap_done, conv_done, silu_done, gate_done, bc_hi, dt_done,
            dl_clamped, dl_log, du_done, skip_done, decay_done, driven,
            scanned, weighed, state_read, y_gated, h_read, acc_read,
            row_sum, l1_clear, rows_in, outer_done, lines_read, lines_sq,
            lines_sqrt, lines_done, feat_w_done, feat_r_done, sig_done, ks_ones,
            pt_read, pv_read, z_done, out_sum, out_left] + q_in + k_in + neg_in

        def claim(plan, unit):
            banks, _, need, _ = plan[unit]
            if need["a"]:
                nc.tensor.wait_ge(drained_a, need["a"])
            if need["v"]:
                nc.tensor.wait_ge(drained_v, need["v"])
            return ps[:, banks[0]:banks[-1] + 1, :].rearrange("p b n -> p (b n)")

        def full(eng, plan, unit):
            banks, ready, _, _ = plan[unit]
            eng.wait_ge(ring_filled, ready)
            return ps[:, banks[0]:banks[-1] + 1, :].rearrange("p b n -> p (b n)")

        def drained(eng, plan, unit, who):
            eng.wait_ge(drained_a if who == "a" else drained_v, plan[unit][3][who])

        chain = {"v": 0, "a": 0, "p": 0}

        def link(who, ins):
            chain[who] += 1
            signal = {"v": chain_v, "a": chain_a, "p": chain_p}[who]
            ins.then_inc(signal, 1)
            {"v": nc.vector, "a": nc.scalar, "p": nc.gpsimd}[who].wait_ge(signal, chain[who])

        def end_round(eng, n, leader=False):
            chain.update(v=0, a=0, p=0)
            eng.sem_inc(round_done, 1)
            if leader:
                eng.wait_ge(round_done, 5)
                for one in per_round + [round_done]:
                    eng.sem_clear(one)
                eng.sem_inc(round_go, 1)
            else:
                eng.wait_ge(round_go, n)
                eng.sem_inc(round_seen, 1)

        def wide(ap, middle):
            return ap.unsqueeze(1).broadcast_to([ap.shape[0], middle, ap.shape[1]])

        def tokens(t, n=P, shift=1):
            return slice(shift + t * P, shift + t * P + n)

        def products(eng, dst, c6):
            by_q = dst[:, :, :].rearrange("p t (q h) -> p t q h", h=H)
            at = 0
            for p in range(6):
                n = 6 - p
                last = eng.tensor_tensor(by_q[:, :, at:at + n, :],
                                         c6[:, :, :, p].unsqueeze(2).broadcast_to([P, NT, n, H]),
                                         c6[:, :, :, p:6].rearrange("p t h q -> p t q h"), ALU.mult)
                at += n
            return last

        block = ctx.enter_context(nc.Block())

        @block.sync
        def _(sp):
            sp.dma_start(p_all[:, :], p_in).then_inc(params_in, 16)
            sp.dma_start(x_row[:, :, :], x_in[0].rearrange("(t p) d -> p t d", p=P)).then_inc(x_loaded, 16)
            sp.dma_start(moe1[:, :, :], moe1_in).then_inc(moe_in, 16)
            sp.dma_start(moe2[:, :, :], moe2_in).then_inc(moe_in, 16)
            sp.dma_start(w_all[:, :], w_in).then_inc(weights_in, 16)
            sp.wait_ge(x_loaded, 16)
            end_round(sp, 1, leader=True)
            with sp.Fori(0, B) as b:
                sp.dma_start(x_row[:, :, :], x_in[bass.ds(b, 1), :, :].rearrange("a (t p) d -> p (a t) d", p=P))\
                  .then_inc(x_loaded, 16)
                sp.wait_ge(xn_done, NT + 1)
                sp.wait_ge(l1_clear, 1)
                for r in range(8):
                    sp.dma_start(even[r:r + 1, (r % 4) * D:(r % 4 + 1) * D], xn1[1 + 2 * r:2 + 2 * r, 0, :])\
                      .then_inc(rows_in, 16)
                sp.dma_start(odd[:, :], xn1[2:18:2, 0, :]).then_inc(rows_in, 16)
                sp.dma_start(odd_hi[4:8, :], xn1[10:18:2, 0, :]).then_inc(rows_in, 16)
                sp.wait_ge(ks_ones, 1)
                for g in range(2):
                    for i, (hi, lo, dst, signal, order) in enumerate(
                            ((q_hi, q_lo, qs, q_in, "hhl"), (k_hi, k_lo, ks, k_in, "hlh"))):
                        for who in "av":
                            drained(sp, ROW_PLAN, ("qk", g, i, 1), who)
                        for j in range(8):
                            slot, base = 4 * g + j // 2, 64 * (j % 2)
                            for r, part in enumerate(order):
                                src = hi if part == "h" else lo
                                sp.dma_start(dst[base + DH * r:base + DH * (r + 1), slot, :].bitcast(F32),
                                             src[DH * j:DH * (j + 1), :].bitcast(F32)).then_inc(signal[slot], 16)
                for g in range(NG):
                    for who in "av":
                        drained(sp, ROW_PLAN, ("mt", g), who)
                    sp.dma_start(qs[48:128:64, g, :].bitcast(F32), neg_hi[:, :].bitcast(F32)).then_inc(neg_in[g], 16)
                    sp.dma_start(qs[49:128:64, g, :].bitcast(F32), neg_lo[:, :].bitcast(F32)).then_inc(neg_in[g], 16)
                for i in range(NT // 2):
                    sp.wait_ge(out_sum, i + 1)
                    sp.dma_start(
                        out[bass.ds(b, 1), 2 * i * P:(2 * i + 2) * P, :].rearrange("a (t p) d -> p (a t) d", p=P),
                        done[:, i, :, :]).then_inc(out_left, 16)
                sp.wait_ge(out_left, 16 * (NT // 2))
                end_round(sp, b + 2, leader=True)

        @block.tensor
        def _(pe):
            mm, tp = nc.tensor.matmul, nc.tensor.transpose

            def normalised_T(plan, prefix, xn, base):
                for unit in LN_UNITS:
                    _, c, k = unit
                    bank = claim(plan, prefix + unit)
                    pe.wait_ge(xn_done, base + TC * (c + 1))
                    for tt in range(TC):
                        last = tp(bank[:, tt * P:(tt + 1) * P], xn[:, TC * c + tt, k * P:(k + 1) * P], ident)
                    last.then_inc(ring_filled, 1)

            def mlp(plan, tag, c, n_hidden, up, src, down, hidden, base, fresh):
                for m in range(n_hidden + 1):
                    if m < n_hidden:
                        bank = claim(plan, (tag, c, m))
                        for k in range(KD):
                            last = mm(bank, up[:, k, m * P:(m + 1) * P], src[k], start=(k == 0), stop=(k == KD - 1))
                        last.then_inc(ring_filled, 1)
                    if m >= 1:
                        j = m - 1
                        drained(pe, plan, (tag, c, j), "a")
                        for tt in range(TC):
                            last = mm(acc_tile(tt), hidden[:, (base + j) % 3, tt * P:(tt + 1) * P], down[:, j, :],
                                      start=(fresh and j == 0 and tt % 2 == 0), stop=(j == n_hidden - 1),
                                      skip_group_check=True)
                        last.then_inc(h_read, 1)

            pe.wait_ge(params_in, 16)
            normalised_T(MOE_PLAN, (), moe_xn, 0)
            pe.wait_ge(moe_in, 32)
            for c in range(NC):
                drained(pe, MOE_PLAN, ("xt", c, 1), "a")
                if c:
                    pe.wait_ge(acc_read, 2 * c)
                mlp(MOE_PLAN, "h", c, ME, moe1, [xT[:, k, tokens(TC * c, HALF)] for k in range(KD)], moe2, moe_h,
                    ME * c, True)
            pe.wait_ge(weights_in, 16)
            pe.wait_ge(setup_a, 6)
            pe.wait_ge(setup_v, 3)
            end_round(pe, 1)

            def layer0(c):
                plan = ROW_PLAN
                w = weight("in", KD)
                drained(pe, plan, ("xt", c, 1), "a")
                for m in range(MI):
                    bank = claim(plan, ("xm", c, m))
                    for k in range(KD):
                        last = mm(bank, w[:, k, m * P:(m + 1) * P], xT[:, k, tokens(TC * c, HALF)],
                                  start=(k == 0), stop=(k == KD - 1))
                    last.then_inc(ring_filled, 1)
                for t in range(TC):
                    bank = claim(plan, ("res", c, t))
                    for k in range(KD):
                        last = mm(bank, xT[:, k, tokens(TC * c + t)], w[:, k, DI:2 * DI],
                                  start=(k == 0), stop=(k == KD - 1))
                    last.then_inc(ring_filled, 1)
                w = weight("xproj", MI)
                bank = claim(plan, ("xd", c))
                for m in range(MI):
                    pe.wait_ge(silu_done, MI * c + m + 1)
                    last = mm(bank[0:DTR + 2 * NS, :], w[:, m, :], xm[:, m, :], start=(m == 0), stop=(m == MI - 1))
                last.then_inc(ring_filled, 1)
                w = weight("dt")
                for m in range(MI):
                    bank = claim(plan, ("dl", c, m))
                    pe.wait_ge(dt_done, c + 1)
                    mm(bank, w[0:DTR, m * P:(m + 1) * P], dt_low[:, :], start=True, stop=True)\
                        .then_inc(ring_filled, 1)

                def spread(n):
                    for name, col in (("B", n), ("C", NS + n)):
                        bank = claim(plan, (name, c, n))
                        mm(bank, pick_r[:, col:col + 1].broadcast_to([4 * NS, P]), bc_parts[:, :],
                           start=True, stop=True).then_inc(ring_filled, 1)

                def add_y(u):
                    for d in range(MI):
                        for t in range(TC):
                            last = mm(y_acc[:, t, d * P:(d + 1) * P],
                                      state[:, (c * (NS + 1) + u) % 3, d, t * P:(t + 1) * P], ident,
                                      is_transpose=True, start=(u == 0 and d == 0), stop=(u == NS),
                                      skip_group_check=True)
                    last.then_inc(state_read, 1)

                drained(pe, plan, ("xd", c), "v")
                spread(0)
                spread(1)
                if c:
                    pe.wait_ge(acc_read, 2 * c)
                    pe.wait_ge(y_gated, TC * c)
                pe.wait_ge(skip_done, c + 1)
                add_y(0)
                for n in range(NS):
                    if n + 2 < NS:
                        spread(n + 2)
                    pe.wait_ge(weighed, c * NS + n + 1)
                    add_y(n + 1)
                for d in range(MI):
                    bank = claim(plan, ("yt", c, d))
                    for t in range(TC):
                        if d == 0:
                            pe.wait_ge(y_gated, TC * c + t + 1)
                        last = tp(bank[:, t * P:(t + 1) * P], gate[:, t, d * P:(d + 1) * P], ident)
                    last.then_inc(ring_filled, 1)
                w = weight("oproj", MI)
                drained(pe, plan, ("yt", c, MI - 1), "a")
                for k in range(KD):
                    bank = claim(plan, ("m", c, k))
                    for d in range(MI):
                        last = mm(bank, w[:, d, k * P:(k + 1) * P], yT[:, d, :], start=(d == 0), stop=(d == MI - 1))
                    last.then_inc(ring_filled, 1)
                drained(pe, plan, ("m", c, KD - 1), "a")
                for tt in range(TC):
                    for k in range(KD):
                        mm(acc_tile(tt)[:, k * P:(k + 1) * P], mT[:, k, tt * P:(tt + 1) * P], ident,
                           is_transpose=True, start=(tt % 2 == 0 and k == 0), stop=False, skip_group_check=True)
                mlp(plan, "h", c, MF, weight("f1", KD), [mT[:, k, :] for k in range(KD)], weight("f2", MF), h0,
                    MF * c, False)

            def attention():
                plan = ROW_PLAN
                u = 0
                for e in EVENTS:
                    kind, h = e[0], e[1]
                    g, base = h // 2, 64 * (h % 2)
                    if kind == "sm":
                        it = e[2]
                        both = claim(plan, e)
                        if it == 0 and h % 2 == 0:
                            pe.wait_ge(q_in[g], 96)
                            pe.wait_ge(k_in[g], 96)
                        width = (it + 1) * P
                        for at in range(0, width, HALF):
                            n = min(HALF, width - at)
                            mm(both[:, at:at + n], qs[base:base + 48, g, it * P:(it + 1) * P],
                               ks[base:base + 48, g, at:at + n], start=True, stop=(at + n < width),
                               skip_group_check=True)
                        mm(both[:, it * P:width], ident_b[:, :], mask_b[:, 0, :], start=False, stop=True,
                           skip_group_check=True).then_inc(ring_filled, 1)
                    elif kind == "mt":
                        g = e[1]
                        both = claim(plan, e)
                        drained(pe, plan, ("sm", 2 * g + 1, NT - 1), "v")
                        for it in range(NT):
                            last = tp(both[0:2, it * P:(it + 1) * P], smax[:, it, 2 * g:2 * g + 2], ident)
                        last.then_inc(ring_filled, 1)
                    elif kind == "st":
                        jt = e[2]
                        both = claim(plan, e)
                        if jt == 0 and h % 2 == 0:
                            pe.wait_ge(neg_in[g], 32)
                        width = (NT - jt) * P
                        for at in range(0, width, HALF):
                            n = min(HALF, width - at)
                            mm(both[:, at:at + n], ks[base:base + 50, g, jt * P:(jt + 1) * P],
                               qs[base:base + 50, g, jt * P + at:jt * P + at + n], start=True, stop=(at > 0),
                               skip_group_check=True)
                        mm(both[:, 0:P], ident_b[:, :], mask_b[:, 1, :], start=False, stop=True,
                           skip_group_check=True).then_inc(ring_filled, 1)
                    else:
                        jt = e[2]
                        drained(pe, plan, ("st", h, jt), "a")
                        if jt == 0 and h >= 2:
                            pe.wait_ge(pv_read, h - 1)
                        for it in range(jt, NT):
                            last = mm(pv_acc[h % 2][:, it, :], ptab[:, u % PT_RING, (it - jt) * P:(it - jt + 1) * P],
                                      vals[:, jt, h, :], start=(jt == 0 and it == 0), stop=(it == jt),
                                      skip_group_check=True)
                        last.then_inc(pt_read, 1)
                        u += 1

            def layer1():
                plan = ROW_PLAN
                normalised_T(plan, ("1",), xn1, NT)
                ta, tb = weight("ta", KD), weight("tb", KD)
                for t in range(NT):
                    if t % TC == 0:
                        drained(pe, plan, ("1", "xt", t // TC, 1), "a")
                    bank = claim(plan, ("pa", t))
                    for k in range(KD):
                        last = mm(bank[:, 0:464], xT[:, k, tokens(t)], ta[:, k, :], start=(k == 0), stop=(k == KD - 1))
                    last.then_inc(ring_filled, 1)
                    bank = claim(plan, ("pb", t))
                    for k in range(KD):
                        mm(bank[:, 0:D], xT[:, k, tokens(t)], tb[:, k, 0:D], start=(k == 0), stop=(k == KD - 1),
                           skip_group_check=True)
                    for k in range(KD):
                        last = mm(bank[:, D:D + 64], xT[:, k, tokens(t, shift=0)], tb[:, k, D:D + 64],
                                  start=(k == 0), stop=(k == KD - 1), skip_group_check=True)
                    last.then_inc(ring_filled, 1)
                for c in range(NC):
                    bank = claim(plan, ("lt", c))
                    pe.wait_ge(lines_done, 1)
                    for tt in range(TC):
                        last = tp(bank[0:6 * H, tt * P:(tt + 1) * P],
                                  lines[:, TC * c + tt, 0:H, :].rearrange("p h j -> p (h j)"), ident)
                    last.then_inc(ring_filled, 1)
                for c in range(NC):
                    bank = claim(plan, ("jw", c))
                    drained(pe, plan, ("lt", c), "a")
                    for tt in range(TC):
                        last = mm(bank[:, tt * 96:(tt + 1) * 96], linesT[:, (TC * c + tt) * P:(TC * c + tt + 1) * P],
                                  param("jdiag")[0:96, :], start=True, stop=True)
                    last.then_inc(ring_filled, 1)
                pe.wait_ge(feat_r_done, 1)
                pe.wait_ge(feat_w_done, 1)
                for ch in range(FCH):
                    for c in range(NC):
                        for name, feat in (("fw", feat_w), ("fr", feat_r)):
                            bank = claim(plan, (name, ch, c))
                            for tt in range(TC):
                                last = tp(bank[0:FR, tt * P:(tt + 1) * P],
                                          feat[:, TC * c + tt, ch * FR:(ch + 1) * FR], ident)
                            last.then_inc(ring_filled, 1)
                bank = claim(plan, ("ms",))
                drained(pe, plan, ("fr", FCH - 1, NC - 1), "v")
                pick = param("sumpq").rearrange("p (c h) -> p c h", c=FCH)
                for t in range(NT):
                    for ch in range(FCH):
                        last = mm(bank[:, t * H:(t + 1) * H], prod[0:FR, ch, t * P:(t + 1) * P], pick[0:FR, ch, :],
                                  start=(ch == 0), stop=(ch == FCH - 1))
                last.then_inc(ring_filled, 1)
                w = weight("qk", KD)
                for g in range(2):
                    for i in range(2):
                        for c in range(NC):
                            bank = claim(plan, ("qk", g, i, c))
                            for k in range(KD):
                                last = mm(bank, w[:, k, i * D + g * P:i * D + (g + 1) * P],
                                          xT[:, k, tokens(TC * c, HALF)], start=(k == 0), stop=(k == KD - 1))
                            last.then_inc(ring_filled, 1)
                attention()
                for c in range(NC):
                    for k in range(KD):
                        bank = claim(plan, ("zt", k, c))
                        pe.wait_ge(z_done, 1)
                        for tt in range(TC):
                            last = tp(bank[:, tt * P:(tt + 1) * P], z[:, TC * c + tt, k * P:(k + 1) * P], ident)
                        last.then_inc(ring_filled, 1)
                pe.wait_ge(rows_in, 160)
                for k in range(KD):
                    for c in range(NC):
                        bank = claim(plan, ("e1", k, c))
                        mm(bank, odd[0:4, k * P:(k + 1) * P], even[0:4, c * HALF:(c + 1) * HALF],
                           start=True, stop=True).then_inc(ring_filled, 1)
                by_c = even[:, :].rearrange("e (r i c) -> e c r i", r=4, c=4)
                for q in range(MF // 2):
                    bank = claim(plan, ("e2", q))
                    for j in range(2):
                        last = mm(bank[:, j * D:(j + 1) * D].rearrange("p (r i) -> p r i", r=4),
                                  odd_hi[:, j * P:(j + 1) * P], by_c[:, q], start=True, stop=True)
                    last.then_inc(ring_filled, 1)
                for c in range(NC):
                    if c:
                        pe.wait_ge(acc_read, 4 + 2 * c)
                    else:
                        drained(pe, plan, ("st", H - 1, NT - 1), "a")
                        drained(pe, plan, ("sm", H - 1, NT - 1), "v")
                    drained(pe, plan, ("zt", 1, c), "a")
                    for tt in range(TC):
                        for k in range(KD):
                            mm(acc_tile(tt), zT[:, k, (TC * c + tt) * P:(TC * c + tt + 1) * P],
                               weight("out", KD)[:, k, :], start=(tt % 2 == 0 and k == 0), stop=False,
                               skip_group_check=True)
                    drained(pe, plan, ("e2", MF // 2 - 1), "v")
                    mlp(plan, "g", c, MF, g1, [xT[:, k, tokens(TC * c, HALF)] for k in range(KD)], g2, h1,
                        MF * (NC + c), False)

            with pe.Fori(0, B) as b:
                normalised_T(ROW_PLAN, (), mix, 0)
                for c in range(NC):
                    layer0(c)
                bank = claim(ROW_PLAN, ("mu",))
                pe.wait_ge(row_sum, 1)
                mm(bank[:, 0:1], param("mean"), row_mv[:, 0:1], start=True, stop=True).then_inc(ring_filled, 1)
                bank = claim(ROW_PLAN, ("var",))
                pe.wait_ge(row_sum, 2)
                mm(bank[:, 0:1], param("mean"), row_q[:, 1:2], start=True, stop=True).then_inc(ring_filled, 1)
                layer1()
                end_round(pe, b + 2)

        @block.scalar
        def _(act):
            def f(out_, in_, func, **kw):
                return nc.scalar.activation(out_, in_, func, **kw)

            def deviation(n):
                act.wait_ge(ln_var, n)
                f(ln_std[:, :], ln_std[:, :], ACT.Sqrt).then_inc(ln_sqrt, 1)

            def keep_xT(plan, prefix):
                for unit in LN_UNITS:
                    _, c, k = unit
                    bank = full(act, plan, prefix + unit)
                    f(xT[:, k, tokens(TC * c, HALF)], bank, ACT.Copy).then_inc(drained_a, 1)

            def hidden(plan, tag, c, n_hidden, func, bias, dst, base):
                for m in range(n_hidden):
                    bank = full(act, plan, (tag, c, m))
                    if base + m >= 3:
                        act.wait_ge(h_read, base + m - 2)
                    kw = {"bias": bias[:, m:m + 1]} if bias is not None else {}
                    f(dst[:, (base + m) % 3, :], bank, func, **kw).then_inc(drained_a, 1)

            act.wait_ge(params_in, 16)
            f(ident_b[:, :], ident, ACT.Copy).then_inc(setup_a, 1)
            f(mask_b[:, 0, :], param("mask"), ACT.Copy).then_inc(setup_a, 1)
            f(mask_b[:, 1, :], param("maskt"), ACT.Copy).then_inc(setup_a, 1)
            f(pick_r[:, :], param("pick")[0:4 * NS, :], ACT.Copy).then_inc(setup_a, 1)
            f(neg_a[:, :], param("alog"), ACT.Exp).then_inc(setup_a, 1)
            act.wait_ge(setup_a, 5)
            f(neg_a[:, :], neg_a[:, :], ACT.Copy, scale=-1.0).then_inc(setup_a, 1)
            deviation(1)
            keep_xT(MOE_PLAN, ())
            for c in range(NC):
                hidden(MOE_PLAN, "h", c, ME, ACT.Gelu_apprx_tanh, None, moe_h, ME * c)
            act.wait_ge(setup_a, 6)
            end_round(act, 1)

            def layer0(c):
                plan = ROW_PLAN
                if c:
                    act.wait_ge(conv_done, 3 * MI)
                    f(raw[:, :, 0:NCONV - 1], raw[:, :, HALF:HALF + NCONV - 1], ACT.Copy).then_inc(pad_zero, 1)
                act.wait_ge(pad_zero, c + 1)
                taps = param("convw").rearrange("p (m k) -> p m k", m=MI)
                for m in range(MI):
                    bank = full(act, plan, ("xm", c, m))
                    f(raw[:, m, NCONV - 1:], bank, ACT.Copy).then_inc(tap_done, 1)
                    f(xm[:, m, :], bank, ACT.Identity, scale=taps[:, m, NCONV - 1:NCONV],
                      bias=param("convb")[:, m:m + 1]).then_inc(drained_a, 1)
                for t in range(TC):
                    bank = full(act, plan, ("res", c, t))
                    if t == 0 and c:
                        drained(act, plan, ("yt", c - 1, MI - 1), "a")
                    f(gate[:, t, :], bank, ACT.Silu).then_inc(drained_a, 1)
                for m in range(MI):
                    act.wait_ge(conv_done, 3 * MI * c + 2 * MI + m + 1)
                    f(xm[:, m, :], xm[:, m, :], ACT.Silu).then_inc(silu_done, 1)
                bank = full(act, plan, ("xd", c))
                f(bc_parts[0:2 * NS, :], bank[DTR:DTR + 2 * NS, :], ACT.Copy).then_inc(bc_hi, 1)
                for m in range(MI):
                    act.wait_ge(dl_clamped, MI * c + m + 1)
                    link("a", f(du[:, m, :], du[:, m, :], ACT.Exp))
                for m in range(MI):
                    f(du[:, m, :], du[:, m, :], ACT.Ln, bias=1.0).then_inc(dl_log, 1)

                def b_wide_copy(n):
                    j = c * NS + n
                    bank = full(act, plan, ("B", c, n))
                    if j >= 3:
                        act.wait_ge(driven, j - 2)
                    f(b_wide[:, j % 3, :], bank, ACT.Copy).then_inc(drained_a, 1)

                b_wide_copy(0)
                drained(act, plan, ("dl", c, MI - 1), "v")
                for n in range(NS):
                    j = c * NS + n
                    if j >= 2:
                        act.wait_ge(scanned, MI * (j - 1))
                    for d in range(MI):
                        f(decay[:, j % 2, d, :], delta[:, d, :], ACT.Exp,
                          scale=neg_a[:, d * NS + n:d * NS + n + 1]).then_inc(decay_done, 1)
                    if n + 1 < NS:
                        b_wide_copy(n + 1)
                for d in range(MI):
                    bank = full(act, plan, ("yt", c, d))
                    f(yT[:, d, :], bank, ACT.Copy).then_inc(drained_a, 1)
                for k in range(KD):
                    bank = full(act, plan, ("m", c, k))
                    f(mT[:, k, :], bank, ACT.Copy).then_inc(drained_a, 1)
                hidden(plan, "h", c, MF, ACT.Gelu, param("fb1"), h0, MF * c)

            def attention():
                plan = ROW_PLAN
                u = 0
                for e in EVENTS:
                    if e[0] == "mt":
                        g = e[1]
                        both = full(act, plan, e)
                        if g == 0:
                            for slot in range(NG):
                                act.wait_ge(k_in[slot], 96)
                        else:
                            act.wait_ge(neg_in[g - 1], 32)
                        f(neg_hi[:, :], both[0:2, :], ACT.Copy, scale=-1.0).then_inc(drained_a, 1)
                    elif e[0] == "st":
                        h, jt = e[1], e[2]
                        both = full(act, plan, e)
                        if u == 0:
                            for slot in range(NG):
                                act.wait_ge(q_in[slot], 96)
                        if u >= PT_RING:
                            act.wait_ge(pt_read, u - PT_RING + 1)
                        width = (NT - jt) * P
                        f(ptab[:, u % PT_RING, 0:width], both[:, 0:width], ACT.Exp, scale=float(DH) ** -0.5)\
                            .then_inc(drained_a, 1)
                        u += 1

            def layer1():
                plan = ROW_PLAN
                deviation(3)
                keep_xT(plan, ("1",))
                for t in range(NT):
                    bank = full(act, plan, ("pa", t))
                    f(pt1[:, t, 64:128], bank[:, D:D + 64], ACT.Copy).then_inc(tap_done, 1)
                    f(pt2[:, t, :], bank[:, D + 64:D + 192], ACT.Copy).then_inc(drained_a, 1)
                    bank = full(act, plan, ("pb", t))
                    f(pt1[:, t, 0:64], bank[:, D:D + 64], ACT.Copy).then_inc(drained_a, 1)
                act.wait_ge(lines_sq, 1)
                f(norm[:, :], norm[:, :], ACT.Sqrt).then_inc(lines_sqrt, 1)
                for c in range(NC):
                    bank = full(act, plan, ("lt", c))
                    f(linesT[:, c * HALF:(c + 1) * HALF], bank[0:6 * H, :], ACT.Copy).then_inc(drained_a, 1)
                for c in range(NC):
                    bank = full(act, plan, ("jw", c))
                    f(jlines[:, TC * c:TC * (c + 1), :, :].rearrange("p t h j -> p (t h j)"), bank[:, 0:TC * 6 * H],
                      ACT.Copy).then_inc(drained_a, 1)
                drained(act, plan, ("ms",), "v")
                f(mem_in[:, :, :], mem_in[:, :, :], ACT.Sigmoid).then_inc(sig_done, 1)
                f(gate_in[:, :, :], gate_in[:, :, :], ACT.Sigmoid).then_inc(sig_done, 1)
                act.wait_ge(ks_ones, 1)
                for g in range(2):
                    for i, (hi, signal) in enumerate(((q_hi, q_in), (k_hi, k_in))):
                        if g:
                            for slot in range(4):
                                act.wait_ge(signal[slot], 96)
                        for c in range(NC):
                            bank = full(act, plan, ("qk", g, i, c))
                            f(hi[:, c * HALF:(c + 1) * HALF], bank, ACT.Identity,
                              bias=param("qkb")[:, 2 * i + g:2 * i + g + 1]).then_inc(drained_a, 1)
                attention()
                for c in range(NC):
                    for k in range(KD):
                        bank = full(act, plan, ("zt", k, c))
                        f(zT[:, k, c * HALF:(c + 1) * HALF], bank, ACT.Copy).then_inc(drained_a, 1)
                for c in range(NC):
                    hidden(plan, "g", c, MF, ACT.Gelu, param("gb1"), h1, MF * (NC + c))

            with act.Fori(0, B) as b:
                deviation(1)
                keep_xT(ROW_PLAN, ())
                for c in range(NC):
                    layer0(c)
                act.wait_ge(ln_var, 2)
                f(row_q[:, 2:3], row_q[:, 2:3], ACT.Sqrt).then_inc(ln_sqrt, 1)
                layer1()
                end_round(act, b + 2)

        @block.vector
        def _(dve):
            V = nc.vector

            def normalise(x, xn, n):
                for t in range(NT):
                    last = V.bn_stats(ln_stats[:, t, :], x[:, t, :])
                link("v", last)
                for t in range(NT):
                    last = V.bn_aggr(ln_mv[:, t, :], ln_stats[:, t, :])
                link("v", last)
                V.tensor_scalar(ln_std[:, :], ln_mv[:, :, 1], EPS, None, ALU.add).then_inc(ln_var, 1)
                dve.wait_ge(ln_sqrt, n)
                link("v", V.reciprocal(ln_rstd[:, :], ln_std[:, :]))
                for t in range(NT):
                    V.tensor_scalar(xn[:, t, :], x[:, t, :], ln_mv[:, t, 0:1], ln_rstd[:, t:t + 1], ALU.subtract,
                                    ALU.mult).then_inc(xn_done, 1)

            V.memset(xT[:, :, 0:1], 0.0).then_inc(setup_v, 1)
            dve.wait_ge(params_in, 16)
            V.tensor_tensor(out_bias[:, :], param("outb"), param("gb2"), ALU.add).then_inc(setup_v, 1)
            ew = param("ew").rearrange("p (t k) -> p t k", k=2)
            V.tensor_tensor(ew_sum[:, :], ew[:, :, 0], ew[:, :, 1], ALU.add).then_inc(setup_v, 1)
            dve.wait_ge(setup_v, 3)
            dve.wait_ge(x_loaded, 16)
            normalise(x_row, moe_xn, 1)
            for c in range(NC):
                dve.wait_ge(h_read, ME * (c + 1))
                for tt in range(TC):
                    t = TC * c + tt
                    ins = V.tensor_scalar(moe[:, t, :], acc_tile(tt), ew_sum[:, t:t + 1], None, ALU.mult)
                    if tt % 2:
                        ins.then_inc(acc_read, 1)
            dve.wait_ge(acc_read, 2 * NC)
            end_round(dve, 1)

            def layer0(c):
                plan = ROW_PLAN
                taps = param("convw").rearrange("p (m k) -> p m k", m=MI)
                for k in range(NCONV - 1):
                    for m in range(MI):
                        step = 3 * MI * c + MI * k + m
                        if k == 0:
                            drained(dve, plan, ("xm", c, m), "a")
                        else:
                            dve.wait_ge(conv_done, step + 1 - MI)
                        V.scalar_tensor_tensor(xm[:, m, :], raw[:, m, k:k + HALF], taps[:, m, k:k + 1], xm[:, m, :],
                                               ALU.mult, ALU.add).then_inc(conv_done, 1)
                bank = full(dve, plan, ("xd", c))
                dve.wait_ge(bc_hi, c + 1)
                V.tensor_copy(dt_low[:, :], bank[0:DTR, :]).then_inc(dt_done, 1)
                V.tensor_tensor(bc_parts[2 * NS:4 * NS, :], bank[DTR:DTR + 2 * NS, :],
                                bc_parts[0:2 * NS, :].bitcast(F32), ALU.subtract).then_inc(drained_v, 1)
                bias = param("dtb")
                for m in range(MI):
                    bank = full(dve, plan, ("dl", c, m))
                    V.tensor_scalar(du[:, m, :], bank, bias[:, m:m + 1], CAP, ALU.add, ALU.min)\
                        .then_inc(dl_clamped, 1)
                for m in range(MI):
                    bank = full(dve, plan, ("dl", c, m))
                    dve.wait_ge(dl_log, MI * c + m + 1)
                    V.scalar_tensor_tensor(delta[:, m, :], bank, bias[:, m:m + 1], du[:, m, :], ALU.add, ALU.max)\
                        .then_inc(drained_v, 1)
                for m in range(MI):
                    drained(dve, plan, ("dl", c, m), "v")
                    V.tensor_tensor(du[:, m, :], delta[:, m, :], xm[:, m, :], ALU.mult).then_inc(du_done, 1)
                for n in range(NS):
                    j = c * NS + n
                    slot = (c * (NS + 1) + n + 1) % 3
                    dve.wait_ge(driven, j + 1)
                    for d in range(MI):
                        dve.wait_ge(decay_done, MI * j + d + 1)
                        V.tensor_tensor_scan(state[:, slot, d, :], decay[:, j % 2, d, :], state[:, slot, d, :],
                                             carry[:, n, d:d + 1] if c else 0.0, ALU.mult, ALU.add)\
                            .then_inc(scanned, 1)
                    dve.wait_ge(scanned, MI * (j + 1))
                    if c == 0:
                        link("v", V.tensor_copy(carry[:, n, :], state[:, slot, :, HALF - 1]))
                    bank = full(dve, plan, ("C", c, n))
                    V.tensor_tensor(state[:, slot, :, :], state[:, slot, :, :], wide(bank, MI), ALU.mult)\
                        .then_inc(weighed, 1)
                    dve.wait_ge(weighed, j + 1)
                    dve.sem_inc(drained_v, 1)
                dve.wait_ge(state_read, (c + 1) * (NS + 1))
                for t in range(TC):
                    V.tensor_tensor(gate[:, t, :], y_acc[:, t, :], gate[:, t, :], ALU.mult).then_inc(y_gated, 1)
                dve.wait_ge(h_read, MF * (c + 1))
                for a in range(2):
                    t = TC * c + 2 * a
                    V.tensor_tensor(mix[:, t:t + 2, :], ps[:, a, :].rearrange("p (t d) -> p t d", t=2),
                                    wide(param("fb2"), 2), ALU.add).then_inc(acc_read, 1)
                    dve.wait_ge(acc_read, 2 * c + a + 1)
                    link("v", V.bn_stats(row_stats[:, 2 * c + a, :], mix[:, t:t + 2, :].rearrange("p t d -> p (t d)")))

            def finish_layer0():
                V.bn_aggr(row_mv[:, :], row_stats[:, :, :].rearrange("p a b -> p (a b)")).then_inc(row_sum, 1)
                bank = full(dve, ROW_PLAN, ("mu",))
                dve.wait_ge(row_sum, 1)
                V.tensor_copy(row_q[:, 0:1], bank[:, 0:1]).then_inc(drained_v, 1)
                drained(dve, ROW_PLAN, ("mu",), "v")
                link("v", V.tensor_tensor(row_q[:, 4:5], row_mv[:, 0:1], row_q[:, 0:1], ALU.subtract))
                V.scalar_tensor_tensor(row_q[:, 1:2], row_q[:, 4:5], row_q[:, 4:5], row_mv[:, 1:2], ALU.mult,
                                       ALU.add).then_inc(row_sum, 1)
                bank = full(dve, ROW_PLAN, ("var",))
                V.tensor_scalar(row_q[:, 2:3], bank[:, 0:1], EPS, None, ALU.add).then_inc(drained_v, 1)
                drained(dve, ROW_PLAN, ("var",), "v")
                dve.sem_inc(ln_var, 1)
                dve.wait_ge(ln_sqrt, 2)
                link("v", V.reciprocal(row_q[:, 3:4], row_q[:, 2:3]))
                for t in range(NT):
                    last = V.tensor_scalar(mix[:, t, :], mix[:, t, :], row_q[:, 0:1], row_q[:, 3:4], ALU.subtract,
                                           ALU.mult)
                link("v", last)
                dve.wait_ge(moe_added, 1)
                link("v", V.tensor_tensor(x_row[:, :, :], x_row[:, :, :], mix[:, :, :], ALU.add))

            def line_coordinates(t):
                dve.wait_ge(outer_done, t + 1)
                o = outer[:, t % 2]
                at = 0
                for i in range(3):
                    last = V.tensor_tensor(lines[:, t, :, at:at + 3 - i], o[:, :, i, i + 1:4], o[:, :, i + 1:4, i],
                                           ALU.subtract)
                    at += 3 - i
                last.then_inc(lines_read, 1)

            def memory():
                plan = ROW_PLAN
                V.memset(gsum[:, :, 0:1], 0.0)
                for t in range(NT):
                    bank = full(dve, plan, ("pa", t))
                    drained(dve, plan, ("pa", t), "a")
                    V.tensor_tensor(vals[:, t, :, 0:DH], bank[:, 0:D].rearrange("p (h d) -> p h d", h=H),
                                    param("vb").rearrange("p (h d) -> p h d", h=H), ALU.add)
                    V.tensor_tensor(gate_in[:, t, :], bank[:, 448:464], param("mgb"), ALU.add)\
                        .then_inc(drained_v, 1)
                    bank = full(dve, plan, ("pb", t))
                    drained(dve, plan, ("pb", t), "a")
                    V.tensor_tensor(z[:, t, :], bank[:, 0:D], param("mvb"), ALU.add).then_inc(drained_v, 1)
                    if t >= 1:
                        line_coordinates(t - 1)
                line_coordinates(NT - 1)
                dve.wait_ge(lines_read, NT)
                square = feat_w[:, :, 0:2 * H * 6].rearrange("p t (h j) -> p t h j", j=6)
                flat = "p t h j -> p (t h) j"
                link("v", V.tensor_tensor(square, lines[:, :, :, :], lines[:, :, :, :], ALU.mult))
                V.tensor_reduce(norm[:, :].rearrange("p (t h) -> p t h", t=NT), square, AX_X, ALU.add)\
                    .then_inc(lines_sq, 1)
                dve.wait_ge(lines_sqrt, 1)
                link("v", V.tensor_scalar(norm[:, :], norm[:, :], 1e-12, None, ALU.max))
                link("v", V.reciprocal(norm[:, :], norm[:, :]))
                V.tensor_tensor(lines[:, :, :, :].rearrange(flat), lines[:, :, :, :].rearrange(flat),
                                norm[:, :].unsqueeze(2).broadcast_to([P, NT * 2 * H, 6]), ALU.mult)\
                    .then_inc(lines_done, 1)
                drained(dve, plan, ("jw", NC - 1), "a")
                products(V, feat_w, jlines[:, :, :, :]).then_inc(feat_w_done, 1)
                rate = param("decay")[0:FR, :]
                for ch in range(FCH):
                    for c in range(NC):
                        bank = full(dve, plan, ("fw", ch, c))
                        g = gsum[:, ch % 2]
                        V.tensor_tensor_scan(g[:, 1 + c * HALF:1 + (c + 1) * HALF],
                                             rate.broadcast_to([FR, HALF]), bank[0:FR, :],
                                             g[:, HALF:HALF + 1] if c else 0.0, ALU.mult, ALU.add)\
                            .then_inc(drained_v, 1)
                        drained(dve, plan, ("fw", ch, c), "v")
                        bank = full(dve, plan, ("fr", ch, c))
                        V.scalar_tensor_tensor(prod[0:FR, ch, c * HALF:(c + 1) * HALF], g[:, c * HALF:(c + 1) * HALF],
                                               rate, bank[0:FR, :], ALU.mult, ALU.mult).then_inc(drained_v, 1)
                bank = full(dve, plan, ("ms",))
                V.tensor_tensor(mem_in[:, :, :], bank[:, 0:NT * H].rearrange("p (t h) -> p t h", t=NT),
                                wide(param("mscale"), NT), ALU.mult).then_inc(drained_v, 1)
                dve.wait_ge(sig_done, 2)
                link("v", V.tensor_tensor(mem_in[:, :, :], mem_in[:, :, :], gate_in[:, :, :], ALU.mult))
                link("v", V.tensor_reduce(gate8[:, :], mem_in[:, :, :], AX_X, ALU.add))
                link("v", V.tensor_scalar(gate8[:, :], gate8[:, :], 1.0 / H, None, ALU.mult))
                for t in range(NT):
                    last = V.tensor_scalar(z[:, t, :], z[:, t, :], gate8[:, t:t + 1], None, ALU.mult)
                link("v", last)

            def attention():
                plan = ROW_PLAN
                u = 0
                for e in EVENTS:
                    kind = e[0]
                    if kind == "sm":
                        h, it = e[1], e[2]
                        both = full(dve, plan, e)
                        V.tensor_reduce(smax[:, it, h:h + 1], both[:, 0:(it + 1) * P], AX_X, ALU.max)\
                            .then_inc(drained_v, 1)
                    elif kind == "mt":
                        drained(dve, plan, e, "a")
                        V.scalar_tensor_tensor(neg_lo[:, :], full(dve, plan, e)[0:2, :], -1.0,
                                               neg_hi[:, :].bitcast(F32), ALU.mult, ALU.subtract)\
                            .then_inc(drained_v, 1)
                    elif kind == "pv":
                        h, jt = e[1], e[2]
                        u += 1
                        if jt == NT - 1:
                            dve.wait_ge(pt_read, u)
                            acc = pv_acc[h % 2]
                            link("v", V.reciprocal(rden[:, h % 2, :], acc[:, :, DH]))
                            V.tensor_tensor(seq[:, h % 2], acc[:, :, 0:DH],
                                            rden[:, h % 2, :].unsqueeze(2).broadcast_to([P, NT, DH]), ALU.mult)\
                                .then_inc(pv_read, 1)
                            dve.wait_ge(pv_read, h + 1)
                            part = z[:, :, h * DH:(h + 1) * DH]
                            last = V.tensor_tensor(part, part, seq[:, h % 2], ALU.add)
                last.then_inc(z_done, 1)

            def layer1():
                plan = ROW_PLAN
                normalise(x_row, xn1, 3)
                memory()
                for g in range(2):
                    for i, (hi, lo, signal) in enumerate(((q_hi, q_lo, q_in), (k_hi, k_lo, k_in))):
                        if g:
                            for slot in range(4):
                                dve.wait_ge(signal[slot], 96)
                        for c in range(NC):
                            bank = full(dve, plan, ("qk", g, i, c))
                            drained(dve, plan, ("qk", g, i, c), "a")
                            half = slice(c * HALF, (c + 1) * HALF)
                            V.scalar_tensor_tensor(lo[:, half], bank, param("qkb")[:, 2 * i + g:2 * i + g + 1],
                                                   hi[:, half].bitcast(F32), ALU.add, ALU.subtract)\
                                .then_inc(drained_v, 1)
                attention()
                scale = param("scale")
                w1, w2 = weight("g1", KD), weight("g2", MF)
                for k in range(KD):
                    for c in range(NC):
                        bank = full(dve, plan, ("e1", k, c))
                        half = slice(c * HALF, (c + 1) * HALF)
                        V.scalar_tensor_tensor(g1[:, k, half], bank, scale, w1[:, k, half], ALU.mult, ALU.add)\
                            .then_inc(drained_v, 1)
                for q in range(MF // 2):
                    bank = full(dve, plan, ("e2", q))
                    V.scalar_tensor_tensor(g2[:, 2 * q:2 * q + 2, :], bank.rearrange("p (k n) -> p k n", k=2), scale,
                                           w2[:, 2 * q:2 * q + 2, :], ALU.mult, ALU.add).then_inc(drained_v, 1)
                link("v", V.tensor_tensor(x_row[:, :, :], x_row[:, :, :], wide(out_bias[:, :], NT), ALU.add))
                for c in range(NC):
                    dve.wait_ge(h_read, MF * (NC + c + 1))
                    for a in range(2):
                        i = 2 * c + a
                        V.tensor_tensor(done[:, i, :, :], ps[:, a, :].rearrange("p (t d) -> p t d", t=2),
                                        x_row[:, 2 * i:2 * i + 2, :], ALU.add).then_inc(out_sum, 1)
                        dve.wait_ge(out_sum, i + 1)
                        dve.sem_inc(acc_read, 1)

            with dve.Fori(0, B) as b:
                V.memset(raw[:, :, 0:NCONV - 1], 0.0).then_inc(pad_zero, 1)
                dve.wait_ge(x_loaded, 16)
                normalise(x_row, mix, 1)
                for c in range(NC):
                    layer0(c)
                finish_layer0()
                layer1()
                end_round(dve, b + 2)

        @block.gpsimd
        def _(pool):
            G = nc.gpsimd
            end_round(pool, 1)

            def layer0(c):
                plan = ROW_PLAN
                w = c * (NS + 1)
                pool.wait_ge(silu_done, MI * (c + 1))
                if c:
                    pool.wait_ge(state_read, w - 2)
                for d in range(MI):
                    last = G.tensor_scalar(state[:, w % 3, d, :], xm[:, d, :], param("dskip")[:, d:d + 1], None,
                                           ALU.mult)
                last.then_inc(skip_done, 1)
                pool.wait_ge(du_done, MI * (c + 1))
                for n in range(NS):
                    j, w = c * NS + n, c * (NS + 1) + n + 1
                    drained(pool, plan, ("B", c, n), "a")
                    if w >= 3:
                        pool.wait_ge(state_read, w - 2)
                    G.tensor_tensor(state[:, w % 3, :, :], du[:, :, :], wide(b_wide[:, j % 3, :], MI), ALU.mult)\
                        .then_inc(driven, 1)

            def layer1():
                plan = ROW_PLAN
                pool.wait_ge(xn_done, NT + 1)
                G.memset(vals[:, :, :, DH], 1.0)
                G.memset(odd_hi[:, :], 0.0)
                G.memset(even[:, :], 0.0).then_inc(l1_clear, 1)
                for t in range(NT):
                    drained(pool, plan, ("pb", t), "a")
                    if t >= 2:
                        pool.wait_ge(lines_read, t - 1)
                    a = pt1[:, t, :].rearrange("p (l i) -> p l i", i=4)
                    b = pt2[:, t, :].rearrange("p (l i) -> p l i", i=4)
                    G.tensor_tensor(outer[:, t % 2], a.unsqueeze(3).broadcast_to([P, 2 * H, 4, 4]),
                                    b.unsqueeze(2).broadcast_to([P, 2 * H, 4, 4]), ALU.mult)\
                        .then_inc(outer_done, 1)
                pool.wait_ge(lines_done, 1)
                products(G, feat_r, lines[:, :, H:2 * H, :]).then_inc(feat_r_done, 1)
                pool.wait_ge(rows_in, 160)
                drained(pool, plan, ("ms",), "v")
                G.memset(ks[:, :, :].bitcast(F32), 1.0).then_inc(ks_ones, 1)

            with pool.Fori(0, B) as b:
                pool.wait_ge(xn_done, NT)
                link("p", G.tensor_tensor(x_row[:, :, :], x_row[:, :, :], moe[:, :, :], ALU.add))
                G.memset(moe[:, :, :], 0.0).then_inc(moe_added, 1)
                for c in range(NC):
                    layer0(c)
                layer1()
                end_round(pool, b + 2)


def _slices(w):
    k = w.shape[0] // P
    return w.reshape(k, P, -1).transpose(1, 0, 2).reshape(P, -1)


def _cols(v):
    return v.reshape(-1, P).T


def kernel(**inputs):
    import numpy as np
    import concourse.bacc as bacc
    from concourse.bass_utils import run_bass_kernel_spmd

    a = {k: np.asarray(v) for k, v in inputs.items()}
    f32 = np.float32

    def everywhere(v):
        return np.broadcast_to(v.reshape(1, -1), (P, v.size))

    def padded(m):
        out = np.zeros((P, m.shape[1]), f32)
        out[:m.shape[0]] = m
        return out

    qkv, in_w = a["L1_attn_qkv_w"], a["L0_attn_in_proj_w"]
    w = {
        "in": _slices(in_w.T), "xproj": _slices(a["L0_attn_x_proj_w"].T), "dt": padded(a["L0_attn_dt_proj_w"].T),
        "oproj": _slices(a["L0_attn_out_proj_w"].T), "f1": _slices(a["L0_attn_ffn_w1"].T),
        "f2": _slices(a["L0_attn_ffn_w2"].T), "qk": _slices(qkv[:, 0:2 * D]),
        "ta": _slices(np.concatenate([qkv[:, 2 * D:], a["L1_attn_w1_read"], a["L1_attn_w2_write"],
                                      a["L1_attn_w2_read"], a["L1_attn_memg_w"]], 1)),
        "tb": _slices(np.concatenate([a["L1_attn_memv_w"], a["L1_attn_w1_write"]], 1)),
        "out": _slices(a["L1_attn_out_w"]), "g1": _slices(a["L1_ffn_W1"].T), "g2": _slices(a["L1_ffn_W2"].T),
    }
    jdiag = np.zeros((P, 6 * H), f32)
    for h in range(H):
        jdiag[6 * h:6 * h + 6, 6 * h:6 * h + 6] = a["L1_attn_J"]
    sumpq = np.zeros((P, FCH, H), f32)
    pairs = [(i, j) for i in range(6) for j in range(i, 6)]
    for n, (i, j) in enumerate(pairs):
        for h in range(H):
            sumpq[(n % 7) * H + h, n // 7, h] = 1.0 if i == j else 2.0
    pick = np.zeros((P, 2 * NS), f32)
    for n in range(2 * NS):
        pick[n, n] = pick[2 * NS + n, n] = 1.0
    above = np.triu(np.full((P, P), -1e30, f32), 1)
    rate = np.zeros((P, 1), f32)
    for n in range(7):
        rate[n * H:(n + 1) * H, 0] = a["L1_attn_decays"]
    qkv_b = a["L1_attn_qkv_b"]
    p = {
        "convw": a["L0_attn_conv_w"].reshape(MI, P, NCONV).transpose(1, 0, 2).reshape(P, -1),
        "convb": _cols(a["L0_attn_conv_b"]), "dtb": _cols(a["L0_attn_dt_proj_b"]), "alog": _slices(a["L0_attn_A_log"]),
        "dskip": _cols(a["L0_attn_D"]), "fb1": _cols(a["L0_attn_ffn_b1"]), "qkb": _cols(qkv_b[0:2 * D]),
        "gb1": _cols(a["L1_ffn_b1"]), "scale": everywhere(a["L1_ffn_scale"]), "decay": rate,
        "fb2": everywhere(a["L0_attn_ffn_b2"]), "vb": everywhere(qkv_b[2 * D:]),
        "mvb": everywhere(a["L1_attn_memv_b"]), "mgb": everywhere(a["L1_attn_memg_b"]),
        "mscale": everywhere(a["L1_attn_mem_scale"]), "outb": everywhere(a["L1_attn_out_b"]),
        "gb2": everywhere(a["L1_ffn_b2"]), "jdiag": jdiag, "ident": np.eye(P, dtype=f32), "mask": above,
        "maskt": above.T, "sumpq": sumpq.reshape(P, -1), "pick": pick, "mean": np.full((P, P), 1.0 / P, f32),
        "ew": a["L0_ffn_expert_weights"].reshape(NT, P, 2).transpose(1, 0, 2).reshape(P, -1),
    }
    arrays = {
        "x": a["L0_attn_seq_embeddings"],
        "weights": np.concatenate([w[n] for n, _ in WEIGHTS], 1),
        "params": np.concatenate([p[n] for n, _ in PARAMS], 1),
        "expert1": a["L0_ffn_w1"].reshape(KD, P, ME * P).transpose(1, 0, 2),
        "expert2": a["L0_ffn_w2"].reshape(ME, P, D).transpose(1, 0, 2),
    }
    arrays = {f"in_{k}": np.ascontiguousarray(v) for k, v in arrays.items()}
    nc = bacc.Bacc("TRN2", target_bir_lowering=False, num_devices=1)
    args = [nc.dram_tensor(k, v.shape, mybir.dt.from_np(v.dtype), kind="ExternalInput").ap()
            for k, v in arrays.items()]
    out = nc.dram_tensor("out", (B, S, D), F32, kind="ExternalOutput").ap()
    build(nc, *args, out)
    return run_bass_kernel_spmd(nc, [arrays], core_ids=[0]).results[0]["out"]
```

```python
from contextlib import ExitStack

import concourse.bass as bass
from concourse import mybir

F32 = mybir.dt.float32
F32R = mybir.dt.float32r
BF16 = mybir.dt.bfloat16
ALU = mybir.AluOpType
ACT = mybir.ActivationFunctionType
AX_X = mybir.AxisListType.X

P = 128
B, S, D = 8, 1024, 256
NT = S // P
KD = D // P
HALF = 512
NC = S // HALF
TC = HALF // P
DI, NS, DTR, NCONV = 512, 16, 64, 4
MI = DI // P
FF = 1024
MF = FF // P
ME = 2048 // P
H, DH, NG = 16, 16, 8
VC = 2 * (DH + 1)
VW = 64
SLOTS = 4
NPQ = 21
FCH = 3
FR = 7 * H
EPS = 1e-5
CAP = 30.0
LN_UNITS = [("xt", c, k) for c in range(NC) for k in range(KD)]

WEIGHTS = [("in", KD * 2 * DI), ("xproj", MI * (DTR + 2 * NS)), ("dt", DI), ("oproj", MI * D), ("qk", KD * 2 * D), ("ta", KD * 464), ("tb", KD * 320), ("out", KD * D),
           ("g1", KD * FF), ("g2", MF * D), ("f1", KD * FF), ("f2", MF * D)]
PARAMS = [("convw", MI * NCONV), ("convb", MI), ("dtb", MI), ("alog", MI * NS), ("dskip", MI), ("fb1", MF),
          ("qkb", 4), ("gb1", MF), ("scale", 1), ("decay", 1), ("fb2", D), ("vb", D), ("mvb", D), ("mgb", H),
          ("mscale", H), ("outb", D), ("gb2", D), ("jdiag", 6 * H), ("ident", P), ("mask", P), ("maskt", P),
          ("sumpq", FCH * H), ("sel", VC), ("pick", 2 * NS), ("mean", P), ("ew", 2 * NT)]


def columns(layout):
    at, out = 0, {}
    for name, n in layout:
        out[name] = (at, at + n)
        at += n
    return out, at


W_AT, W_ALL_COLS = columns(WEIGHTS)
W_COLS = W_AT["f1"][0]
P_AT, P_COLS = columns(PARAMS)


def ring_plan(units):
    plan, owner, count = {}, {}, {"a": 0, "v": 0}
    for n, (name, banks, drainers) in enumerate(units):
        need = {"a": 0, "v": 0}
        for bank in banks:
            for who, k in owner.get(bank, {}).items():
                need[who] = max(need[who], k)
        for who in drainers:
            count[who] += 1
        for bank in banks:
            owner[bank] = {who: count[who] for who in drainers}
        assert name not in plan
        plan[name] = (banks, n + 1, need, dict(owner[banks[0]]))
    return plan


def narrow(names, start=0):
    return [(name, [4 + (start + i) % 4], who) for i, (name, who) in enumerate(names)]


def moe_names():
    out = [(u, "a") for u in LN_UNITS]
    for c in range(NC):
        out += [(("h", c, m), "a") for m in range(ME)]
    return out


def layer0_names():
    out = [(u, "a") for u in LN_UNITS]
    for c in range(NC):
        out += [(("xm", c, m), "a") for m in range(MI)]
        out += [(("res", c, t), "a") for t in range(TC)]
        out += [(("xd", c), "v")]
        out += [(("dl", c, m), "v") for m in range(MI)]
        for n in range(NS):
            out += [(("B", c, n), "a"), (("C", c, n), "v")]
        out += [(("yt", c, m), "a") for m in range(MI)]
        out += [(("m", c, k), "a") for k in range(KD)]
        out += [(("h", c, m), "a") for m in range(MF)]
    return out + [(("mu",), "v"), (("var",), "v")]


def layer1_names():
    out = [(("1",) + u, "a") for u in LN_UNITS]
    for t in range(NT):
        out += [(("pa", t), "av"), (("pb", t), "av")]
    out += [(("lt", c), "a") for c in range(NC)]
    out += [(("jw", c), "a") for c in range(NC)]
    for ch in range(FCH):
        for c in range(NC):
            out += [(("fw", ch, c), "v"), (("fr", ch, c), "v")]
    out += [(("qk", 0, i, c), "av") for i in range(2) for c in range(NC)]
    out += [(("ms",), "v")]
    return out + [(("qk", 1, i, c), "av") for i in range(2) for c in range(NC)]


def attention_events():
    ev = []

    def maxima(g):
        return [("sm", 2 * g + p, it) for p in range(2) for it in range(NT)]

    def exps(g):
        return [("st", 2 * g + p, jt) for p in range(2) for jt in range(NT)]

    for g in (0, 1):
        ev += maxima(g) + [("mt", g)]
    for g in range(NG):
        st, sm = exps(g), maxima(g + 2) if g + 2 < NG else []
        for i in range(len(st)):
            ev.append(st[i])
            if sm:
                ev.append(sm[i])
        if sm:
            ev.append(("mt", g + 2))
    out, late, turn = [], [], []
    for e in ev + [None] * (PV_LAG + TURN_LAG):
        if e:
            out.append(e)
        if e is None or e[0] == "st":
            if e:
                late.append(("pv",) + e[1:])
            if turn and turn[0][0] == 0:
                out.append(("ot", turn.pop(0)[1]))
            turn = [(n - 1, g) for n, g in turn]
            if late and (e is None or len(late) > PV_LAG):
                pv = late.pop(0)
                out.append(pv)
                if pv[1] % 2 == 1 and pv[2] == NT - 1:
                    turn.append((TURN_LAG - 1, pv[1] // 2))
    return out


PV_LAG = 2
TURN_LAG = 2
EVENTS = attention_events()
EXPS = [e for e in EVENTS if e[0] == "st"]
PT_RING = 3
LO_POOL = (4, 5, 6, 7)
WIDE = [[4, 5], [6, 7], [0, 1]]


def wide_units():
    who = {"sm": "v", "st": "a", "mt": "av", "ot": "v"}
    units = [e for e in EVENTS if e[0] in who]
    return [(e, WIDE[i % 3], who[e[0]]) for i, e in enumerate(units)]


def tail_names():
    out = [(("zt", k, c), "a") for c in range(NC) for k in range(KD)]
    out += [(("e1", k, c), "v") for k in range(KD) for c in range(NC)]
    out += [(("e2", q), "v") for q in range(MF // 2)]
    for c in range(NC):
        out += [(("g", c, m), "a") for m in range(MF)]
    return out


MOE_PLAN = ring_plan(narrow(moe_names()))
_units = narrow(layer0_names())
_units += narrow(layer1_names(), len(_units))
_units += wide_units()
_units += narrow(tail_names())
ROW_PLAN = ring_plan(_units)


def lo_count(u, who):
    return sum(1 for e in EXPS[:u] if (e[2] in LO_POOL) == (who == "p"))


def build(nc, x_in, w_in, p_in, moe1_in, moe2_in, resid, out):
    ctx = ExitStack()
    with ctx:
        def sb(name, shape, dt=F32, where=ctx):
            return where.enter_context(nc.sbuf_tensor(name, shape, dt))

        def sem(name):
            return ctx.enter_context(nc.semaphore(name))

        w_all = sb("w_all", [P, W_COLS])
        mlp0_at = -(-nc.sbuf_base // 32) * 32
        sb("mlp0_place", [P, W_ALL_COLS - W_COLS + 8])
        p_all = sb("p_all", [P, P_COLS])
        x_row = sb("x_row", [P, NT, D])
        xT = sb("xT", [P, KD, S + 1])
        neg_a = sb("neg_a", [P, MI * NS])
        ident_b = sb("ident_b", [P, P], BF16)
        mask_b = sb("mask_b", [P, 2, P], BF16)
        pick_r = sb("pick_r", [2 * 2 * NS, 2 * NS], F32R)
        out_bias = sb("out_bias", [P, D])
        ew_sum = sb("ew_sum", [P, NT])
        ln_stats = sb("ln_stats", [P, NT, 6])
        ln_mv = sb("ln_mv", [P, NT, 2])
        ln_std = sb("ln_std", [P, NT])
        ln_rstd = sb("ln_rstd", [P, NT])
        row_stats = sb("row_stats", [P, 4, 6])
        row_mv = sb("row_mv", [P, 2])
        row_q = sb("row_q", [P, 8])

        def weight(name, k=None):
            a, b = W_AT[name]
            v = w_all[:, a:b]
            return v if k is None else v.rearrange("p (k n) -> p k n", k=k)

        def param(name):
            a, b = P_AT[name]
            return p_all[:, a:b]

        ident = param("ident")

        arena_at = -(-nc.sbuf_base // 32) * 32
        arena_end = nc.sbuf_usable_end // 32 * 32
        sb("arena", [P, (arena_end - arena_at) // 4])

        def place(at, *buffers):
            views = []
            for name, shape, *dt in buffers:
                views.append(nc.alloc_sbuf_tensor_at(name, shape, dt[0] if dt else F32, offset=at))
                n = 4
                for extent in shape[1:]:
                    n *= extent
                at += -(-n // 32) * 32
            assert at <= arena_end, (at, arena_end)
            return views + [at]

        w_mlp0, = place(mlp0_at, ("w_mlp0", [P, W_ALL_COLS - W_COLS]))[:-1]
        k_odd, = place(mlp0_at, ("k_odd", [P, SLOTS, S], F32R))[:-1]
        w_up0 = w_mlp0[:, 0:KD * FF].rearrange("p (k n) -> p k n", k=KD)
        w_down0 = w_mlp0[:, KD * FF:].rearrange("p (k n) -> p k n", k=MF)

        moe1, moe2, moe_xn, moe_h, _ = place(
            arena_at, ("moe1", [P, KD, ME * P]), ("moe2", [P, ME, D]), ("moe_xn", [P, NT, D]),
            ("moe_h", [P, 3, HALF]))

        (mix, raw, xm, delta, du, gate, dt_low, bc_parts, b_wide, decay, state, carry, mT, h0, _) = place(
            arena_at, ("mix", [P, NT, D]), ("raw", [P, MI, NCONV - 1 + HALF]), ("xm", [P, MI, HALF]),
            ("delta", [P, MI, HALF]), ("du", [P, MI, HALF]), ("gate", [P, TC, DI]), ("dt_low", [DTR, HALF]),
            ("bc_parts", [4 * NS, HALF], F32R), ("b_wide", [P, 3, HALF]), ("decay", [P, 2, MI, HALF]),
            ("state", [P, 3, MI, HALF]), ("carry", [P, NS, MI]), ("mT", [P, KD, HALF]), ("h0", [P, 3, HALF]))
        yT = xm

        (vals, z, rows, rden, seq, smax, body_at) = place(
            arena_at, ("vals", [P, NT * H * VC + VW], F32R), ("z", [P, NT, D]), ("rows", [P, 2, S], F32R),
            ("rden", [P, NT, 2]), ("seq", [P, NT, 2, DH]), ("smax", [P, NT, H]))
        vals_pad = vals[:, NT * H * VC:]
        vals_by_head = vals[:, 0:NT * H * VC].rearrange("p (t h s d) -> p t h s d", t=NT, h=H, s=2)
        even, odd, odd_hi = (rows[0:8, 0, :].bitcast(F32), rows[0:8, 1, 0:D].bitcast(F32),
                             rows[0:8, 1, D:2 * D].bitcast(F32))
        neg_hi, neg_lo = rows[32:34, 0, :], rows[32:34, 1, :]
        (xn1, pt1, pt2, outer, lines, norm, linesT, jlines, feat_w, feat_r, gsum, prod, gate_in, mem_in,
         gate8, _) = place(
            body_at, ("xn1", [P, NT, D]), ("pt1", [P, NT, 2 * 4 * H]), ("pt2", [P, NT, 2 * 4 * H]),
            ("outer", [P, 2, 2 * H, 4, 4]), ("lines", [P, NT, 2 * H, 6]), ("norm", [P, NT * 2 * H]),
            ("linesT", [6 * H, S]), ("jlines", [P, NT, H, 6]), ("feat_w", [P, NT, NPQ * H]),
            ("feat_r", [P, NT, NPQ * H]), ("gsum", [FR, 2, S + 1]), ("prod", [P, FCH, S]),
            ("gate_in", [P, NT, H]), ("mem_in", [P, NT, H]), ("gate8", [P, NT]))
        v_sum = feat_r[:, :, 0:D]
        qs, k_even, pt_at = place(body_at, ("qs", [P, SLOTS, S], F32R), ("k_even", [P, SLOTS, S], F32R))
        exps, exps_hi, *parts1, oT, _ = place(
            pt_at, ("exps", [P, PT_RING, S]), ("exps_hi", [P, PT_RING, S], F32R),
            *[(f"part1{i}", [P, S], F32R) for i in range(4)], ("oT", [P, S]))
        ks = [k_even, k_odd]
        exps_lo, _ = place(pt_at, ("exps_lo", [P, PT_RING, S], F32R))
        *parts0, _ = place(pt_at, *[(f"part0{i}", [P, S], F32R) for i in range(4)])
        parts = [parts0, parts1]
        zT, g1, g2, h1, done, _ = place(
            body_at, ("zT", [P, KD, S]), ("g1", [P, KD, FF]), ("g2", [P, MF, D]), ("h1", [P, 3, HALF]),
            ("done", [P, NT // 2, 2, D]))

        ps = ctx.enter_context(nc.psum_tensor("ps", [P, 8, 512], F32))
        y_acc = ps[:, 0:4, :]
        mlp_acc = [ps[:, 0:2, :], ps[:, 0:2, :]]
        pv_acc = ps[0:VW, 2:4, :].rearrange("p b n -> p (b n)")

        def acc_tile(tt):
            return ps[:, tt // 2, (tt % 2) * D:(tt % 2 + 1) * D]

        params_in = sem("params_in")
        weights_in = sem("weights_in")
        mlp0_in = sem("mlp0_in")
        moe_in = sem("moe_in")
        setup_v = sem("setup_v")
        setup_a = sem("setup_a")
        setup_p = sem("setup_p")
        round_done = sem("round_done")
        round_go = sem("round_go")
        round_seen = sem("round_seen")
        x_loaded = sem("x_loaded")
        chain_v = sem("chain_v")
        chain_a = sem("chain_a")
        chain_p = sem("chain_p")
        ring_filled = sem("ring_filled")
        drained_a = sem("drained_a")
        drained_v = sem("drained_v")
        ln_var = sem("ln_var")
        ln_sqrt = sem("ln_sqrt")
        xn_done = sem("xn_done")
        resid_in = sem("resid_in")
        resid_out = sem("resid_out")
        pad_zero = sem("pad_zero")
        tap_done = sem("tap_done")
        conv_done = sem("conv_done")
        silu_done = sem("silu_done")
        gate_done = sem("gate_done")
        bc_hi = sem("bc_hi")
        dt_done = sem("dt_done")
        dl_clamped = sem("dl_clamped")
        dl_log = sem("dl_log")
        du_done = sem("du_done")
        skip_done = sem("skip_done")
        decay_done = sem("decay_done")
        driven = sem("driven")
        scanned = sem("scanned")
        weighed = sem("weighed")
        state_read = sem("state_read")
        y_gated = sem("y_gated")
        h_read = sem("h_read")
        acc_read = sem("acc_read")
        row_sum = sem("row_sum")
        l1_clear = sem("l1_clear")
        rows_in = sem("rows_in")
        outer_done = sem("outer_done")
        lines_read = sem("lines_read")
        lines_sq = sem("lines_sq")
        lines_sqrt = sem("lines_sqrt")
        lines_done = sem("lines_done")
        feat_w_done = sem("feat_w_done")
        feat_r_done = sem("feat_r_done")
        sig_done = sem("sig_done")
        gates_read = sem("gates_read")
        k_odd_clear = sem("k_odd_clear")
        stacks_clear = sem("stacks_clear")
        pt_read = sem("pt_read")
        exps_hi_done = sem("exps_hi_done")
        exps_lo_v = sem("exps_lo_v")
        exps_lo_p = sem("exps_lo_p")
        v_summed = sem("v_summed")
        vals_hi = sem("vals_hi")
        vals_done = sem("vals_done")
        oT_done = sem("oT_done")
        seq_done = sem("seq_done")
        z_done = sem("z_done")
        out_sum = sem("out_sum")
        out_left = sem("out_left")
        q_in = [sem(f"q_in{g}") for g in range(NG)]
        k_in = [sem(f"k_in{g}") for g in range(NG)]
        neg_in = [sem(f"neg_in{g}") for g in range(NG)]
        per_round = [
            x_loaded, mlp0_in, chain_v, chain_a, chain_p, ring_filled, drained_a,
            drained_v, ln_var, ln_sqrt, xn_done, resid_in, pad_zero,
            tap_done, conv_done, silu_done, gate_done, bc_hi, dt_done,
            dl_clamped, dl_log, du_done, skip_done, decay_done, driven,
            scanned, weighed, state_read, y_gated, h_read, acc_read,
            row_sum, l1_clear, rows_in, outer_done, lines_read, lines_sq,
            lines_sqrt, gates_read, lines_done, feat_w_done, feat_r_done, sig_done, k_odd_clear, stacks_clear,
            pt_read, exps_hi_done, exps_lo_v, exps_lo_p, v_summed, vals_hi,
            vals_done, oT_done, seq_done, z_done, out_sum, out_left] + q_in + k_in + neg_in

        def claim(plan, unit):
            banks, _, need, _ = plan[unit]
            if need["a"]:
                nc.tensor.wait_ge(drained_a, need["a"])
            if need["v"]:
                nc.tensor.wait_ge(drained_v, need["v"])
            return ps[:, banks[0]:banks[-1] + 1, :].rearrange("p b n -> p (b n)")

        def full(eng, plan, unit):
            banks, ready, _, _ = plan[unit]
            eng.wait_ge(ring_filled, ready)
            return ps[:, banks[0]:banks[-1] + 1, :].rearrange("p b n -> p (b n)")

        def drained(eng, plan, unit, who):
            eng.wait_ge(drained_a if who == "a" else drained_v, plan[unit][3][who])

        chain = {"v": 0, "a": 0, "p": 0}

        def link(who, ins):
            chain[who] += 1
            signal = {"v": chain_v, "a": chain_a, "p": chain_p}[who]
            ins.then_inc(signal, 1)
            {"v": nc.vector, "a": nc.scalar, "p": nc.gpsimd}[who].wait_ge(signal, chain[who])

        def end_round(eng, n, leader=False):
            chain.update(v=0, a=0, p=0)
            eng.sem_inc(round_done, 1)
            if leader:
                eng.wait_ge(round_done, 5)
                for one in per_round + [round_done]:
                    eng.sem_clear(one)
                eng.sem_inc(round_go, 1)
            else:
                eng.wait_ge(round_go, n)
                eng.sem_inc(round_seen, 1)

        def wide(ap, middle):
            return ap.unsqueeze(1).broadcast_to([ap.shape[0], middle, ap.shape[1]])

        def tokens(t, n=P, shift=1):
            return slice(shift + t * P, shift + t * P + n)

        def products(eng, dst, c6):
            by_q = dst[:, :, :].rearrange("p t (q h) -> p t q h", h=H)
            at = 0
            for p in range(6):
                n = 6 - p
                last = eng.tensor_tensor(by_q[:, :, at:at + n, :],
                                         c6[:, :, :, p].unsqueeze(2).broadcast_to([P, NT, n, H]),
                                         c6[:, :, :, p:6].rearrange("p t h q -> p t q h"), ALU.mult)
                at += n
            return last

        block = ctx.enter_context(nc.Block())

        @block.sync
        def _(sp):
            sp.dma_start(p_all[:, :], p_in).then_inc(params_in, 16)
            sp.dma_start(x_row[:, :, :], x_in[0].rearrange("(t p) d -> p t d", p=P)).then_inc(x_loaded, 16)
            sp.dma_start(moe1[:, :, :], moe1_in).then_inc(moe_in, 16)
            sp.dma_start(moe2[:, :, :], moe2_in).then_inc(moe_in, 16)
            sp.dma_start(w_all[:, :], w_in[:, 0:W_COLS]).then_inc(weights_in, 16)
            sp.dma_start(w_mlp0[:, :], w_in[:, W_COLS:]).then_inc(weights_in, 16)
            sp.dma_start(resid[1:B], x_in[1:B]).then_inc(resid_out, 16)
            sp.wait_ge(x_loaded, 16)
            sp.wait_ge(acc_read, 2 * NC)
            sp.dma_start(resid[0].rearrange("(t p) d -> p t d", p=P), x_row[:, :, :]).then_inc(resid_out, 16)
            sp.wait_ge(resid_out, 32)
            end_round(sp, 1, leader=True)
            with sp.Fori(0, B) as b:
                sp.dma_start(mix[:, :, :], x_in[bass.ds(b, 1), :, :].rearrange("a (t p) d -> p (a t) d", p=P))\
                  .then_inc(x_loaded, 16)
                sp.dma_start(x_row[:, :, :], resid[bass.ds(b, 1), :, :].rearrange("a (t p) d -> p (a t) d", p=P))\
                  .then_inc(resid_in, 16)
                sp.wait_ge(xn_done, NT + 1)
                sp.wait_ge(l1_clear, 1)
                for r in range(8):
                    sp.dma_start(even[r:r + 1, (r % 4) * D:(r % 4 + 1) * D], xn1[1 + 2 * r:2 + 2 * r, 0, :])\
                      .then_inc(rows_in, 16)
                sp.dma_start(odd, xn1[2:18:2, 0, :]).then_inc(rows_in, 16)
                sp.dma_start(odd_hi[4:8, :], xn1[10:18:2, 0, :]).then_inc(rows_in, 16)
                sp.wait_ge(k_odd_clear, 1)
                sp.wait_ge(stacks_clear, 1)
                def stack(g):
                    group = g // 4
                    q_hi, q_lo, k_hi, k_lo = parts[group]
                    for i in range(2):
                        for who in "av":
                            drained(sp, ROW_PLAN, ("qk", group, i, 1), who)
                    if g >= SLOTS:
                        full(sp, ROW_PLAN, ("st", 2 * (g - SLOTS) + 1, NT - 1))
                        for row in (48, 112):
                            sp.dma_start(qs[row:row + 2, g % SLOTS, :].bitcast(F32),
                                         k_odd[0:2, g % SLOTS, :].bitcast(F32)).then_inc(q_in[g], 16)
                    for half in range(2):
                        for hi, lo, dst, signal, order in ((q_hi, q_lo, qs, q_in, "hhl"),
                                                           (k_hi, k_lo, ks[half], k_in, "hlh")):
                            j = 2 * (g % 4) + half
                            for r, part in enumerate(order):
                                src = hi if part == "h" else lo
                                row = 64 * half + DH * r
                                sp.dma_start(dst[row:row + DH, g % SLOTS, :].bitcast(F32),
                                             src[DH * j:DH * (j + 1), :].bitcast(F32)).then_inc(signal[g], 16)

                def maxima_rows(g):
                    for who in "av":
                        drained(sp, ROW_PLAN, ("mt", g), who)
                    for row, part in ((48, neg_hi), (49, neg_lo)):
                        sp.dma_start(qs[row:128:64, g % SLOTS, :].bitcast(F32), part.bitcast(F32))\
                          .then_inc(neg_in[g], 16)

                stack(0)
                stack(1)
                maxima_rows(0)
                stack(2)
                maxima_rows(1)
                stack(3)
                for g in range(2, NG):
                    maxima_rows(g)
                    if g + 2 < NG:
                        stack(g + 2)
                for i in range(NT // 2):
                    sp.wait_ge(out_sum, i + 1)
                    sp.dma_start(
                        out[bass.ds(b, 1), 2 * i * P:(2 * i + 2) * P, :].rearrange("a (t p) d -> p (a t) d", p=P),
                        done[:, i, :, :]).then_inc(out_left, 16)
                    if i == 0:
                        sp.dma_start(w_mlp0[:, :], w_in[:, W_COLS:]).then_inc(mlp0_in, 16)
                sp.wait_ge(out_left, 16 * (NT // 2))
                sp.wait_ge(mlp0_in, 16)
                end_round(sp, b + 2, leader=True)

        @block.tensor
        def _(pe):
            mm, tp = nc.tensor.matmul, nc.tensor.transpose

            def normalised_T(plan, prefix, xn, base):
                for unit in LN_UNITS:
                    _, c, k = unit
                    bank = claim(plan, prefix + unit)
                    pe.wait_ge(xn_done, base + TC * (c + 1))
                    for tt in range(TC):
                        last = tp(bank[:, tt * P:(tt + 1) * P], xn[:, TC * c + tt, k * P:(k + 1) * P], ident)
                    last.then_inc(ring_filled, 1)

            def mlp(plan, tag, c, n_hidden, up, src, down, hidden, base, fresh):
                for m in range(n_hidden + 1):
                    if m < n_hidden:
                        bank = claim(plan, (tag, c, m))
                        for k in range(KD):
                            last = mm(bank, up[:, k, m * P:(m + 1) * P], src[k], start=(k == 0), stop=(k == KD - 1))
                        last.then_inc(ring_filled, 1)
                    if m >= 1:
                        j = m - 1
                        drained(pe, plan, (tag, c, j), "a")
                        for tt in range(TC):
                            last = mm(acc_tile(tt), hidden[:, (base + j) % 3, tt * P:(tt + 1) * P], down[:, j, :],
                                      start=(fresh and j == 0 and tt % 2 == 0), stop=(j == n_hidden - 1),
                                      skip_group_check=True)
                        last.then_inc(h_read, 1)

            pe.wait_ge(params_in, 16)
            normalised_T(MOE_PLAN, (), moe_xn, 0)
            pe.wait_ge(moe_in, 32)
            for c in range(NC):
                drained(pe, MOE_PLAN, ("xt", c, 1), "a")
                if c:
                    pe.wait_ge(acc_read, 2 * c)
                mlp(MOE_PLAN, "h", c, ME, moe1, [xT[:, k, tokens(TC * c, HALF)] for k in range(KD)], moe2, moe_h,
                    ME * c, True)
            pe.wait_ge(weights_in, 32)
            pe.wait_ge(setup_a, 6)
            pe.wait_ge(setup_v, 3)
            end_round(pe, 1)

            def layer0(c):
                plan = ROW_PLAN
                w = weight("in", KD)
                drained(pe, plan, ("xt", c, 1), "a")
                for m in range(MI):
                    bank = claim(plan, ("xm", c, m))
                    for k in range(KD):
                        last = mm(bank, w[:, k, m * P:(m + 1) * P], xT[:, k, tokens(TC * c, HALF)],
                                  start=(k == 0), stop=(k == KD - 1))
                    last.then_inc(ring_filled, 1)
                for t in range(TC):
                    bank = claim(plan, ("res", c, t))
                    for k in range(KD):
                        last = mm(bank, xT[:, k, tokens(TC * c + t)], w[:, k, DI:2 * DI],
                                  start=(k == 0), stop=(k == KD - 1))
                    last.then_inc(ring_filled, 1)
                w = weight("xproj", MI)
                bank = claim(plan, ("xd", c))
                for m in range(MI):
                    pe.wait_ge(silu_done, MI * c + m + 1)
                    last = mm(bank[0:DTR + 2 * NS, :], w[:, m, :], xm[:, m, :], start=(m == 0), stop=(m == MI - 1))
                last.then_inc(ring_filled, 1)
                w = weight("dt")
                for m in range(MI):
                    bank = claim(plan, ("dl", c, m))
                    pe.wait_ge(dt_done, c + 1)
                    mm(bank, w[0:DTR, m * P:(m + 1) * P], dt_low[:, :], start=True, stop=True)\
                        .then_inc(ring_filled, 1)

                def spread(n):
                    for name, col in (("B", n), ("C", NS + n)):
                        bank = claim(plan, (name, c, n))
                        mm(bank, pick_r[:, col:col + 1].broadcast_to([4 * NS, P]), bc_parts[:, :],
                           start=True, stop=True).then_inc(ring_filled, 1)

                def add_y(u):
                    for d in range(MI):
                        for t in range(TC):
                            last = mm(y_acc[:, t, d * P:(d + 1) * P],
                                      state[:, (c * (NS + 1) + u) % 3, d, t * P:(t + 1) * P], ident,
                                      is_transpose=True, start=(u == 0 and d == 0), stop=(u == NS),
                                      skip_group_check=True)
                    last.then_inc(state_read, 1)

                drained(pe, plan, ("xd", c), "v")
                spread(0)
                spread(1)
                if c:
                    pe.wait_ge(acc_read, 2 * c)
                    pe.wait_ge(y_gated, TC * c)
                pe.wait_ge(skip_done, c + 1)
                add_y(0)
                for n in range(NS):
                    if n + 2 < NS:
                        spread(n + 2)
                    pe.wait_ge(weighed, c * NS + n + 1)
                    add_y(n + 1)
                for d in range(MI):
                    bank = claim(plan, ("yt", c, d))
                    for t in range(TC):
                        if d == 0:
                            pe.wait_ge(y_gated, TC * c + t + 1)
                        last = tp(bank[:, t * P:(t + 1) * P], gate[:, t, d * P:(d + 1) * P], ident)
                    last.then_inc(ring_filled, 1)
                w = weight("oproj", MI)
                drained(pe, plan, ("yt", c, MI - 1), "a")
                for k in range(KD):
                    bank = claim(plan, ("m", c, k))
                    for d in range(MI):
                        last = mm(bank, w[:, d, k * P:(k + 1) * P], yT[:, d, :], start=(d == 0), stop=(d == MI - 1))
                    last.then_inc(ring_filled, 1)
                drained(pe, plan, ("m", c, KD - 1), "a")
                for tt in range(TC):
                    for k in range(KD):
                        mm(acc_tile(tt)[:, k * P:(k + 1) * P], mT[:, k, tt * P:(tt + 1) * P], ident,
                           is_transpose=True, start=(tt % 2 == 0 and k == 0), stop=False, skip_group_check=True)
                mlp(plan, "h", c, MF, w_up0, [mT[:, k, :] for k in range(KD)], w_down0, h0,
                    MF * c, False)

            def attention():
                plan = ROW_PLAN
                u = 0
                for e in EVENTS:
                    kind, h = e[0], e[1]
                    g = h // 2
                    if kind == "sm":
                        it = e[2]
                        both = claim(plan, e)
                        if it == 0 and h % 2 == 0:
                            pe.wait_ge(q_in[g], 96 if g < SLOTS else 128)
                            pe.wait_ge(k_in[g], 96)
                        width = (it + 1) * P
                        for at in range(0, width, HALF):
                            n = min(HALF, width - at)
                            mm(both[:, at:at + n], qs[:, g % SLOTS, it * P:(it + 1) * P],
                               ks[h % 2][:, g % SLOTS, at:at + n], start=True, stop=(at + n < width),
                               skip_group_check=True)
                        mm(both[:, it * P:width], ident_b[:, :], mask_b[:, 0, :], start=False, stop=True,
                           skip_group_check=True).then_inc(ring_filled, 1)
                    elif kind == "mt":
                        g = e[1]
                        both = claim(plan, e)
                        drained(pe, plan, ("sm", 2 * g + 1, NT - 1), "v")
                        for it in range(NT):
                            last = tp(both[0:2, it * P:(it + 1) * P], smax[:, it, 2 * g:2 * g + 2], ident)
                        last.then_inc(ring_filled, 1)
                    elif kind == "st":
                        jt = e[2]
                        both = claim(plan, e)
                        if jt == 0 and h % 2 == 0:
                            pe.wait_ge(neg_in[g], 32)
                        width = (NT - jt) * P
                        for at in range(0, width, HALF):
                            n = min(HALF, width - at)
                            mm(both[:, at:at + n], ks[h % 2][:, g % SLOTS, jt * P:(jt + 1) * P],
                               qs[:, g % SLOTS, jt * P + at:jt * P + at + n], start=True, stop=(at > 0),
                               skip_group_check=True)
                        mm(both[:, 0:P], ident_b[:, :], mask_b[:, 1, :], start=False, stop=True,
                           skip_group_check=True).then_inc(ring_filled, 1)
                    elif kind == "pv":
                        jt = e[2]
                        if u == 0:
                            pe.wait_ge(vals_done, 1)
                        pe.wait_ge(exps_hi_done, u + 1)
                        first = (jt * H + h) * VC
                        for part in (exps_hi, exps_lo):
                            if part is exps_lo:
                                if jt in LO_POOL:
                                    pe.wait_ge(exps_lo_p, lo_count(u + 1, "p"))
                                else:
                                    pe.wait_ge(exps_lo_v, lo_count(u + 1, "v"))
                            for at in (0, HALF):
                                lo = max(at, jt * P)
                                if jt == 0 and h and part is exps_hi:
                                    pe.wait_ge(oT_done, 2 * h - 1 + (at > 0))
                                if lo < at + HALF:
                                    last = mm(pv_acc[:, lo:at + HALF], vals[:, first:first + VW],
                                              part[:, u % PT_RING, lo - jt * P:at + HALF - jt * P],
                                              start=(jt == 0 and part is exps_hi),
                                              stop=(jt == NT - 1 or (at == 0 and jt == TC - 1)) and part is exps_lo,
                                              skip_group_check=True)
                        last.then_inc(pt_read, 1)
                        u += 1
                    else:
                        g = e[1]
                        both = claim(plan, e)
                        pe.wait_ge(oT_done, 4 * (g + 1))
                        for t in range(NT):
                            last = mm(both[:, t * VC:(t + 1) * VC], oT[:, t * P:(t + 1) * P], param("sel"),
                                      start=(t == 0), stop=(t == NT - 1), skip_group_check=True)
                        last.then_inc(ring_filled, 1)

            def layer1():
                plan = ROW_PLAN
                normalised_T(plan, ("1",), xn1, NT)
                ta, tb = weight("ta", KD), weight("tb", KD)
                for t in range(NT):
                    if t % TC == 0:
                        drained(pe, plan, ("1", "xt", t // TC, 1), "a")
                    bank = claim(plan, ("pa", t))
                    for k in range(KD):
                        last = mm(bank[:, 0:464], xT[:, k, tokens(t)], ta[:, k, :], start=(k == 0), stop=(k == KD - 1))
                    last.then_inc(ring_filled, 1)
                    bank = claim(plan, ("pb", t))
                    for k in range(KD):
                        mm(bank[:, 0:D], xT[:, k, tokens(t)], tb[:, k, 0:D], start=(k == 0), stop=(k == KD - 1),
                           skip_group_check=True)
                    for k in range(KD):
                        last = mm(bank[:, D:D + 64], xT[:, k, tokens(t, shift=0)], tb[:, k, D:D + 64],
                                  start=(k == 0), stop=(k == KD - 1), skip_group_check=True)
                    last.then_inc(ring_filled, 1)
                for c in range(NC):
                    bank = claim(plan, ("lt", c))
                    pe.wait_ge(lines_done, 1)
                    for tt in range(TC):
                        last = tp(bank[0:6 * H, tt * P:(tt + 1) * P],
                                  lines[:, TC * c + tt, 0:H, :].rearrange("p h j -> p (h j)"), ident)
                    last.then_inc(ring_filled, 1)
                for c in range(NC):
                    bank = claim(plan, ("jw", c))
                    drained(pe, plan, ("lt", c), "a")
                    for tt in range(TC):
                        last = mm(bank[:, tt * 96:(tt + 1) * 96], linesT[:, (TC * c + tt) * P:(TC * c + tt + 1) * P],
                                  param("jdiag")[0:96, :], start=True, stop=True)
                    last.then_inc(ring_filled, 1)
                pe.wait_ge(feat_r_done, 1)
                pe.wait_ge(feat_w_done, 1)
                for ch in range(FCH):
                    for c in range(NC):
                        for name, feat in (("fw", feat_w), ("fr", feat_r)):
                            bank = claim(plan, (name, ch, c))
                            for tt in range(TC):
                                last = tp(bank[0:FR, tt * P:(tt + 1) * P],
                                          feat[:, TC * c + tt, ch * FR:(ch + 1) * FR], ident)
                            last.then_inc(ring_filled, 1)
                w = weight("qk", KD)

                def project(g):
                    for i in range(2):
                        for c in range(NC):
                            bank = claim(plan, ("qk", g, i, c))
                            for k in range(KD):
                                last = mm(bank, w[:, k, i * D + g * P:i * D + (g + 1) * P],
                                          xT[:, k, tokens(TC * c, HALF)], start=(k == 0), stop=(k == KD - 1))
                            last.then_inc(ring_filled, 1)

                project(0)
                bank = claim(plan, ("ms",))
                drained(pe, plan, ("fr", FCH - 1, NC - 1), "v")
                pick = param("sumpq").rearrange("p (c h) -> p c h", c=FCH)
                for t in range(NT):
                    for ch in range(FCH):
                        last = mm(bank[:, t * H:(t + 1) * H], prod[0:FR, ch, t * P:(t + 1) * P], pick[0:FR, ch, :],
                                  start=(ch == 0), stop=(ch == FCH - 1))
                last.then_inc(ring_filled, 1)
                project(1)
                attention()
                for c in range(NC):
                    for k in range(KD):
                        bank = claim(plan, ("zt", k, c))
                        pe.wait_ge(z_done, 1)
                        for tt in range(TC):
                            last = tp(bank[:, tt * P:(tt + 1) * P], z[:, TC * c + tt, k * P:(k + 1) * P], ident)
                        last.then_inc(ring_filled, 1)
                pe.wait_ge(rows_in, 160)
                for k in range(KD):
                    for c in range(NC):
                        bank = claim(plan, ("e1", k, c))
                        mm(bank, odd[0:4, k * P:(k + 1) * P], even[0:4, c * HALF:(c + 1) * HALF],
                           start=True, stop=True).then_inc(ring_filled, 1)
                by_c = even[:, :].rearrange("e (r i c) -> e c r i", r=4, c=4)
                for q in range(MF // 2):
                    bank = claim(plan, ("e2", q))
                    for j in range(2):
                        last = mm(bank[:, j * D:(j + 1) * D].rearrange("p (r i) -> p r i", r=4),
                                  odd_hi[:, j * P:(j + 1) * P], by_c[:, q], start=True, stop=True)
                    last.then_inc(ring_filled, 1)
                for c in range(NC):
                    if c:
                        pe.wait_ge(acc_read, 4 + 2 * c)
                    else:
                        drained(pe, plan, ("st", H - 1, NT - 1), "a")
                        drained(pe, plan, ("sm", H - 1, NT - 1), "v")
                    drained(pe, plan, ("zt", 1, c), "a")
                    for tt in range(TC):
                        for k in range(KD):
                            mm(acc_tile(tt), zT[:, k, (TC * c + tt) * P:(TC * c + tt + 1) * P],
                               weight("out", KD)[:, k, :], start=(tt % 2 == 0 and k == 0), stop=False,
                               skip_group_check=True)
                    drained(pe, plan, ("e2", MF // 2 - 1), "v")
                    mlp(plan, "g", c, MF, g1, [xT[:, k, tokens(TC * c, HALF)] for k in range(KD)], g2, h1,
                        MF * (NC + c), False)

            with pe.Fori(0, B) as b:
                normalised_T(ROW_PLAN, (), mix, 0)
                for c in range(NC):
                    layer0(c)
                bank = claim(ROW_PLAN, ("mu",))
                pe.wait_ge(row_sum, 1)
                mm(bank[:, 0:1], param("mean"), row_mv[:, 0:1], start=True, stop=True).then_inc(ring_filled, 1)
                bank = claim(ROW_PLAN, ("var",))
                pe.wait_ge(row_sum, 2)
                mm(bank[:, 0:1], param("mean"), row_q[:, 1:2], start=True, stop=True).then_inc(ring_filled, 1)
                layer1()
                end_round(pe, b + 2)

        @block.scalar
        def _(act):
            def f(out_, in_, func, **kw):
                return nc.scalar.activation(out_, in_, func, **kw)

            def deviation(n):
                act.wait_ge(ln_var, n)
                f(ln_std[:, :], ln_std[:, :], ACT.Sqrt).then_inc(ln_sqrt, 1)

            def keep_xT(plan, prefix):
                for unit in LN_UNITS:
                    _, c, k = unit
                    bank = full(act, plan, prefix + unit)
                    f(xT[:, k, tokens(TC * c, HALF)], bank, ACT.Copy).then_inc(drained_a, 1)

            def hidden(plan, tag, c, n_hidden, func, bias, dst, base):
                for m in range(n_hidden):
                    bank = full(act, plan, (tag, c, m))
                    if base + m >= 3:
                        act.wait_ge(h_read, base + m - 2)
                    kw = {"bias": bias[:, m:m + 1]} if bias is not None else {}
                    f(dst[:, (base + m) % 3, :], bank, func, **kw).then_inc(drained_a, 1)

            act.wait_ge(params_in, 16)
            f(ident_b[:, :], ident, ACT.Copy).then_inc(setup_a, 1)
            f(mask_b[:, 0, :], param("mask"), ACT.Copy).then_inc(setup_a, 1)
            f(mask_b[:, 1, :], param("maskt"), ACT.Copy).then_inc(setup_a, 1)
            f(pick_r[:, :], param("pick")[0:4 * NS, :], ACT.Copy).then_inc(setup_a, 1)
            f(neg_a[:, :], param("alog"), ACT.Exp).then_inc(setup_a, 1)
            act.wait_ge(setup_a, 5)
            f(neg_a[:, :], neg_a[:, :], ACT.Copy, scale=-1.0).then_inc(setup_a, 1)
            deviation(1)
            keep_xT(MOE_PLAN, ())
            for c in range(NC):
                hidden(MOE_PLAN, "h", c, ME, ACT.Gelu_apprx_tanh, None, moe_h, ME * c)
            act.wait_ge(setup_a, 6)
            end_round(act, 1)

            def layer0(c):
                plan = ROW_PLAN
                if c:
                    act.wait_ge(conv_done, 3 * MI)
                    f(raw[:, :, 0:NCONV - 1], raw[:, :, HALF:HALF + NCONV - 1], ACT.Copy).then_inc(pad_zero, 1)
                act.wait_ge(pad_zero, c + 1)
                taps = param("convw").rearrange("p (m k) -> p m k", m=MI)
                for m in range(MI):
                    bank = full(act, plan, ("xm", c, m))
                    f(raw[:, m, NCONV - 1:], bank, ACT.Copy).then_inc(tap_done, 1)
                    f(xm[:, m, :], bank, ACT.Identity, scale=taps[:, m, NCONV - 1:NCONV],
                      bias=param("convb")[:, m:m + 1]).then_inc(drained_a, 1)
                for t in range(TC):
                    bank = full(act, plan, ("res", c, t))
                    if t == 0 and c:
                        drained(act, plan, ("yt", c - 1, MI - 1), "a")
                    f(gate[:, t, :], bank, ACT.Silu).then_inc(drained_a, 1)
                for m in range(MI):
                    act.wait_ge(conv_done, 3 * MI * c + 2 * MI + m + 1)
                    f(xm[:, m, :], xm[:, m, :], ACT.Silu).then_inc(silu_done, 1)
                bank = full(act, plan, ("xd", c))
                f(bc_parts[0:2 * NS, :], bank[DTR:DTR + 2 * NS, :], ACT.Copy).then_inc(bc_hi, 1)
                for m in range(MI):
                    act.wait_ge(dl_clamped, MI * c + m + 1)
                    link("a", f(du[:, m, :], du[:, m, :], ACT.Exp))
                for m in range(MI):
                    f(du[:, m, :], du[:, m, :], ACT.Ln, bias=1.0).then_inc(dl_log, 1)

                def b_wide_copy(n):
                    j = c * NS + n
                    bank = full(act, plan, ("B", c, n))
                    if j >= 3:
                        act.wait_ge(driven, j - 2)
                    f(b_wide[:, j % 3, :], bank, ACT.Copy).then_inc(drained_a, 1)

                b_wide_copy(0)
                drained(act, plan, ("dl", c, MI - 1), "v")
                for n in range(NS):
                    j = c * NS + n
                    if j >= 2:
                        act.wait_ge(scanned, MI * (j - 1))
                    for d in range(MI):
                        f(decay[:, j % 2, d, :], delta[:, d, :], ACT.Exp,
                          scale=neg_a[:, d * NS + n:d * NS + n + 1]).then_inc(decay_done, 1)
                    if n + 1 < NS:
                        b_wide_copy(n + 1)
                for d in range(MI):
                    bank = full(act, plan, ("yt", c, d))
                    f(yT[:, d, :], bank, ACT.Copy).then_inc(drained_a, 1)
                for k in range(KD):
                    bank = full(act, plan, ("m", c, k))
                    f(mT[:, k, :], bank, ACT.Copy).then_inc(drained_a, 1)
                hidden(plan, "h", c, MF, ACT.Gelu, param("fb1"), h0, MF * c)

            def attention():
                plan = ROW_PLAN
                u = 0
                for e in EVENTS:
                    if e[0] == "mt":
                        g = e[1]
                        both = full(act, plan, e)
                        if g:
                            act.wait_ge(neg_in[g - 1], 32)
                        f(neg_hi, both[0:2, :], ACT.Copy, scale=-1.0).then_inc(drained_a, 1)
                    elif e[0] == "st":
                        h, jt = e[1], e[2]
                        both = full(act, plan, e)
                        if u == 0:
                            for slot in range(SLOTS):
                                act.wait_ge(q_in[slot], 96)
                                act.wait_ge(k_in[slot], 96)
                        if u >= PT_RING:
                            act.wait_ge(pt_read, u - PT_RING + 1)
                        width = (NT - jt) * P
                        f(exps[:, u % PT_RING, 0:width], both[:, 0:width], ACT.Exp,
                          scale=float(DH) ** -0.5).then_inc(drained_a, 1)
                        drained(act, plan, e, "a")
                        f(exps_hi[:, u % PT_RING, 0:width], exps[:, u % PT_RING, 0:width], ACT.Copy)\
                            .then_inc(exps_hi_done, 1)
                        u += 1

            def layer1():
                plan = ROW_PLAN
                deviation(3)
                keep_xT(plan, ("1",))
                for t in range(NT):
                    bank = full(act, plan, ("pa", t))
                    f(pt1[:, t, 64:128], bank[:, D:D + 64], ACT.Copy).then_inc(tap_done, 1)
                    f(pt2[:, t, :], bank[:, D + 64:D + 192], ACT.Copy).then_inc(drained_a, 1)
                    bank = full(act, plan, ("pb", t))
                    f(pt1[:, t, 0:64], bank[:, D:D + 64], ACT.Copy).then_inc(drained_a, 1)
                act.wait_ge(lines_sq, 1)
                f(norm[:, :], norm[:, :], ACT.Sqrt).then_inc(lines_sqrt, 1)
                for c in range(NC):
                    bank = full(act, plan, ("lt", c))
                    f(linesT[:, c * HALF:(c + 1) * HALF], bank[0:6 * H, :], ACT.Copy).then_inc(drained_a, 1)
                for c in range(NC):
                    bank = full(act, plan, ("jw", c))
                    f(jlines[:, TC * c:TC * (c + 1), :, :].rearrange("p t h j -> p (t h j)"), bank[:, 0:TC * 6 * H],
                      ACT.Copy).then_inc(drained_a, 1)

                def keep_hi(g):
                    for i, hi in enumerate((parts[g][0], parts[g][2])):
                        for c in range(NC):
                            bank = full(act, plan, ("qk", g, i, c))
                            f(hi[:, c * HALF:(c + 1) * HALF], bank, ACT.Identity,
                              bias=param("qkb")[:, 2 * i + g:2 * i + g + 1]).then_inc(drained_a, 1)

                keep_hi(0)
                drained(act, plan, ("ms",), "v")
                f(mem_in[:, :, :], mem_in[:, :, :], ACT.Sigmoid).then_inc(sig_done, 1)
                f(gate_in[:, :, :], gate_in[:, :, :], ACT.Sigmoid).then_inc(sig_done, 1)
                act.wait_ge(gates_read, 1)
                keep_hi(1)
                attention()
                for c in range(NC):
                    for k in range(KD):
                        bank = full(act, plan, ("zt", k, c))
                        f(zT[:, k, c * HALF:(c + 1) * HALF], bank, ACT.Copy).then_inc(drained_a, 1)
                for c in range(NC):
                    hidden(plan, "g", c, MF, ACT.Gelu, param("gb1"), h1, MF * (NC + c))

            with act.Fori(0, B) as b:
                deviation(1)
                keep_xT(ROW_PLAN, ())
                for c in range(NC):
                    layer0(c)
                act.wait_ge(ln_var, 2)
                f(row_q[:, 2:3], row_q[:, 2:3], ACT.Sqrt).then_inc(ln_sqrt, 1)
                layer1()
                end_round(act, b + 2)

        @block.vector
        def _(dve):
            V = nc.vector

            def normalise(x, xn, n):
                for t in range(NT):
                    last = V.bn_stats(ln_stats[:, t, :], x[:, t, :])
                link("v", last)
                for t in range(NT):
                    last = V.bn_aggr(ln_mv[:, t, :], ln_stats[:, t, :])
                link("v", last)
                V.tensor_scalar(ln_std[:, :], ln_mv[:, :, 1], EPS, None, ALU.add).then_inc(ln_var, 1)
                dve.wait_ge(ln_sqrt, n)
                link("v", V.reciprocal(ln_rstd[:, :], ln_std[:, :]))
                for t in range(NT):
                    V.tensor_scalar(xn[:, t, :], x[:, t, :], ln_mv[:, t, 0:1], ln_rstd[:, t:t + 1], ALU.subtract,
                                    ALU.mult).then_inc(xn_done, 1)

            V.memset(xT[:, :, 0:1], 0.0).then_inc(setup_v, 1)
            dve.wait_ge(params_in, 16)
            V.tensor_tensor(out_bias[:, :], param("outb"), param("gb2"), ALU.add).then_inc(setup_v, 1)
            ew = param("ew").rearrange("p (t k) -> p t k", k=2)
            V.tensor_tensor(ew_sum[:, :], ew[:, :, 0], ew[:, :, 1], ALU.add).then_inc(setup_v, 1)
            dve.wait_ge(setup_v, 3)
            dve.wait_ge(x_loaded, 16)
            normalise(x_row, moe_xn, 1)
            for c in range(NC):
                dve.wait_ge(h_read, ME * (c + 1))
                for tt in range(TC):
                    t = TC * c + tt
                    ins = V.scalar_tensor_tensor(x_row[:, t, :], acc_tile(tt), ew_sum[:, t:t + 1], x_row[:, t, :],
                                                 ALU.mult, ALU.add)
                    if tt % 2:
                        ins.then_inc(acc_read, 1)
            dve.wait_ge(acc_read, 2 * NC)
            end_round(dve, 1)

            def layer0(c):
                plan = ROW_PLAN
                taps = param("convw").rearrange("p (m k) -> p m k", m=MI)
                for k in range(NCONV - 1):
                    for m in range(MI):
                        step = 3 * MI * c + MI * k + m
                        if k == 0:
                            drained(dve, plan, ("xm", c, m), "a")
                        else:
                            dve.wait_ge(conv_done, step + 1 - MI)
                        V.scalar_tensor_tensor(xm[:, m, :], raw[:, m, k:k + HALF], taps[:, m, k:k + 1], xm[:, m, :],
                                               ALU.mult, ALU.add).then_inc(conv_done, 1)
                bank = full(dve, plan, ("xd", c))
                dve.wait_ge(bc_hi, c + 1)
                V.tensor_copy(dt_low[:, :], bank[0:DTR, :]).then_inc(dt_done, 1)
                V.tensor_tensor(bc_parts[2 * NS:4 * NS, :], bank[DTR:DTR + 2 * NS, :],
                                bc_parts[0:2 * NS, :].bitcast(F32), ALU.subtract).then_inc(drained_v, 1)
                bias = param("dtb")
                for m in range(MI):
                    bank = full(dve, plan, ("dl", c, m))
                    V.tensor_scalar(du[:, m, :], bank, bias[:, m:m + 1], CAP, ALU.add, ALU.min)\
                        .then_inc(dl_clamped, 1)
                for m in range(MI):
                    bank = full(dve, plan, ("dl", c, m))
                    dve.wait_ge(dl_log, MI * c + m + 1)
                    V.scalar_tensor_tensor(delta[:, m, :], bank, bias[:, m:m + 1], du[:, m, :], ALU.add, ALU.max)\
                        .then_inc(drained_v, 1)
                for m in range(MI):
                    drained(dve, plan, ("dl", c, m), "v")
                    V.tensor_tensor(du[:, m, :], delta[:, m, :], xm[:, m, :], ALU.mult).then_inc(du_done, 1)
                for n in range(NS):
                    j = c * NS + n
                    slot = (c * (NS + 1) + n + 1) % 3
                    dve.wait_ge(driven, j + 1)
                    for d in range(MI):
                        dve.wait_ge(decay_done, MI * j + d + 1)
                        V.tensor_tensor_scan(state[:, slot, d, :], decay[:, j % 2, d, :], state[:, slot, d, :],
                                             carry[:, n, d:d + 1] if c else 0.0, ALU.mult, ALU.add)\
                            .then_inc(scanned, 1)
                    dve.wait_ge(scanned, MI * (j + 1))
                    if c == 0:
                        link("v", V.tensor_copy(carry[:, n, :], state[:, slot, :, HALF - 1]))
                    bank = full(dve, plan, ("C", c, n))
                    V.tensor_tensor(state[:, slot, :, :], state[:, slot, :, :], wide(bank, MI), ALU.mult)\
                        .then_inc(weighed, 1)
                    dve.wait_ge(weighed, j + 1)
                    dve.sem_inc(drained_v, 1)
                dve.wait_ge(state_read, (c + 1) * (NS + 1))
                for t in range(TC):
                    V.tensor_tensor(gate[:, t, :], y_acc[:, t, :], gate[:, t, :], ALU.mult).then_inc(y_gated, 1)
                dve.wait_ge(h_read, MF * (c + 1))
                for a in range(2):
                    t = TC * c + 2 * a
                    V.tensor_tensor(mix[:, t:t + 2, :], ps[:, a, :].rearrange("p (t d) -> p t d", t=2),
                                    wide(param("fb2"), 2), ALU.add).then_inc(acc_read, 1)
                    dve.wait_ge(acc_read, 2 * c + a + 1)
                    link("v", V.bn_stats(row_stats[:, 2 * c + a, :], mix[:, t:t + 2, :].rearrange("p t d -> p (t d)")))

            def finish_layer0():
                V.bn_aggr(row_mv[:, :], row_stats[:, :, :].rearrange("p a b -> p (a b)")).then_inc(row_sum, 1)
                bank = full(dve, ROW_PLAN, ("mu",))
                dve.wait_ge(row_sum, 1)
                V.tensor_copy(row_q[:, 0:1], bank[:, 0:1]).then_inc(drained_v, 1)
                drained(dve, ROW_PLAN, ("mu",), "v")
                link("v", V.tensor_tensor(row_q[:, 4:5], row_mv[:, 0:1], row_q[:, 0:1], ALU.subtract))
                V.scalar_tensor_tensor(row_q[:, 1:2], row_q[:, 4:5], row_q[:, 4:5], row_mv[:, 1:2], ALU.mult,
                                       ALU.add).then_inc(row_sum, 1)
                bank = full(dve, ROW_PLAN, ("var",))
                V.tensor_scalar(row_q[:, 2:3], bank[:, 0:1], EPS, None, ALU.add).then_inc(drained_v, 1)
                drained(dve, ROW_PLAN, ("var",), "v")
                dve.sem_inc(ln_var, 1)
                dve.wait_ge(ln_sqrt, 2)
                link("v", V.reciprocal(row_q[:, 3:4], row_q[:, 2:3]))
                for t in range(NT):
                    last = V.tensor_scalar(mix[:, t, :], mix[:, t, :], row_q[:, 0:1], row_q[:, 3:4], ALU.subtract,
                                           ALU.mult)
                link("v", last)
                dve.wait_ge(resid_in, 16)
                link("v", V.tensor_tensor(x_row[:, :, :], x_row[:, :, :], mix[:, :, :], ALU.add))

            def line_coordinates(t):
                dve.wait_ge(outer_done, t + 1)
                o = outer[:, t % 2]
                at = 0
                for i in range(3):
                    last = V.tensor_tensor(lines[:, t, :, at:at + 3 - i], o[:, :, i, i + 1:4], o[:, :, i + 1:4, i],
                                           ALU.subtract)
                    at += 3 - i
                last.then_inc(lines_read, 1)

            def keep_lo(g):
                for i, (hi, lo) in enumerate((parts[g][0:2], parts[g][2:4])):
                    for c in range(NC):
                        bank = full(dve, ROW_PLAN, ("qk", g, i, c))
                        drained(dve, ROW_PLAN, ("qk", g, i, c), "a")
                        half = slice(c * HALF, (c + 1) * HALF)
                        V.scalar_tensor_tensor(lo[:, half], bank, param("qkb")[:, 2 * i + g:2 * i + g + 1],
                                               hi[:, half].bitcast(F32), ALU.add, ALU.subtract)\
                            .then_inc(drained_v, 1)

            def memory():
                plan = ROW_PLAN
                V.memset(gsum[:, :, 0:1], 0.0)
                for t in range(NT):
                    bank = full(dve, plan, ("pa", t))
                    drained(dve, plan, ("pa", t), "a")
                    V.tensor_tensor(v_sum[:, t, :], bank[:, 0:D], param("vb"), ALU.add).then_inc(v_summed, 1)
                    V.tensor_tensor(gate_in[:, t, :], bank[:, 448:464], param("mgb"), ALU.add)\
                        .then_inc(drained_v, 1)
                    bank = full(dve, plan, ("pb", t))
                    drained(dve, plan, ("pb", t), "a")
                    V.tensor_tensor(z[:, t, :], bank[:, 0:D], param("mvb"), ALU.add).then_inc(drained_v, 1)
                    if t >= 1:
                        line_coordinates(t - 1)
                line_coordinates(NT - 1)
                dve.wait_ge(lines_read, NT)
                square = feat_w[:, :, 0:2 * H * 6].rearrange("p t (h j) -> p t h j", j=6)
                flat = "p t h j -> p (t h) j"
                link("v", V.tensor_tensor(square, lines[:, :, :, :], lines[:, :, :, :], ALU.mult))
                V.tensor_reduce(norm[:, :].rearrange("p (t h) -> p t h", t=NT), square, AX_X, ALU.add)\
                    .then_inc(lines_sq, 1)
                dve.wait_ge(lines_sqrt, 1)
                link("v", V.tensor_scalar(norm[:, :], norm[:, :], 1e-12, None, ALU.max))
                link("v", V.reciprocal(norm[:, :], norm[:, :]))
                V.tensor_tensor(lines[:, :, :, :].rearrange(flat), lines[:, :, :, :].rearrange(flat),
                                norm[:, :].unsqueeze(2).broadcast_to([P, NT * 2 * H, 6]), ALU.mult)\
                    .then_inc(lines_done, 1)
                drained(dve, plan, ("jw", NC - 1), "a")
                products(V, feat_w, jlines[:, :, :, :]).then_inc(feat_w_done, 1)
                dve.wait_ge(feat_w_done, 1)
                rate = param("decay")[0:FR, :]
                for ch in range(FCH):
                    for c in range(NC):
                        bank = full(dve, plan, ("fw", ch, c))
                        g = gsum[:, ch % 2]
                        V.tensor_tensor_scan(g[:, 1 + c * HALF:1 + (c + 1) * HALF],
                                             rate.broadcast_to([FR, HALF]), bank[0:FR, :],
                                             g[:, HALF:HALF + 1] if c else 0.0, ALU.mult, ALU.add)\
                            .then_inc(drained_v, 1)
                        drained(dve, plan, ("fw", ch, c), "v")
                        bank = full(dve, plan, ("fr", ch, c))
                        V.scalar_tensor_tensor(prod[0:FR, ch, c * HALF:(c + 1) * HALF], g[:, c * HALF:(c + 1) * HALF],
                                               rate, bank[0:FR, :], ALU.mult, ALU.mult).then_inc(drained_v, 1)
                keep_lo(0)
                bank = full(dve, plan, ("ms",))
                V.tensor_tensor(mem_in[:, :, :], bank[:, 0:NT * H].rearrange("p (t h) -> p t h", t=NT),
                                wide(param("mscale"), NT), ALU.mult).then_inc(drained_v, 1)
                dve.wait_ge(sig_done, 2)
                link("v", V.tensor_tensor(mem_in[:, :, :], mem_in[:, :, :], gate_in[:, :, :], ALU.mult))
                link("v", V.tensor_reduce(gate8[:, :], mem_in[:, :, :], AX_X, ALU.add))
                link("v", V.tensor_scalar(gate8[:, :], gate8[:, :], 1.0 / H, None, ALU.mult))
                for t in range(NT):
                    last = V.tensor_scalar(z[:, t, :], z[:, t, :], gate8[:, t:t + 1], None, ALU.mult)
                last.then_inc(gates_read, 1)
                dve.wait_ge(gates_read, 1)

            def attention():
                plan = ROW_PLAN
                u = 0
                for e in EVENTS:
                    kind = e[0]
                    if kind == "sm":
                        h, it = e[1], e[2]
                        both = full(dve, plan, e)
                        V.tensor_reduce(smax[:, it, h:h + 1], both[:, 0:(it + 1) * P], AX_X, ALU.max)\
                            .then_inc(drained_v, 1)
                    elif kind == "mt":
                        drained(dve, plan, e, "a")
                        V.scalar_tensor_tensor(neg_lo, full(dve, plan, e)[0:2, :], -1.0,
                                               neg_hi.bitcast(F32), ALU.mult, ALU.subtract)\
                            .then_inc(drained_v, 1)
                    elif kind == "pv":
                        h, jt = e[1], e[2]
                        if jt not in LO_POOL:
                            dve.wait_ge(exps_hi_done, u + 1)
                            at = (slice(None), u % PT_RING, slice(0, (NT - jt) * P))
                            V.tensor_tensor(exps_lo[at], exps[at],
                                            exps_hi[at].bitcast(F32), ALU.subtract)\
                                .then_inc(exps_lo_v, 1)
                        u += 1
                        if jt in (TC - 1, NT - 1):
                            half = slice(0, HALF) if jt < TC else slice(HALF, S)
                            dve.wait_ge(pt_read, u)
                            if h >= 2 and h % 2 == 0 and jt < TC:
                                full(dve, plan, ("ot", h // 2 - 1))
                            V.tensor_copy(oT[VW * (h % 2):VW * (h % 2 + 1), half], pv_acc[:, half])\
                                .then_inc(oT_done, 1)
                    elif kind == "ot":
                        g = e[1]
                        bank = full(dve, plan, e)[:, 0:NT * VC].rearrange("p (t h d) -> p t h d", t=NT, h=2)
                        link("v", V.reciprocal(rden[:, :, :], bank[:, :, :, DH]))
                        V.tensor_tensor(seq[:, :, :, :], bank[:, :, :, 0:DH],
                                        rden[:, :, :].unsqueeze(3).broadcast_to([P, NT, 2, DH]), ALU.mult)\
                            .then_inc(drained_v, 1)
                        drained(dve, plan, e, "v")
                        part = z[:, :, g * 2 * DH:(g + 1) * 2 * DH]
                        last = V.tensor_tensor(part, part, seq[:, :, :, :].rearrange("p t h d -> p t (h d)"), ALU.add)
                last.then_inc(z_done, 1)

            def layer1():
                plan = ROW_PLAN
                normalise(x_row, xn1, 3)
                memory()
                keep_lo(1)
                attention()
                scale = param("scale")
                w1, w2 = weight("g1", KD), weight("g2", MF)
                for k in range(KD):
                    for c in range(NC):
                        bank = full(dve, plan, ("e1", k, c))
                        half = slice(c * HALF, (c + 1) * HALF)
                        V.scalar_tensor_tensor(g1[:, k, half], bank, scale, w1[:, k, half], ALU.mult, ALU.add)\
                            .then_inc(drained_v, 1)
                for q in range(MF // 2):
                    bank = full(dve, plan, ("e2", q))
                    V.scalar_tensor_tensor(g2[:, 2 * q:2 * q + 2, :], bank.rearrange("p (k n) -> p k n", k=2), scale,
                                           w2[:, 2 * q:2 * q + 2, :], ALU.mult, ALU.add).then_inc(drained_v, 1)
                link("v", V.tensor_tensor(x_row[:, :, :], x_row[:, :, :], wide(out_bias[:, :], NT), ALU.add))
                for c in range(NC):
                    dve.wait_ge(h_read, MF * (NC + c + 1))
                    for a in range(2):
                        i = 2 * c + a
                        V.tensor_tensor(done[:, i, :, :], ps[:, a, :].rearrange("p (t d) -> p t d", t=2),
                                        x_row[:, 2 * i:2 * i + 2, :], ALU.add).then_inc(out_sum, 1)
                        dve.wait_ge(out_sum, i + 1)
                        dve.sem_inc(acc_read, 1)

            with dve.Fori(0, B) as b:
                V.memset(raw[:, :, 0:NCONV - 1], 0.0).then_inc(pad_zero, 1)
                dve.wait_ge(x_loaded, 16)
                normalise(mix, mix, 1)
                for c in range(NC):
                    layer0(c)
                finish_layer0()
                layer1()
                end_round(dve, b + 2)

        @block.gpsimd
        def _(pool):
            G = nc.gpsimd
            end_round(pool, 1)

            def layer0(c):
                plan = ROW_PLAN
                w = c * (NS + 1)
                pool.wait_ge(silu_done, MI * (c + 1))
                if c:
                    pool.wait_ge(state_read, w - 2)
                for d in range(MI):
                    last = G.tensor_scalar(state[:, w % 3, d, :], xm[:, d, :], param("dskip")[:, d:d + 1], None,
                                           ALU.mult)
                last.then_inc(skip_done, 1)
                pool.wait_ge(du_done, MI * (c + 1))
                for n in range(NS):
                    j, w = c * NS + n, c * (NS + 1) + n + 1
                    drained(pool, plan, ("B", c, n), "a")
                    if w >= 3:
                        pool.wait_ge(state_read, w - 2)
                    G.tensor_tensor(state[:, w % 3, :, :], du[:, :, :], wide(b_wide[:, j % 3, :], MI), ALU.mult)\
                        .then_inc(driven, 1)

            def layer1():
                plan = ROW_PLAN
                pool.wait_ge(xn_done, NT + 1)
                link("p", G.memset(k_odd[0:64, :, :].bitcast(F32), 0.0))
                G.memset(k_odd[64:128, :, :].bitcast(F32), 1.0).then_inc(k_odd_clear, 1)
                pool.wait_ge(k_odd_clear, 1)
                G.memset(odd_hi, 0.0)
                G.memset(even, 0.0).then_inc(l1_clear, 1)
                G.memset(vals_by_head[:, :, :, 0, DH].bitcast(F32), 1.0)
                G.memset(vals_by_head[:, :, :, 1, DH].bitcast(F32), 0.0)
                G.memset(vals_pad.bitcast(F32), 0.0)
                for t in range(NT):
                    drained(pool, plan, ("pb", t), "a")
                    if t >= 2:
                        pool.wait_ge(lines_read, t - 1)
                    a = pt1[:, t, :].rearrange("p (l i) -> p l i", i=4)
                    b = pt2[:, t, :].rearrange("p (l i) -> p l i", i=4)
                    G.tensor_tensor(outer[:, t % 2], a.unsqueeze(3).broadcast_to([P, 2 * H, 4, 4]),
                                    b.unsqueeze(2).broadcast_to([P, 2 * H, 4, 4]), ALU.mult)\
                        .then_inc(outer_done, 1)
                by_head = v_sum.rearrange("p t (h d) -> p t h d", h=H)
                pool.wait_ge(v_summed, NT)
                G.tensor_copy(vals_by_head[:, :, :, 0, 0:DH], by_head).then_inc(vals_hi, 1)
                pool.wait_ge(vals_hi, 1)
                G.tensor_tensor(vals_by_head[:, :, :, 1, 0:DH], by_head,
                                vals_by_head[:, :, :, 0, 0:DH].bitcast(F32), ALU.subtract).then_inc(vals_done, 1)
                pool.wait_ge(vals_done, 1)
                pool.wait_ge(lines_done, 1)
                products(G, feat_r, lines[:, :, H:2 * H, :]).then_inc(feat_r_done, 1)
                pool.wait_ge(feat_r_done, 1)
                pool.wait_ge(feat_w_done, 1)
                pool.wait_ge(rows_in, 160)
                link("p", G.memset(qs[:, :, :].bitcast(F32), 0.0))
                link("p", G.memset(k_even[64:128, :, :].bitcast(F32), 0.0))
                G.memset(k_even[32:64, :, :].bitcast(F32), 1.0).then_inc(stacks_clear, 1)
                pool.wait_ge(stacks_clear, 1)
                for u, (_, _, jt) in enumerate(EXPS):
                    if jt in LO_POOL:
                        pool.wait_ge(exps_hi_done, u + 1)
                        at = (slice(None), u % PT_RING, slice(0, (NT - jt) * P))
                        G.tensor_tensor(exps_lo[at], exps[at],
                                        exps_hi[at].bitcast(F32), ALU.subtract)\
                            .then_inc(exps_lo_p, 1)

            with pool.Fori(0, B) as b:
                for c in range(NC):
                    layer0(c)
                layer1()
                end_round(pool, b + 2)


def _slices(w):
    k = w.shape[0] // P
    return w.reshape(k, P, -1).transpose(1, 0, 2).reshape(P, -1)


def _cols(v):
    return v.reshape(-1, P).T


def kernel(**inputs):
    import numpy as np
    import concourse.bacc as bacc
    from concourse.bass_utils import run_bass_kernel_spmd

    a = {k: np.asarray(v) for k, v in inputs.items()}
    f32 = np.float32

    def everywhere(v):
        return np.broadcast_to(v.reshape(1, -1), (P, v.size))

    def padded(m):
        out = np.zeros((P, m.shape[1]), f32)
        out[:m.shape[0]] = m
        return out

    qkv, in_w = a["L1_attn_qkv_w"], a["L0_attn_in_proj_w"]
    w = {
        "in": _slices(in_w.T), "xproj": _slices(a["L0_attn_x_proj_w"].T), "dt": padded(a["L0_attn_dt_proj_w"].T),
        "oproj": _slices(a["L0_attn_out_proj_w"].T), "f1": _slices(a["L0_attn_ffn_w1"].T),
        "f2": _slices(a["L0_attn_ffn_w2"].T), "qk": _slices(qkv[:, 0:2 * D]),
        "ta": _slices(np.concatenate([qkv[:, 2 * D:], a["L1_attn_w1_read"], a["L1_attn_w2_write"],
                                      a["L1_attn_w2_read"], a["L1_attn_memg_w"]], 1)),
        "tb": _slices(np.concatenate([a["L1_attn_memv_w"], a["L1_attn_w1_write"]], 1)),
        "out": _slices(a["L1_attn_out_w"]), "g1": _slices(a["L1_ffn_W1"].T), "g2": _slices(a["L1_ffn_W2"].T),
    }
    jdiag = np.zeros((P, 6 * H), f32)
    for h in range(H):
        jdiag[6 * h:6 * h + 6, 6 * h:6 * h + 6] = a["L1_attn_J"]
    sumpq = np.zeros((P, FCH, H), f32)
    pairs = [(i, j) for i in range(6) for j in range(i, 6)]
    for n, (i, j) in enumerate(pairs):
        for h in range(H):
            sumpq[(n % 7) * H + h, n // 7, h] = 1.0 if i == j else 2.0
    pick = np.zeros((P, 2 * NS), f32)
    for n in range(2 * NS):
        pick[n, n] = pick[2 * NS + n, n] = 1.0
    sel = np.zeros((P, VC), f32)
    for h in range(2):
        for i in range(2):
            for d in range(DH + 1):
                sel[VW * h + i * (DH + 1) + d, h * (DH + 1) + d] = 1.0
    above = np.triu(np.full((P, P), -1e30, f32), 1)
    rate = np.zeros((P, 1), f32)
    for n in range(7):
        rate[n * H:(n + 1) * H, 0] = a["L1_attn_decays"]
    qkv_b = a["L1_attn_qkv_b"]
    p = {
        "convw": a["L0_attn_conv_w"].reshape(MI, P, NCONV).transpose(1, 0, 2).reshape(P, -1),
        "convb": _cols(a["L0_attn_conv_b"]), "dtb": _cols(a["L0_attn_dt_proj_b"]), "alog": _slices(a["L0_attn_A_log"]),
        "dskip": _cols(a["L0_attn_D"]), "fb1": _cols(a["L0_attn_ffn_b1"]), "qkb": _cols(qkv_b[0:2 * D]),
        "gb1": _cols(a["L1_ffn_b1"]), "scale": everywhere(a["L1_ffn_scale"]), "decay": rate,
        "fb2": everywhere(a["L0_attn_ffn_b2"]), "vb": everywhere(qkv_b[2 * D:]),
        "mvb": everywhere(a["L1_attn_memv_b"]), "mgb": everywhere(a["L1_attn_memg_b"]),
        "mscale": everywhere(a["L1_attn_mem_scale"]), "outb": everywhere(a["L1_attn_out_b"]),
        "gb2": everywhere(a["L1_ffn_b2"]), "jdiag": jdiag, "ident": np.eye(P, dtype=f32), "mask": above,
        "sel": sel, "maskt": above.T, "sumpq": sumpq.reshape(P, -1), "pick": pick, "mean": np.full((P, P), 1.0 / P, f32),
        "ew": a["L0_ffn_expert_weights"].reshape(NT, P, 2).transpose(1, 0, 2).reshape(P, -1),
    }
    arrays = {
        "x": a["L0_attn_seq_embeddings"],
        "weights": np.concatenate([w[n] for n, _ in WEIGHTS], 1),
        "params": np.concatenate([p[n] for n, _ in PARAMS], 1),
        "expert1": a["L0_ffn_w1"].reshape(KD, P, ME * P).transpose(1, 0, 2),
        "expert2": a["L0_ffn_w2"].reshape(ME, P, D).transpose(1, 0, 2),
    }
    arrays = {f"in_{k}": np.ascontiguousarray(v) for k, v in arrays.items()}
    nc = bacc.Bacc("TRN2", target_bir_lowering=False, num_devices=1)
    args = [nc.dram_tensor(k, v.shape, mybir.dt.from_np(v.dtype), kind="ExternalInput").ap()
            for k, v in arrays.items()]
    resid = nc.dram_tensor("resid", (B, S, D), F32, kind="Internal").ap()
    out = nc.dram_tensor("out", (B, S, D), F32, kind="ExternalOutput").ap()
    build(nc, *args, resid, out)
    return run_bass_kernel_spmd(nc, [arrays], core_ids=[0]).results[0]["out"]
```

```python
from contextlib import ExitStack

import concourse.bass as bass
from concourse import mybir

F32 = mybir.dt.float32
F32R = mybir.dt.float32r
BF16 = mybir.dt.bfloat16
ALU = mybir.AluOpType
ACT = mybir.ActivationFunctionType
AX_X = mybir.AxisListType.X

P = 128
B, S, D = 8, 1024, 256
NT = S // P
KD = D // P
HALF = 512
NC = S // HALF
TC = HALF // P
DI, NS, DTR, NCONV = 512, 16, 64, 4
MI = DI // P
FF = 1024
MF = FF // P
ME = 2048 // P
H, DH, NG = 16, 16, 8
VC = 2 * (DH + 1)
VW = 64
SLOTS = 4
NPQ = 21
FCH = 3
FR = 7 * H
EPS = 1e-5
CAP = 30.0
LN_UNITS = [("xt", c, k) for c in range(NC) for k in range(KD)]

WEIGHTS = [("in", KD * 2 * DI), ("xproj", MI * (DTR + 2 * NS)), ("dt", DI), ("oproj", MI * D), ("qk", KD * 2 * D), ("ta", KD * 464), ("tb", KD * 320), ("out", KD * D),
           ("g1", KD * FF), ("g2", MF * D), ("f1", KD * FF), ("f2", MF * D)]
PARAMS = [("convw", MI * NCONV), ("convb", MI), ("dtb", MI), ("alog", MI * NS), ("dskip", MI), ("fb1", MF),
          ("qkb", 4), ("gb1", MF), ("scale", 1), ("decay", 1), ("fb2", D), ("vb", D), ("mvb", D), ("mgb", H),
          ("mscale", H), ("outb", D), ("gb2", D), ("jdiag", 6 * H), ("ident", P), ("mask", P), ("maskt", P),
          ("sumpq", FCH * H), ("sel", VC), ("pick", 2 * NS), ("mean", P), ("ew", 2 * NT)]


def columns(layout):
    at, out = 0, {}
    for name, n in layout:
        out[name] = (at, at + n)
        at += n
    return out, at


W_AT, W_ALL_COLS = columns(WEIGHTS)
W_COLS = W_AT["f1"][0]
P_AT, P_COLS = columns(PARAMS)


def ring_plan(units):
    plan, owner, count = {}, {}, {"a": 0, "v": 0}
    for n, (name, banks, drainers) in enumerate(units):
        need = {"a": 0, "v": 0}
        for bank in banks:
            for who, k in owner.get(bank, {}).items():
                need[who] = max(need[who], k)
        for who in drainers:
            count[who] += 1
        for bank in banks:
            owner[bank] = {who: count[who] for who in drainers}
        assert name not in plan
        plan[name] = (banks, n + 1, need, dict(owner[banks[0]]))
    return plan


def narrow(names, start=0):
    return [(name, [4 + (start + i) % 4], who) for i, (name, who) in enumerate(names)]


def moe_names():
    out = [(u, "a") for u in LN_UNITS]
    for c in range(NC):
        out += [(("h", c, m), "a") for m in range(ME)]
    return out


def fill(c, n):
    if c == 0:
        return None
    if n < MF:
        return ("h", c - 1, n)
    if OUT_FROM <= n < OUT_FROM + TC:
        return ("o", c - 1, n - OUT_FROM)
    return None


OUT_FROM = MF + 2


def layer0_units():
    out = narrow([(u, "a") for u in LN_UNITS])

    def b_unit(c, n):
        return (("B", c, n), [4], "a")

    def c_unit(c, n):
        return (("C", c, n), [5 + n % 2], "v")

    for c in range(NC):
        names = [(("xm", c, m), "a") for m in range(MI)]
        names += [(("res", c, t), "a") for t in range(TC)]
        names += [(("xd", c), "v")]
        names += [(("dl", c, m), "v") for m in range(MI)]
        out += narrow(names)
        out += [b_unit(c, 0), c_unit(c, 0), b_unit(c, 1), c_unit(c, 1)]
        for n in range(NS):
            if n + 2 < NS:
                out += [b_unit(c, n + 2)]
            if fill(c, n):
                out += [(fill(c, n), [7], "a" if n < MF else "v")]
            if n + 2 < NS:
                out += [c_unit(c, n + 2)]
        names = [(("yt", c, m), "a") for m in range(MI)]
        names += [(("m", c, k), "a") for k in range(KD)]
        if c == NC - 1:
            names += [(("h", c, m), "a") for m in range(MF)]
            names += [(("o", c, t), "v") for t in range(TC)]
            names += [(("mu",), "v"), (("var",), "v")]
        out += narrow(names)
    return out


def layer1_names():
    out = [(("1",) + u, "a") for u in LN_UNITS]
    for t in range(NT):
        out += [(("pa", t), "av"), (("pb", t), "av")]
    out += [(("lt", c), "a") for c in range(NC)]
    out += [(("jw", c), "a") for c in range(NC)]
    for ch in range(FCH):
        for c in range(NC):
            out += [(("fw", ch, c), "v"), (("fr", ch, c), "v")]
    out += [(("qk", 0, i, c), "av") for i in range(2) for c in range(NC)]
    out += [(("ms",), "v")]
    return out + [(("qk", 1, i, c), "av") for i in range(2) for c in range(NC)]


TILE_ORDER = (0, 7, 1, 6, 2, 5, 3, 4)
LAST_TILE = TILE_ORDER[-1]


def attention_events():
    sm = [("sm", h, it) for h in range(H) for it in TILE_ORDER]
    st = [("st", h, jt) for h in range(H) for jt in TILE_ORDER]
    ev, turn = [], []

    def maxima(i):
        if i < len(sm):
            ev.append(sm[i])
        if 0 < i - ROWS_LAG < len(sm) and (i - ROWS_LAG + 1) % (2 * NT) == 0:
            ev.append(("mt", (i - ROWS_LAG) // (2 * NT)))

    for i in range(MAX_LEAD):
        maxima(i)
    for u in range(len(st) + PV_LAG + TURN_LAG):
        if u < len(st):
            ev.append(st[u])
        if 0 <= u - PV_LAG < len(st):
            ev.append(("pv",) + st[u - PV_LAG][1:])
            if (u - PV_LAG + 1) % (2 * NT) == 0:
                turn.append((u + TURN_LAG, (u - PV_LAG) // (2 * NT)))
        if turn and turn[0][0] == u:
            ev.append(("ot", turn.pop(0)[1]))
        maxima(MAX_LEAD + u)
        if 0 <= u - LO_LAG < len(st):
            ev.append(("lo",) + st[u - LO_LAG][1:])
    return ev


def exps_plan():
    plan, at = [], 0
    for u, (_, _, jt) in enumerate(EXPS):
        width = (NT - jt) * P
        if at + width > RING_COLS:
            at = 0
        need = max([n + 1 for n, (a, w, _) in enumerate(plan) if a < at + width and at < a + w], default=0)
        plan.append((at, width, need))
        at += width
    return plan


MAX_LEAD = 24
ROWS_LAG = 3
LO_LAG = 1
PV_LAG = 3
TURN_LAG = 2
EVENTS = attention_events()
EXPS = [e for e in EVENTS if e[0] == "st"]
RING_COLS = 3 * S
EXPS_AT = exps_plan()
LO_POOL = (4, 5, 6, 7)
WIDE = [[4, 5], [6, 7], [0, 1]]


def wide_units():
    who = {"sm": "v", "st": "a", "mt": "av", "ot": "v"}
    units = [e for e in EVENTS if e[0] in who]
    return [(e, WIDE[i % 3], who[e[0]]) for i, e in enumerate(units)]


def tail_names():
    out = [(("zt", k, c), "a") for c in range(NC) for k in range(KD)]
    out += [(("e1", k, c), "v") for k in range(KD) for c in range(NC)]
    out += [(("e2", q), "v") for q in range(MF // 2)]
    for c in range(NC):
        out += [(("g", c, m), "a") for m in range(MF)]
    return out


MOE_PLAN = ring_plan(narrow(moe_names()))
_units = layer0_units()
_units += narrow(layer1_names(), len(_units))
_units += wide_units()
_units += narrow(tail_names())
ROW_PLAN = ring_plan(_units)


def lo_count(u, who):
    return sum(1 for e in EXPS[:u] if (e[2] in LO_POOL) == (who == "p"))


def build(nc, x_in, w_in, p_in, moe1_in, moe2_in, resid, out):
    ctx = ExitStack()
    with ctx:
        def sb(name, shape, dt=F32, where=ctx):
            return where.enter_context(nc.sbuf_tensor(name, shape, dt))

        def sem(name):
            return ctx.enter_context(nc.semaphore(name))

        w_all = sb("w_all", [P, W_COLS])
        mlp0_at = -(-nc.sbuf_base // 32) * 32
        sb("mlp0_place", [P, W_ALL_COLS - W_COLS + 8])
        p_all = sb("p_all", [P, P_COLS])
        x_row = sb("x_row", [P, NT, D])
        xT = sb("xT", [P, KD, S + 1])
        neg_a = sb("neg_a", [P, MI * NS])
        ident_b = sb("ident_b", [P, P], BF16)
        mask_b = sb("mask_b", [P, 2, P], BF16)
        pick_r = sb("pick_r", [2 * 2 * NS, 2 * NS], F32R)
        out_bias = sb("out_bias", [P, D])
        ew_sum = sb("ew_sum", [P, NT])
        ln_stats = sb("ln_stats", [P, NT, 6])
        ln_mv = sb("ln_mv", [P, NT, 2])
        ln_std = sb("ln_std", [P, NT])
        ln_rstd = sb("ln_rstd", [P, NT])
        row_stats = sb("row_stats", [P, NT, 6])
        row_mv = sb("row_mv", [P, 2])
        row_q = sb("row_q", [P, 8])

        def weight(name, k=None):
            a, b = W_AT[name]
            v = w_all[:, a:b]
            return v if k is None else v.rearrange("p (k n) -> p k n", k=k)

        def param(name):
            a, b = P_AT[name]
            return p_all[:, a:b]

        ident = param("ident")

        arena_at = -(-nc.sbuf_base // 32) * 32
        arena_end = nc.sbuf_usable_end // 32 * 32
        sb("arena", [P, (arena_end - arena_at) // 4])

        def place(at, *buffers):
            views = []
            for name, shape, *dt in buffers:
                views.append(nc.alloc_sbuf_tensor_at(name, shape, dt[0] if dt else F32, offset=at))
                n = 4
                for extent in shape[1:]:
                    n *= extent
                at += -(-n // 32) * 32
            assert at <= arena_end, (at, arena_end)
            return views + [at]

        w_mlp0, = place(mlp0_at, ("w_mlp0", [P, W_ALL_COLS - W_COLS]))[:-1]
        k_odd, = place(mlp0_at, ("k_odd", [P, SLOTS, S], F32R))[:-1]
        w_up0 = w_mlp0[:, 0:KD * FF].rearrange("p (k n) -> p k n", k=KD)
        w_down0 = w_mlp0[:, KD * FF:].rearrange("p (k n) -> p k n", k=MF)

        _, moe1, moe2, moe_h, _ = place(
            arena_at, ("mix_place", [P, NT, D]), ("moe1", [P, KD, ME * P]), ("moe2", [P, ME, D]),
            ("moe_h", [P, 3, HALF]))

        (mix, raw, xm, delta, du, gate, dt_low, bc_parts, b_wide, decay, state, carry, mT, h0, _) = place(
            arena_at, ("mix", [P, NT, D]), ("raw", [P, MI, NCONV - 1 + HALF]), ("xm", [P, MI, HALF]),
            ("delta", [P, MI, HALF]), ("du", [P, MI, HALF]), ("gate", [P, TC, DI]), ("dt_low", [DTR, HALF]),
            ("bc_parts", [4 * NS, HALF], F32R), ("b_wide", [P, 3, HALF]), ("decay", [P, 2, MI, HALF]),
            ("state", [P, 3, MI, HALF]), ("carry", [P, NS, MI]), ("mT", [P, KD, HALF]), ("h0", [P, MF, HALF]))
        yT = xm

        (vals, z, rows, rden, seq, smax, body_at) = place(
            arena_at, ("vals", [P, NT * H * VC + VW], F32R), ("z", [P, NT, D]), ("rows", [P, 2, S], F32R),
            ("rden", [P, NT, 2]), ("seq", [P, NT, 2, DH]), ("smax", [P, NT, H]))
        vals_pad = vals[:, NT * H * VC:]
        vals_by_head = vals[:, 0:NT * H * VC].rearrange("p (t h s d) -> p t h s d", t=NT, h=H, s=2)
        even, odd, odd_hi = (rows[0:8, 0, :].bitcast(F32), rows[0:8, 1, 0:D].bitcast(F32),
                             rows[0:8, 1, D:2 * D].bitcast(F32))
        neg_hi, neg_lo = rows[32:34, 0, :], rows[32:34, 1, :]
        (xn1, pt1, pt2, outer, lines, norm, linesT, jlines, feat_w, feat_r, gsum, prod, gate_in, mem_in,
         gate8, _) = place(
            body_at, ("xn1", [P, NT, D]), ("pt1", [P, NT, 2 * 4 * H]), ("pt2", [P, NT, 2 * 4 * H]),
            ("outer", [P, 2, 2 * H, 4, 4]), ("lines", [P, NT, 2 * H, 6]), ("norm", [P, NT * 2 * H]),
            ("linesT", [6 * H, S]), ("jlines", [P, NT, H, 6]), ("feat_w", [P, NT, NPQ * H]),
            ("feat_r", [P, NT, NPQ * H]), ("gsum", [FR, 2, S + 1]), ("prod", [P, FCH, S]),
            ("gate_in", [P, NT, H]), ("mem_in", [P, NT, H]), ("gate8", [P, NT]))
        v_sum = feat_r[:, :, 0:D]
        qs, k_even, pt_at = place(body_at, ("qs", [P, SLOTS, S], F32R), ("k_even", [P, SLOTS, S], F32R))
        exps, exps_hi, *parts1, oT, _ = place(
            pt_at, ("exps", [P, RING_COLS]), ("exps_hi", [P, RING_COLS], F32R),
            *[(f"part1{i}", [P, S], F32R) for i in range(4)], ("oT", [P, S]))
        ks = [k_even, k_odd]
        exps_lo, _ = place(pt_at, ("exps_lo", [P, RING_COLS], F32R))
        *parts0, _ = place(pt_at, *[(f"part0{i}", [P, S], F32R) for i in range(4)])
        parts = [parts0, parts1]
        zT, g1, g2, h1, done, _ = place(
            body_at, ("zT", [P, KD, S]), ("g1", [P, KD, FF]), ("g2", [P, MF, D]), ("h1", [P, 3, HALF]),
            ("done", [P, NT // 2, 2, D]))

        ps = ctx.enter_context(nc.psum_tensor("ps", [P, 8, 512], F32))
        y_acc = ps[:, 0:4, :]
        pv_acc = ps[0:VW, 2:4, :].rearrange("p b n -> p (b n)")

        def acc_tile(tt):
            return ps[:, tt // 2, (tt % 2) * D:(tt % 2 + 1) * D]

        params_in = sem("params_in")
        weights_in = sem("weights_in")
        mlp0_in = sem("mlp0_in")
        moe_in = sem("moe_in")
        setup_v = sem("setup_v")
        setup_a = sem("setup_a")
        setup_p = sem("setup_p")
        round_done = sem("round_done")
        round_go = sem("round_go")
        round_seen = sem("round_seen")
        x_loaded = sem("x_loaded")
        chain_v = sem("chain_v")
        chain_a = sem("chain_a")
        chain_p = sem("chain_p")
        ring_filled = sem("ring_filled")
        drained_a = sem("drained_a")
        drained_v = sem("drained_v")
        ln_var = sem("ln_var")
        ln_sqrt = sem("ln_sqrt")
        xn_done = sem("xn_done")
        resid_in = sem("resid_in")
        resid_out = sem("resid_out")
        pad_zero = sem("pad_zero")
        tap_done = sem("tap_done")
        conv_done = sem("conv_done")
        silu_done = sem("silu_done")
        gate_done = sem("gate_done")
        bc_hi = sem("bc_hi")
        dt_done = sem("dt_done")
        dl_clamped = sem("dl_clamped")
        dl_log = sem("dl_log")
        du_done = sem("du_done")
        skip_done = sem("skip_done")
        decay_done = sem("decay_done")
        driven = sem("driven")
        scanned = sem("scanned")
        weighed = sem("weighed")
        state_read = sem("state_read")
        y_gated = sem("y_gated")
        h_read = sem("h_read")
        gelu_done = sem("gelu_done")
        tile_mixed = sem("tile_mixed")
        acc_read = sem("acc_read")
        row_sum = sem("row_sum")
        l1_clear = sem("l1_clear")
        rows_in = sem("rows_in")
        outer_done = sem("outer_done")
        lines_read = sem("lines_read")
        lines_sq = sem("lines_sq")
        lines_sqrt = sem("lines_sqrt")
        lines_done = sem("lines_done")
        feat_w_done = sem("feat_w_done")
        feat_r_done = sem("feat_r_done")
        sig_done = sem("sig_done")
        gates_read = sem("gates_read")
        k_odd_clear = sem("k_odd_clear")
        stacks_clear = sem("stacks_clear")
        pt_read = sem("pt_read")
        exps_hi_done = sem("exps_hi_done")
        exps_lo_v = sem("exps_lo_v")
        exps_lo_p = sem("exps_lo_p")
        v_summed = sem("v_summed")
        vals_hi = sem("vals_hi")
        vals_done = sem("vals_done")
        oT_done = sem("oT_done")
        seq_done = sem("seq_done")
        z_done = sem("z_done")
        out_sum = sem("out_sum")
        out_left = sem("out_left")
        q_in = [sem(f"q_in{g}") for g in range(NG)]
        k_in = [sem(f"k_in{g}") for g in range(NG)]
        neg_in = [sem(f"neg_in{g}") for g in range(NG)]
        per_round = [
            x_loaded, mlp0_in, chain_v, chain_a, chain_p, ring_filled, drained_a,
            drained_v, ln_var, ln_sqrt, xn_done, resid_in, pad_zero,
            tap_done, conv_done, silu_done, gate_done, bc_hi, dt_done,
            dl_clamped, dl_log, du_done, skip_done, decay_done, driven,
            scanned, weighed, state_read, y_gated, gelu_done, tile_mixed, h_read, acc_read,
            row_sum, l1_clear, rows_in, outer_done, lines_read, lines_sq,
            lines_sqrt, gates_read, lines_done, feat_w_done, feat_r_done, sig_done, k_odd_clear, stacks_clear,
            pt_read, exps_hi_done, exps_lo_v, exps_lo_p, v_summed, vals_hi,
            vals_done, oT_done, seq_done, z_done, out_sum, out_left] + q_in + k_in + neg_in

        def claim(plan, unit):
            banks, _, need, _ = plan[unit]
            if need["a"]:
                nc.tensor.wait_ge(drained_a, need["a"])
            if need["v"]:
                nc.tensor.wait_ge(drained_v, need["v"])
            return ps[:, banks[0]:banks[-1] + 1, :].rearrange("p b n -> p (b n)")

        def full(eng, plan, unit):
            banks, ready, _, _ = plan[unit]
            eng.wait_ge(ring_filled, ready)
            return ps[:, banks[0]:banks[-1] + 1, :].rearrange("p b n -> p (b n)")

        def drained(eng, plan, unit, who):
            eng.wait_ge(drained_a if who == "a" else drained_v, plan[unit][3][who])

        chain = {"v": 0, "a": 0, "p": 0}

        def link(who, ins):
            chain[who] += 1
            signal = {"v": chain_v, "a": chain_a, "p": chain_p}[who]
            ins.then_inc(signal, 1)
            {"v": nc.vector, "a": nc.scalar, "p": nc.gpsimd}[who].wait_ge(signal, chain[who])

        def end_round(eng, n, leader=False):
            chain.update(v=0, a=0, p=0)
            eng.sem_inc(round_done, 1)
            if leader:
                eng.wait_ge(round_done, 5)
                for one in per_round + [round_done]:
                    eng.sem_clear(one)
                eng.sem_inc(round_go, 1)
            else:
                eng.wait_ge(round_go, n)
                eng.sem_inc(round_seen, 1)

        def wide(ap, middle):
            return ap.unsqueeze(1).broadcast_to([ap.shape[0], middle, ap.shape[1]])

        def tokens(t, n=P, shift=1):
            return slice(shift + t * P, shift + t * P + n)

        def products(eng, dst, c6):
            by_q = dst[:, :, :].rearrange("p t (q h) -> p t q h", h=H)
            at = 0
            for p in range(6):
                n = 6 - p
                last = eng.tensor_tensor(by_q[:, :, at:at + n, :],
                                         c6[:, :, :, p].unsqueeze(2).broadcast_to([P, NT, n, H]),
                                         c6[:, :, :, p:6].rearrange("p t h q -> p t q h"), ALU.mult)
                at += n
            return last

        block = ctx.enter_context(nc.Block())

        @block.sync
        def _(sp):
            sp.dma_start(p_all[:, :], p_in).then_inc(params_in, 16)
            sp.dma_start(x_row[:, :, :], x_in[0].rearrange("(t p) d -> p t d", p=P)).then_inc(x_loaded, 16)
            sp.dma_start(moe1[:, :, :], moe1_in).then_inc(moe_in, 16)
            sp.dma_start(moe2[:, :, :], moe2_in).then_inc(moe_in, 16)
            sp.dma_start(w_all[:, :], w_in[:, 0:W_COLS]).then_inc(weights_in, 16)
            sp.dma_start(w_mlp0[:, :], w_in[:, W_COLS:]).then_inc(weights_in, 16)
            sp.dma_start(resid[1:B], x_in[1:B]).then_inc(resid_out, 16)
            sp.dma_start(resid[B], x_in[0]).then_inc(resid_out, 16)
            sp.wait_ge(x_loaded, 16)
            sp.wait_ge(acc_read, 2 * NC)
            sp.dma_start(resid[0].rearrange("(t p) d -> p t d", p=P), x_row[:, :, :]).then_inc(resid_out, 16)
            sp.wait_ge(resid_out, 48)
            end_round(sp, 1, leader=True)
            with sp.Fori(0, B) as b:
                sp.dma_start(x_row[:, :, :], resid[bass.ds(b, 1), :, :].rearrange("a (t p) d -> p (a t) d", p=P))\
                  .then_inc(resid_in, 16)
                sp.wait_ge(xn_done, 1)
                sp.wait_ge(l1_clear, 1)
                for r in range(8):
                    sp.dma_start(even[r:r + 1, (r % 4) * D:(r % 4 + 1) * D], xn1[1 + 2 * r:2 + 2 * r, 0, :])\
                      .then_inc(rows_in, 16)
                sp.dma_start(odd, xn1[2:18:2, 0, :]).then_inc(rows_in, 16)
                sp.dma_start(odd_hi[4:8, :], xn1[10:18:2, 0, :]).then_inc(rows_in, 16)
                sp.wait_ge(k_odd_clear, 1)
                sp.wait_ge(stacks_clear, 1)
                def stack(g):
                    group = g // 4
                    q_hi, q_lo, k_hi, k_lo = parts[group]
                    for i in range(2):
                        for who in "av":
                            drained(sp, ROW_PLAN, ("qk", group, i, 1), who)
                    if g >= SLOTS:
                        full(sp, ROW_PLAN, ("st", 2 * (g - SLOTS) + 1, LAST_TILE))
                        for row in (48, 112):
                            sp.dma_start(qs[row:row + 2, g % SLOTS, :].bitcast(F32),
                                         k_odd[0:2, g % SLOTS, :].bitcast(F32)).then_inc(q_in[g], 16)
                    for half in range(2):
                        for hi, lo, dst, signal, order in ((q_hi, q_lo, qs, q_in, "hhl"),
                                                           (k_hi, k_lo, ks[half], k_in, "hlh")):
                            j = 2 * (g % 4) + half
                            for r, part in enumerate(order):
                                src = hi if part == "h" else lo
                                row = 64 * half + DH * r
                                sp.dma_start(dst[row:row + DH, g % SLOTS, :].bitcast(F32),
                                             src[DH * j:DH * (j + 1), :].bitcast(F32)).then_inc(signal[g], 16)

                def maxima_rows(g):
                    for who in "av":
                        drained(sp, ROW_PLAN, ("mt", g), who)
                    for row, part in ((48, neg_hi), (49, neg_lo)):
                        sp.dma_start(qs[row:128:64, g % SLOTS, :].bitcast(F32), part.bitcast(F32))\
                          .then_inc(neg_in[g], 16)

                stack(0)
                stack(1)
                maxima_rows(0)
                stack(2)
                stack(3)
                maxima_rows(1)
                for g in range(2, NG):
                    maxima_rows(g)
                    if g + 2 < NG:
                        stack(g + 2)
                sp.wait_ge(pt_read, H * NT)
                sp.dma_start(mix[:, :, :], resid[bass.ds(b + 1, 1), :, :].rearrange("a (t p) d -> p (a t) d", p=P))\
                  .then_inc(x_loaded, 16)
                for i in range(NT // 2):
                    sp.wait_ge(out_sum, i + 1)
                    sp.dma_start(
                        out[bass.ds(b, 1), 2 * i * P:(2 * i + 2) * P, :].rearrange("a (t p) d -> p (a t) d", p=P),
                        done[:, i, :, :]).then_inc(out_left, 16)
                    if i == 0:
                        sp.dma_start(w_mlp0[:, :], w_in[:, W_COLS:]).then_inc(mlp0_in, 16)
                sp.wait_ge(out_left, 16 * (NT // 2))
                sp.wait_ge(mlp0_in, 16)
                end_round(sp, b + 2, leader=True)

        @block.tensor
        def _(pe):
            mm, tp = nc.tensor.matmul, nc.tensor.transpose

            def normalised_T(plan, prefix, xn, base):
                for unit in LN_UNITS:
                    _, c, k = unit
                    bank = claim(plan, prefix + unit)
                    if base is not None:
                        pe.wait_ge(xn_done, base + TC * (c + 1))
                    for tt in range(TC):
                        last = tp(bank[:, tt * P:(tt + 1) * P], xn[:, TC * c + tt, k * P:(k + 1) * P], ident)
                    last.then_inc(ring_filled, 1)

            def mlp(plan, tag, c, n_hidden, up, src, down, hidden, base, fresh):
                for m in range(n_hidden + 1):
                    if m < n_hidden:
                        bank = claim(plan, (tag, c, m))
                        for k in range(KD):
                            last = mm(bank, up[:, k, m * P:(m + 1) * P], src[k], start=(k == 0), stop=(k == KD - 1))
                        last.then_inc(ring_filled, 1)
                    if m >= 1:
                        j = m - 1
                        drained(pe, plan, (tag, c, j), "a")
                        for tt in range(TC):
                            last = mm(acc_tile(tt), hidden[:, (base + j) % 3, tt * P:(tt + 1) * P], down[:, j, :],
                                      start=(fresh and j == 0 and tt % 2 == 0), stop=(j == n_hidden - 1),
                                      skip_group_check=True)
                        last.then_inc(h_read, 1)

            pe.wait_ge(params_in, 16)
            normalised_T(MOE_PLAN, (), mix, 0)
            pe.wait_ge(moe_in, 32)
            for c in range(NC):
                drained(pe, MOE_PLAN, ("xt", c, 1), "a")
                if c:
                    pe.wait_ge(acc_read, 2 * c)
                mlp(MOE_PLAN, "h", c, ME, moe1, [xT[:, k, tokens(TC * c, HALF)] for k in range(KD)], moe2, moe_h,
                    ME * c, True)
            pe.wait_ge(weights_in, 32)
            pe.wait_ge(setup_a, 6)
            pe.wait_ge(setup_v, 3)
            end_round(pe, 1)

            def layer0(c):
                plan = ROW_PLAN
                w = weight("in", KD)
                drained(pe, plan, ("xt", c, 1), "a")
                for m in range(MI):
                    bank = claim(plan, ("xm", c, m))
                    for k in range(KD):
                        last = mm(bank, w[:, k, m * P:(m + 1) * P], xT[:, k, tokens(TC * c, HALF)],
                                  start=(k == 0), stop=(k == KD - 1))
                    last.then_inc(ring_filled, 1)
                for t in range(TC):
                    bank = claim(plan, ("res", c, t))
                    for k in range(KD):
                        last = mm(bank, xT[:, k, tokens(TC * c + t)], w[:, k, DI:2 * DI],
                                  start=(k == 0), stop=(k == KD - 1))
                    last.then_inc(ring_filled, 1)
                w = weight("xproj", MI)
                bank = claim(plan, ("xd", c))
                for m in range(MI):
                    pe.wait_ge(silu_done, MI * c + m + 1)
                    last = mm(bank[0:DTR + 2 * NS, :], w[:, m, :], xm[:, m, :], start=(m == 0), stop=(m == MI - 1))
                last.then_inc(ring_filled, 1)
                w = weight("dt")
                for m in range(MI):
                    bank = claim(plan, ("dl", c, m))
                    pe.wait_ge(dt_done, c + 1)
                    mm(bank, w[0:DTR, m * P:(m + 1) * P], dt_low[:, :], start=True, stop=True)\
                        .then_inc(ring_filled, 1)

                def spread(name, n):
                    bank = claim(plan, (name, c, n))
                    col = n if name == "B" else NS + n
                    mm(bank, pick_r[:, col:col + 1].broadcast_to([4 * NS, P]), bc_parts[:, :],
                       start=True, stop=True).then_inc(ring_filled, 1)

                def add_y(u):
                    for d in range(MI):
                        for t in range(TC):
                            last = mm(y_acc[:, t, d * P:(d + 1) * P],
                                      state[:, (c * (NS + 1) + u) % 3, d, t * P:(t + 1) * P], ident,
                                      is_transpose=True, start=(u == 0 and d == 0), stop=(u == NS),
                                      skip_group_check=True)
                    last.then_inc(state_read, 1)

                drained(pe, plan, ("xd", c), "v")
                for n in range(2):
                    spread("B", n)
                    spread("C", n)
                if c:
                    pe.wait_ge(y_gated, TC * c)
                pe.wait_ge(skip_done, c + 1)
                add_y(0)
                for n in range(NS):
                    if n + 2 < NS:
                        spread("B", n + 2)
                    step = fill(c, n)
                    if step and step[0] == "h":
                        mlp0_up(*step[1:])
                    elif step:
                        mlp0_down(*step[1:])
                    pe.wait_ge(weighed, c * NS + n + 1)
                    if n + 2 < NS:
                        spread("C", n + 2)
                    add_y(n + 1)
                for d in range(MI):
                    bank = claim(plan, ("yt", c, d))
                    for t in range(TC):
                        if d == 0:
                            pe.wait_ge(y_gated, TC * c + t + 1)
                        last = tp(bank[:, t * P:(t + 1) * P], gate[:, t, d * P:(d + 1) * P], ident)
                    last.then_inc(ring_filled, 1)
                w = weight("oproj", MI)
                drained(pe, plan, ("yt", c, MI - 1), "a")
                for k in range(KD):
                    bank = claim(plan, ("m", c, k))
                    for d in range(MI):
                        last = mm(bank, w[:, d, k * P:(k + 1) * P], yT[:, d, :], start=(d == 0), stop=(d == MI - 1))
                    last.then_inc(ring_filled, 1)
                drained(pe, plan, ("m", c, KD - 1), "a")
                if c == NC - 1:
                    for m in range(MF):
                        mlp0_up(c, m)
                    for t in range(TC):
                        mlp0_down(c, t)

            def mlp0_up(c, m):
                bank = claim(ROW_PLAN, ("h", c, m))
                for k in range(KD):
                    last = mm(bank, w_up0[:, k, m * P:(m + 1) * P], mT[:, k, :], start=(k == 0), stop=(k == KD - 1))
                last.then_inc(ring_filled, 1)

            def mlp0_down(c, t):
                bank = claim(ROW_PLAN, ("o", c, t))
                for k in range(KD):
                    mm(bank[:, k * P:(k + 1) * P], mT[:, k, t * P:(t + 1) * P], ident, is_transpose=True,
                       start=(k == 0), stop=False, skip_group_check=True)
                pe.wait_ge(gelu_done, c + 1)
                for m in range(MF):
                    last = mm(bank[:, 0:D], h0[:, m, t * P:(t + 1) * P], w_down0[:, m, :], start=False,
                              stop=(m == MF - 1), skip_group_check=True)
                last.then_inc(ring_filled, 1)

            def attention():
                plan = ROW_PLAN
                u = 0
                for e in EVENTS:
                    kind, h = e[0], e[1]
                    g = h // 2
                    if kind == "sm":
                        it = e[2]
                        both = claim(plan, e)
                        if it == 0 and h % 2 == 0:
                            pe.wait_ge(q_in[g], 96 if g < SLOTS else 128)
                            pe.wait_ge(k_in[g], 96)
                        width = (it + 1) * P
                        for at in range(0, width, HALF):
                            n = min(HALF, width - at)
                            mm(both[:, at:at + n], qs[:, g % SLOTS, it * P:(it + 1) * P],
                               ks[h % 2][:, g % SLOTS, at:at + n], start=True, stop=(at + n < width),
                               skip_group_check=True)
                        mm(both[:, it * P:width], ident_b[:, :], mask_b[:, 0, :], start=False, stop=True,
                           skip_group_check=True).then_inc(ring_filled, 1)
                    elif kind == "mt":
                        g = e[1]
                        both = claim(plan, e)
                        drained(pe, plan, ("sm", 2 * g + 1, LAST_TILE), "v")
                        for it in range(NT):
                            last = tp(both[0:2, it * P:(it + 1) * P], smax[:, it, 2 * g:2 * g + 2], ident)
                        last.then_inc(ring_filled, 1)
                    elif kind == "st":
                        jt = e[2]
                        both = claim(plan, e)
                        if jt == 0 and h % 2 == 0:
                            pe.wait_ge(neg_in[g], 32)
                        width = (NT - jt) * P
                        for at in range(0, width, HALF):
                            n = min(HALF, width - at)
                            mm(both[:, at:at + n], ks[h % 2][:, g % SLOTS, jt * P:(jt + 1) * P],
                               qs[:, g % SLOTS, jt * P + at:jt * P + at + n], start=True, stop=(at > 0),
                               skip_group_check=True)
                        mm(both[:, 0:P], ident_b[:, :], mask_b[:, 1, :], start=False, stop=True,
                           skip_group_check=True).then_inc(ring_filled, 1)
                    elif kind == "pv":
                        jt = e[2]
                        if u == 0:
                            pe.wait_ge(vals_done, 1)
                        pe.wait_ge(exps_hi_done, u + 1)
                        first = (jt * H + h) * VC
                        start = EXPS_AT[u][0] - jt * P
                        for part in (exps_hi, exps_lo):
                            if part is exps_lo:
                                if jt in LO_POOL:
                                    pe.wait_ge(exps_lo_p, lo_count(u + 1, "p"))
                                else:
                                    pe.wait_ge(exps_lo_v, lo_count(u + 1, "v"))
                            for at in (0, HALF):
                                lo = max(at, jt * P)
                                if jt == 0 and h and part is exps_hi:
                                    pe.wait_ge(oT_done, 2 * h - 1 + (at > 0))
                                if lo < at + HALF:
                                    last = mm(pv_acc[:, lo:at + HALF], vals[:, first:first + VW],
                                              part[:, start + lo:start + at + HALF],
                                              start=(jt == 0 and part is exps_hi),
                                              stop=(jt == (LAST_TILE if at else TC - 1) and part is exps_lo),
                                              skip_group_check=True)
                        last.then_inc(pt_read, 1)
                        u += 1
                    elif kind == "ot":
                        g = e[1]
                        both = claim(plan, e)
                        pe.wait_ge(oT_done, 4 * (g + 1))
                        for t in range(NT):
                            last = mm(both[:, t * VC:(t + 1) * VC], oT[:, t * P:(t + 1) * P], param("sel"),
                                      start=(t == 0), stop=(t == NT - 1), skip_group_check=True)
                        last.then_inc(ring_filled, 1)

            def layer1():
                plan = ROW_PLAN
                normalised_T(plan, ("1",), xn1, 0)
                ta, tb = weight("ta", KD), weight("tb", KD)
                for t in range(NT):
                    if t % TC == 0:
                        drained(pe, plan, ("1", "xt", t // TC, 1), "a")
                    bank = claim(plan, ("pa", t))
                    for k in range(KD):
                        last = mm(bank[:, 0:464], xT[:, k, tokens(t)], ta[:, k, :], start=(k == 0), stop=(k == KD - 1))
                    last.then_inc(ring_filled, 1)
                    bank = claim(plan, ("pb", t))
                    for k in range(KD):
                        mm(bank[:, 0:D], xT[:, k, tokens(t)], tb[:, k, 0:D], start=(k == 0), stop=(k == KD - 1),
                           skip_group_check=True)
                    for k in range(KD):
                        last = mm(bank[:, D:D + 64], xT[:, k, tokens(t, shift=0)], tb[:, k, D:D + 64],
                                  start=(k == 0), stop=(k == KD - 1), skip_group_check=True)
                    last.then_inc(ring_filled, 1)
                for c in range(NC):
                    bank = claim(plan, ("lt", c))
                    pe.wait_ge(lines_done, 1)
                    for tt in range(TC):
                        last = tp(bank[0:6 * H, tt * P:(tt + 1) * P],
                                  lines[:, TC * c + tt, 0:H, :].rearrange("p h j -> p (h j)"), ident)
                    last.then_inc(ring_filled, 1)
                for c in range(NC):
                    bank = claim(plan, ("jw", c))
                    drained(pe, plan, ("lt", c), "a")
                    for tt in range(TC):
                        last = mm(bank[:, tt * 96:(tt + 1) * 96], linesT[:, (TC * c + tt) * P:(TC * c + tt + 1) * P],
                                  param("jdiag")[0:96, :], start=True, stop=True)
                    last.then_inc(ring_filled, 1)
                pe.wait_ge(feat_r_done, 1)
                pe.wait_ge(feat_w_done, 1)
                for ch in range(FCH):
                    for c in range(NC):
                        for name, feat in (("fw", feat_w), ("fr", feat_r)):
                            bank = claim(plan, (name, ch, c))
                            for tt in range(TC):
                                last = tp(bank[0:FR, tt * P:(tt + 1) * P],
                                          feat[:, TC * c + tt, ch * FR:(ch + 1) * FR], ident)
                            last.then_inc(ring_filled, 1)
                w = weight("qk", KD)

                def project(g):
                    for i in range(2):
                        for c in range(NC):
                            bank = claim(plan, ("qk", g, i, c))
                            for k in range(KD):
                                last = mm(bank, w[:, k, i * D + g * P:i * D + (g + 1) * P],
                                          xT[:, k, tokens(TC * c, HALF)], start=(k == 0), stop=(k == KD - 1))
                            last.then_inc(ring_filled, 1)

                project(0)
                bank = claim(plan, ("ms",))
                drained(pe, plan, ("fr", FCH - 1, NC - 1), "v")
                pick = param("sumpq").rearrange("p (c h) -> p c h", c=FCH)
                for t in range(NT):
                    for ch in range(FCH):
                        last = mm(bank[:, t * H:(t + 1) * H], prod[0:FR, ch, t * P:(t + 1) * P], pick[0:FR, ch, :],
                                  start=(ch == 0), stop=(ch == FCH - 1))
                last.then_inc(ring_filled, 1)
                project(1)
                attention()
                for c in range(NC):
                    for k in range(KD):
                        bank = claim(plan, ("zt", k, c))
                        pe.wait_ge(z_done, 1)
                        for tt in range(TC):
                            last = tp(bank[:, tt * P:(tt + 1) * P], z[:, TC * c + tt, k * P:(k + 1) * P], ident)
                        last.then_inc(ring_filled, 1)
                pe.wait_ge(rows_in, 160)
                for k in range(KD):
                    for c in range(NC):
                        bank = claim(plan, ("e1", k, c))
                        mm(bank, odd[0:4, k * P:(k + 1) * P], even[0:4, c * HALF:(c + 1) * HALF],
                           start=True, stop=True).then_inc(ring_filled, 1)
                by_c = even[:, :].rearrange("e (r i c) -> e c r i", r=4, c=4)
                for q in range(MF // 2):
                    bank = claim(plan, ("e2", q))
                    for j in range(2):
                        last = mm(bank[:, j * D:(j + 1) * D].rearrange("p (r i) -> p r i", r=4),
                                  odd_hi[:, j * P:(j + 1) * P], by_c[:, q], start=True, stop=True)
                    last.then_inc(ring_filled, 1)
                for c in range(NC):
                    if c:
                        pe.wait_ge(acc_read, 2 * c)
                    else:
                        drained(pe, plan, ("st", H - 1, LAST_TILE), "a")
                        drained(pe, plan, ("sm", H - 1, LAST_TILE), "v")
                    drained(pe, plan, ("zt", 1, c), "a")
                    for tt in range(TC):
                        for k in range(KD):
                            mm(acc_tile(tt), zT[:, k, (TC * c + tt) * P:(TC * c + tt + 1) * P],
                               weight("out", KD)[:, k, :], start=(tt % 2 == 0 and k == 0), stop=False,
                               skip_group_check=True)
                    drained(pe, plan, ("e2", MF // 2 - 1), "v")
                    mlp(plan, "g", c, MF, g1, [xT[:, k, tokens(TC * c, HALF)] for k in range(KD)], g2, h1,
                        MF * c, False)

            with pe.Fori(0, B) as b:
                normalised_T(ROW_PLAN, (), mix, None)
                for c in range(NC):
                    layer0(c)
                bank = claim(ROW_PLAN, ("mu",))
                pe.wait_ge(row_sum, 1)
                mm(bank[:, 0:1], param("mean"), row_mv[:, 0:1], start=True, stop=True).then_inc(ring_filled, 1)
                bank = claim(ROW_PLAN, ("var",))
                pe.wait_ge(row_sum, 2)
                mm(bank[:, 0:1], param("mean"), row_q[:, 1:2], start=True, stop=True).then_inc(ring_filled, 1)
                layer1()
                end_round(pe, b + 2)

        @block.scalar
        def _(act):
            def f(out_, in_, func, **kw):
                return nc.scalar.activation(out_, in_, func, **kw)

            def deviation(n):
                act.wait_ge(ln_var, n)
                f(ln_std[:, :], ln_std[:, :], ACT.Sqrt).then_inc(ln_sqrt, 1)

            def keep_xT(plan, prefix):
                for unit in LN_UNITS:
                    _, c, k = unit
                    bank = full(act, plan, prefix + unit)
                    f(xT[:, k, tokens(TC * c, HALF)], bank, ACT.Copy).then_inc(drained_a, 1)

            def hidden(plan, tag, c, n_hidden, func, bias, dst, base):
                for m in range(n_hidden):
                    bank = full(act, plan, (tag, c, m))
                    if base + m >= 3:
                        act.wait_ge(h_read, base + m - 2)
                    kw = {"bias": bias[:, m:m + 1]} if bias is not None else {}
                    f(dst[:, (base + m) % 3, :], bank, func, **kw).then_inc(drained_a, 1)

            act.wait_ge(params_in, 16)
            f(ident_b[:, :], ident, ACT.Copy).then_inc(setup_a, 1)
            f(mask_b[:, 0, :], param("mask"), ACT.Copy).then_inc(setup_a, 1)
            f(mask_b[:, 1, :], param("maskt"), ACT.Copy).then_inc(setup_a, 1)
            f(pick_r[:, :], param("pick")[0:4 * NS, :], ACT.Copy).then_inc(setup_a, 1)
            f(neg_a[:, :], param("alog"), ACT.Exp).then_inc(setup_a, 1)
            act.wait_ge(setup_a, 5)
            f(neg_a[:, :], neg_a[:, :], ACT.Copy, scale=-1.0).then_inc(setup_a, 1)
            deviation(1)
            keep_xT(MOE_PLAN, ())
            for c in range(NC):
                hidden(MOE_PLAN, "h", c, ME, ACT.Gelu_apprx_tanh, None, moe_h, ME * c)
            act.wait_ge(setup_a, 6)
            end_round(act, 1)

            def layer0(c):
                plan = ROW_PLAN
                if c:
                    act.wait_ge(conv_done, 3 * MI)
                    f(raw[:, :, 0:NCONV - 1], raw[:, :, HALF:HALF + NCONV - 1], ACT.Copy).then_inc(pad_zero, 1)
                act.wait_ge(pad_zero, c + 1)
                taps = param("convw").rearrange("p (m k) -> p m k", m=MI)
                for m in range(MI):
                    bank = full(act, plan, ("xm", c, m))
                    f(raw[:, m, NCONV - 1:], bank, ACT.Copy).then_inc(tap_done, 1)
                    f(xm[:, m, :], bank, ACT.Identity, scale=taps[:, m, NCONV - 1:NCONV],
                      bias=param("convb")[:, m:m + 1]).then_inc(drained_a, 1)
                for t in range(TC):
                    bank = full(act, plan, ("res", c, t))
                    if t == 0 and c:
                        drained(act, plan, ("yt", c - 1, MI - 1), "a")
                    f(gate[:, t, :], bank, ACT.Silu).then_inc(drained_a, 1)
                for m in range(MI):
                    act.wait_ge(conv_done, 3 * MI * c + 2 * MI + m + 1)
                    f(xm[:, m, :], xm[:, m, :], ACT.Silu).then_inc(silu_done, 1)
                bank = full(act, plan, ("xd", c))
                f(bc_parts[0:2 * NS, :], bank[DTR:DTR + 2 * NS, :], ACT.Copy).then_inc(bc_hi, 1)
                for m in range(MI):
                    act.wait_ge(dl_clamped, MI * c + m + 1)
                    link("a", f(du[:, m, :], du[:, m, :], ACT.Exp))
                for m in range(MI):
                    f(du[:, m, :], du[:, m, :], ACT.Ln, bias=1.0).then_inc(dl_log, 1)

                def b_wide_copy(n):
                    j = c * NS + n
                    bank = full(act, plan, ("B", c, n))
                    if j >= 3:
                        act.wait_ge(driven, j - 2)
                    f(b_wide[:, j % 3, :], bank, ACT.Copy).then_inc(drained_a, 1)

                b_wide_copy(0)
                drained(act, plan, ("dl", c, MI - 1), "v")
                for n in range(NS):
                    j = c * NS + n
                    if j >= 2:
                        act.wait_ge(scanned, MI * (j - 1))
                    for d in range(MI):
                        f(decay[:, j % 2, d, :], delta[:, d, :], ACT.Exp,
                          scale=neg_a[:, d * NS + n:d * NS + n + 1]).then_inc(decay_done, 1)
                    if n + 1 < NS:
                        b_wide_copy(n + 1)
                    step = fill(c, n - 1) if n else None
                    if step and step[0] == "h":
                        m = step[2]
                        f(h0[:, m, :], full(act, plan, step), ACT.Identity, bias=param("fb1")[:, m:m + 1])\
                            .then_inc(drained_a, 1)
                    if c and n == MF:
                        drained(act, plan, ("h", c - 1, MF - 1), "a")
                        f(h0[:, :, :], h0[:, :, :], ACT.Gelu).then_inc(gelu_done, 1)
                for d in range(MI):
                    bank = full(act, plan, ("yt", c, d))
                    f(yT[:, d, :], bank, ACT.Copy).then_inc(drained_a, 1)
                for k in range(KD):
                    bank = full(act, plan, ("m", c, k))
                    f(mT[:, k, :], bank, ACT.Copy).then_inc(drained_a, 1)
                if c == NC - 1:
                    for m in range(MF):
                        ins = f(h0[:, m, :], full(act, plan, ("h", c, m)), ACT.Gelu, bias=param("fb1")[:, m:m + 1])
                        ins.then_inc(drained_a, 1)
                    drained(act, plan, ("h", c, MF - 1), "a")
                    act.sem_inc(gelu_done, 1)

            def attention():
                plan = ROW_PLAN
                u = 0
                for e in EVENTS:
                    if e[0] == "mt":
                        g = e[1]
                        both = full(act, plan, e)
                        if g:
                            act.wait_ge(neg_in[g - 1], 32)
                        f(neg_hi, both[0:2, :], ACT.Copy, scale=-1.0).then_inc(drained_a, 1)
                    elif e[0] == "st":
                        h, jt = e[1], e[2]
                        both = full(act, plan, e)
                        if u == 0:
                            for slot in range(SLOTS):
                                act.wait_ge(q_in[slot], 96)
                                act.wait_ge(k_in[slot], 96)
                        at, width, used = EXPS_AT[u]
                        if used:
                            act.wait_ge(pt_read, used)
                        f(exps[:, at:at + width], both[:, 0:width], ACT.Exp,
                          scale=float(DH) ** -0.5).then_inc(drained_a, 1)
                        drained(act, plan, e, "a")
                        f(exps_hi[:, at:at + width], exps[:, at:at + width], ACT.Copy)\
                            .then_inc(exps_hi_done, 1)
                        u += 1

            def layer1():
                plan = ROW_PLAN
                deviation(2)
                keep_xT(plan, ("1",))
                for t in range(NT):
                    bank = full(act, plan, ("pa", t))
                    f(pt1[:, t, 64:128], bank[:, D:D + 64], ACT.Copy).then_inc(tap_done, 1)
                    f(pt2[:, t, :], bank[:, D + 64:D + 192], ACT.Copy).then_inc(drained_a, 1)
                    bank = full(act, plan, ("pb", t))
                    f(pt1[:, t, 0:64], bank[:, D:D + 64], ACT.Copy).then_inc(drained_a, 1)
                act.wait_ge(lines_sq, 1)
                f(norm[:, :], norm[:, :], ACT.Sqrt).then_inc(lines_sqrt, 1)
                for c in range(NC):
                    bank = full(act, plan, ("lt", c))
                    f(linesT[:, c * HALF:(c + 1) * HALF], bank[0:6 * H, :], ACT.Copy).then_inc(drained_a, 1)
                for c in range(NC):
                    bank = full(act, plan, ("jw", c))
                    f(jlines[:, TC * c:TC * (c + 1), :, :].rearrange("p t h j -> p (t h j)"), bank[:, 0:TC * 6 * H],
                      ACT.Copy).then_inc(drained_a, 1)

                def keep_hi(g):
                    for i, hi in enumerate((parts[g][0], parts[g][2])):
                        for c in range(NC):
                            bank = full(act, plan, ("qk", g, i, c))
                            f(hi[:, c * HALF:(c + 1) * HALF], bank, ACT.Identity,
                              bias=param("qkb")[:, 2 * i + g:2 * i + g + 1]).then_inc(drained_a, 1)

                keep_hi(0)
                drained(act, plan, ("ms",), "v")
                f(mem_in[:, :, :], mem_in[:, :, :], ACT.Sigmoid).then_inc(sig_done, 1)
                f(gate_in[:, :, :], gate_in[:, :, :], ACT.Sigmoid).then_inc(sig_done, 1)
                act.wait_ge(gates_read, 1)
                keep_hi(1)
                attention()
                for c in range(NC):
                    for k in range(KD):
                        bank = full(act, plan, ("zt", k, c))
                        f(zT[:, k, c * HALF:(c + 1) * HALF], bank, ACT.Copy).then_inc(drained_a, 1)
                deviation(3)
                for c in range(NC):
                    hidden(plan, "g", c, MF, ACT.Gelu, param("gb1"), h1, MF * c)

            with act.Fori(0, B) as b:
                keep_xT(ROW_PLAN, ())
                for c in range(NC):
                    layer0(c)
                act.wait_ge(ln_var, 1)
                f(row_q[:, 2:3], row_q[:, 2:3], ACT.Sqrt).then_inc(ln_sqrt, 1)
                layer1()
                end_round(act, b + 2)

        @block.vector
        def _(dve):
            V = nc.vector

            def normalise(x, xn, n):
                for t in range(NT):
                    last = V.bn_stats(ln_stats[:, t, :], x[:, t, :])
                link("v", last)
                for t in range(NT):
                    last = V.bn_aggr(ln_mv[:, t, :], ln_stats[:, t, :])
                link("v", last)
                V.tensor_scalar(ln_std[:, :], ln_mv[:, :, 1], EPS, None, ALU.add).then_inc(ln_var, 1)
                dve.wait_ge(ln_sqrt, n)
                link("v", V.reciprocal(ln_rstd[:, :], ln_std[:, :]))
                for t in range(NT):
                    V.tensor_scalar(xn[:, t, :], x[:, t, :], ln_mv[:, t, 0:1], ln_rstd[:, t:t + 1], ALU.subtract,
                                    ALU.mult).then_inc(xn_done, 1)

            V.memset(xT[:, :, 0:1], 0.0).then_inc(setup_v, 1)
            dve.wait_ge(params_in, 16)
            V.tensor_tensor(out_bias[:, :], param("outb"), param("gb2"), ALU.add).then_inc(setup_v, 1)
            ew = param("ew").rearrange("p (t k) -> p t k", k=2)
            V.tensor_tensor(ew_sum[:, :], ew[:, :, 0], ew[:, :, 1], ALU.add).then_inc(setup_v, 1)
            dve.wait_ge(setup_v, 3)
            dve.wait_ge(x_loaded, 16)
            normalise(x_row, mix, 1)
            for c in range(NC):
                dve.wait_ge(h_read, ME * (c + 1))
                for tt in range(TC):
                    t = TC * c + tt
                    ins = V.scalar_tensor_tensor(x_row[:, t, :], acc_tile(tt), ew_sum[:, t:t + 1], x_row[:, t, :],
                                                 ALU.mult, ALU.add)
                    if tt % 2:
                        ins.then_inc(acc_read, 1)
            dve.wait_ge(acc_read, 2 * NC)
            end_round(dve, 1)

            def layer0(c):
                plan = ROW_PLAN
                taps = param("convw").rearrange("p (m k) -> p m k", m=MI)
                for k in range(NCONV - 1):
                    for m in range(MI):
                        step = 3 * MI * c + MI * k + m
                        if k == 0:
                            drained(dve, plan, ("xm", c, m), "a")
                        else:
                            dve.wait_ge(conv_done, step + 1 - MI)
                        V.scalar_tensor_tensor(xm[:, m, :], raw[:, m, k:k + HALF], taps[:, m, k:k + 1], xm[:, m, :],
                                               ALU.mult, ALU.add).then_inc(conv_done, 1)
                bank = full(dve, plan, ("xd", c))
                dve.wait_ge(bc_hi, c + 1)
                V.tensor_copy(dt_low[:, :], bank[0:DTR, :]).then_inc(dt_done, 1)
                V.tensor_tensor(bc_parts[2 * NS:4 * NS, :], bank[DTR:DTR + 2 * NS, :],
                                bc_parts[0:2 * NS, :].bitcast(F32), ALU.subtract).then_inc(drained_v, 1)
                bias = param("dtb")
                for m in range(MI):
                    bank = full(dve, plan, ("dl", c, m))
                    V.tensor_scalar(du[:, m, :], bank, bias[:, m:m + 1], CAP, ALU.add, ALU.min)\
                        .then_inc(dl_clamped, 1)
                for m in range(MI):
                    bank = full(dve, plan, ("dl", c, m))
                    dve.wait_ge(dl_log, MI * c + m + 1)
                    V.scalar_tensor_tensor(delta[:, m, :], bank, bias[:, m:m + 1], du[:, m, :], ALU.add, ALU.max)\
                        .then_inc(drained_v, 1)
                for m in range(MI):
                    drained(dve, plan, ("dl", c, m), "v")
                    V.tensor_tensor(du[:, m, :], delta[:, m, :], xm[:, m, :], ALU.mult).then_inc(du_done, 1)
                for n in range(NS):
                    j = c * NS + n
                    slot = (c * (NS + 1) + n + 1) % 3
                    dve.wait_ge(driven, j + 1)
                    for d in range(MI):
                        dve.wait_ge(decay_done, MI * j + d + 1)
                        V.tensor_tensor_scan(state[:, slot, d, :], decay[:, j % 2, d, :], state[:, slot, d, :],
                                             carry[:, n, d:d + 1] if c else 0.0, ALU.mult, ALU.add)\
                            .then_inc(scanned, 1)
                    dve.wait_ge(scanned, MI * (j + 1))
                    if c == 0:
                        link("v", V.tensor_copy(carry[:, n, :], state[:, slot, :, HALF - 1]))
                    bank = full(dve, plan, ("C", c, n))
                    V.tensor_tensor(state[:, slot, :, :], state[:, slot, :, :], wide(bank, MI), ALU.mult)\
                        .then_inc(weighed, 1)
                    dve.wait_ge(weighed, j + 1)
                    dve.sem_inc(drained_v, 1)
                    step = fill(c, n - 1) if n else None
                    if step and step[0] == "o":
                        mixed(*step[1:])
                dve.wait_ge(state_read, (c + 1) * (NS + 1))
                for t in range(TC):
                    V.tensor_tensor(gate[:, t, :], y_acc[:, t, :], gate[:, t, :], ALU.mult).then_inc(y_gated, 1)
                if c == NC - 1:
                    for t in range(TC):
                        mixed(c, t)

            def mixed(c, tt):
                t = TC * c + tt
                bank = full(dve, ROW_PLAN, ("o", c, tt))
                V.tensor_tensor(mix[:, t, :], bank[:, 0:D], param("fb2"), ALU.add).then_inc(drained_v, 1)
                drained(dve, ROW_PLAN, ("o", c, tt), "v")
                V.bn_stats(row_stats[:, t, :], mix[:, t, :]).then_inc(tile_mixed, 1)

            def finish_layer0():
                dve.wait_ge(tile_mixed, NT)
                V.bn_aggr(row_mv[:, :], row_stats[:, :, :].rearrange("p a b -> p (a b)")).then_inc(row_sum, 1)
                bank = full(dve, ROW_PLAN, ("mu",))
                dve.wait_ge(row_sum, 1)
                V.tensor_copy(row_q[:, 0:1], bank[:, 0:1]).then_inc(drained_v, 1)
                drained(dve, ROW_PLAN, ("mu",), "v")
                link("v", V.tensor_tensor(row_q[:, 4:5], row_mv[:, 0:1], row_q[:, 0:1], ALU.subtract))
                V.scalar_tensor_tensor(row_q[:, 1:2], row_q[:, 4:5], row_q[:, 4:5], row_mv[:, 1:2], ALU.mult,
                                       ALU.add).then_inc(row_sum, 1)
                bank = full(dve, ROW_PLAN, ("var",))
                V.tensor_scalar(row_q[:, 2:3], bank[:, 0:1], EPS, None, ALU.add).then_inc(drained_v, 1)
                drained(dve, ROW_PLAN, ("var",), "v")
                dve.sem_inc(ln_var, 1)
                dve.wait_ge(ln_sqrt, 1)
                link("v", V.reciprocal(row_q[:, 3:4], row_q[:, 2:3]))
                for t in range(NT):
                    last = V.tensor_scalar(mix[:, t, :], mix[:, t, :], row_q[:, 0:1], row_q[:, 3:4], ALU.subtract,
                                           ALU.mult)
                link("v", last)
                dve.wait_ge(resid_in, 16)
                link("v", V.tensor_tensor(x_row[:, :, :], x_row[:, :, :], mix[:, :, :], ALU.add))

            def line_coordinates(t):
                dve.wait_ge(outer_done, t + 1)
                o = outer[:, t % 2]
                at = 0
                for i in range(3):
                    last = V.tensor_tensor(lines[:, t, :, at:at + 3 - i], o[:, :, i, i + 1:4], o[:, :, i + 1:4, i],
                                           ALU.subtract)
                    at += 3 - i
                last.then_inc(lines_read, 1)

            def keep_lo(g):
                for i, (hi, lo) in enumerate((parts[g][0:2], parts[g][2:4])):
                    for c in range(NC):
                        bank = full(dve, ROW_PLAN, ("qk", g, i, c))
                        drained(dve, ROW_PLAN, ("qk", g, i, c), "a")
                        half = slice(c * HALF, (c + 1) * HALF)
                        V.scalar_tensor_tensor(lo[:, half], bank, param("qkb")[:, 2 * i + g:2 * i + g + 1],
                                               hi[:, half].bitcast(F32), ALU.add, ALU.subtract)\
                            .then_inc(drained_v, 1)

            def memory():
                plan = ROW_PLAN
                V.memset(gsum[:, :, 0:1], 0.0)
                for t in range(NT):
                    bank = full(dve, plan, ("pa", t))
                    drained(dve, plan, ("pa", t), "a")
                    V.tensor_tensor(v_sum[:, t, :], bank[:, 0:D], param("vb"), ALU.add).then_inc(v_summed, 1)
                    V.tensor_tensor(gate_in[:, t, :], bank[:, 448:464], param("mgb"), ALU.add)\
                        .then_inc(drained_v, 1)
                    bank = full(dve, plan, ("pb", t))
                    drained(dve, plan, ("pb", t), "a")
                    V.tensor_tensor(z[:, t, :], bank[:, 0:D], param("mvb"), ALU.add).then_inc(drained_v, 1)
                    if t >= 1:
                        line_coordinates(t - 1)
                line_coordinates(NT - 1)
                dve.wait_ge(lines_read, NT)
                square = feat_w[:, :, 0:2 * H * 6].rearrange("p t (h j) -> p t h j", j=6)
                flat = "p t h j -> p (t h) j"
                link("v", V.tensor_tensor(square, lines[:, :, :, :], lines[:, :, :, :], ALU.mult))
                V.tensor_reduce(norm[:, :].rearrange("p (t h) -> p t h", t=NT), square, AX_X, ALU.add)\
                    .then_inc(lines_sq, 1)
                dve.wait_ge(lines_sqrt, 1)
                link("v", V.tensor_scalar(norm[:, :], norm[:, :], 1e-12, None, ALU.max))
                link("v", V.reciprocal(norm[:, :], norm[:, :]))
                V.tensor_tensor(lines[:, :, :, :].rearrange(flat), lines[:, :, :, :].rearrange(flat),
                                norm[:, :].unsqueeze(2).broadcast_to([P, NT * 2 * H, 6]), ALU.mult)\
                    .then_inc(lines_done, 1)
                drained(dve, plan, ("jw", NC - 1), "a")
                products(V, feat_w, jlines[:, :, :, :]).then_inc(feat_w_done, 1)
                dve.wait_ge(feat_w_done, 1)
                rate = param("decay")[0:FR, :]
                for ch in range(FCH):
                    for c in range(NC):
                        bank = full(dve, plan, ("fw", ch, c))
                        g = gsum[:, ch % 2]
                        V.tensor_tensor_scan(g[:, 1 + c * HALF:1 + (c + 1) * HALF],
                                             rate.broadcast_to([FR, HALF]), bank[0:FR, :],
                                             g[:, HALF:HALF + 1] if c else 0.0, ALU.mult, ALU.add)\
                            .then_inc(drained_v, 1)
                        drained(dve, plan, ("fw", ch, c), "v")
                        bank = full(dve, plan, ("fr", ch, c))
                        V.scalar_tensor_tensor(prod[0:FR, ch, c * HALF:(c + 1) * HALF], g[:, c * HALF:(c + 1) * HALF],
                                               rate, bank[0:FR, :], ALU.mult, ALU.mult).then_inc(drained_v, 1)
                keep_lo(0)
                bank = full(dve, plan, ("ms",))
                V.tensor_tensor(mem_in[:, :, :], bank[:, 0:NT * H].rearrange("p (t h) -> p t h", t=NT),
                                wide(param("mscale"), NT), ALU.mult).then_inc(drained_v, 1)
                dve.wait_ge(sig_done, 2)
                link("v", V.tensor_tensor(mem_in[:, :, :], mem_in[:, :, :], gate_in[:, :, :], ALU.mult))
                link("v", V.tensor_reduce(gate8[:, :], mem_in[:, :, :], AX_X, ALU.add))
                link("v", V.tensor_scalar(gate8[:, :], gate8[:, :], 1.0 / H, None, ALU.mult))
                for t in range(NT):
                    last = V.tensor_scalar(z[:, t, :], z[:, t, :], gate8[:, t:t + 1], None, ALU.mult)
                last.then_inc(gates_read, 1)
                dve.wait_ge(gates_read, 1)

            def attention():
                plan = ROW_PLAN
                u = made = 0
                for e in EVENTS:
                    kind = e[0]
                    if kind == "sm":
                        h, it = e[1], e[2]
                        both = full(dve, plan, e)
                        V.tensor_reduce(smax[:, it, h:h + 1], both[:, 0:(it + 1) * P], AX_X, ALU.max)\
                            .then_inc(drained_v, 1)
                    elif kind == "lo":
                        if e[2] not in LO_POOL:
                            dve.wait_ge(exps_hi_done, made + 1)
                            at, width, _ = EXPS_AT[made]
                            V.tensor_tensor(exps_lo[:, at:at + width], exps[:, at:at + width],
                                            exps_hi[:, at:at + width].bitcast(F32), ALU.subtract)\
                                .then_inc(exps_lo_v, 1)
                        made += 1
                    elif kind == "mt":
                        drained(dve, plan, e, "a")
                        V.scalar_tensor_tensor(neg_lo, full(dve, plan, e)[0:2, :], -1.0,
                                               neg_hi.bitcast(F32), ALU.mult, ALU.subtract)\
                            .then_inc(drained_v, 1)
                    elif kind == "pv":
                        h, jt = e[1], e[2]
                        u += 1
                        if jt in (TC - 1, LAST_TILE):
                            half = slice(0, HALF) if jt < TC else slice(HALF, S)
                            dve.wait_ge(pt_read, u)
                            if h >= 2 and h % 2 == 0 and jt < TC:
                                full(dve, plan, ("ot", h // 2 - 1))
                            V.tensor_copy(oT[VW * (h % 2):VW * (h % 2 + 1), half], pv_acc[:, half])\
                                .then_inc(oT_done, 1)
                    elif kind == "ot":
                        g = e[1]
                        bank = full(dve, plan, e)[:, 0:NT * VC].rearrange("p (t h d) -> p t h d", t=NT, h=2)
                        link("v", V.reciprocal(rden[:, :, :], bank[:, :, :, DH]))
                        V.tensor_tensor(seq[:, :, :, :], bank[:, :, :, 0:DH],
                                        rden[:, :, :].unsqueeze(3).broadcast_to([P, NT, 2, DH]), ALU.mult)\
                            .then_inc(drained_v, 1)
                        drained(dve, plan, e, "v")
                        part = z[:, :, g * 2 * DH:(g + 1) * 2 * DH]
                        last = V.tensor_tensor(part, part, seq[:, :, :, :].rearrange("p t h d -> p t (h d)"), ALU.add)
                last.then_inc(z_done, 1)

            def layer1():
                plan = ROW_PLAN
                normalise(x_row, xn1, 2)
                memory()
                keep_lo(1)
                attention()
                scale = param("scale")
                w1, w2 = weight("g1", KD), weight("g2", MF)
                for k in range(KD):
                    for c in range(NC):
                        bank = full(dve, plan, ("e1", k, c))
                        half = slice(c * HALF, (c + 1) * HALF)
                        V.scalar_tensor_tensor(g1[:, k, half], bank, scale, w1[:, k, half], ALU.mult, ALU.add)\
                            .then_inc(drained_v, 1)
                for q in range(MF // 2):
                    bank = full(dve, plan, ("e2", q))
                    V.scalar_tensor_tensor(g2[:, 2 * q:2 * q + 2, :], bank.rearrange("p (k n) -> p k n", k=2), scale,
                                           w2[:, 2 * q:2 * q + 2, :], ALU.mult, ALU.add).then_inc(drained_v, 1)
                link("v", V.tensor_tensor(x_row[:, :, :], x_row[:, :, :], wide(out_bias[:, :], NT), ALU.add))
                dve.wait_ge(x_loaded, 16)
                normalise(mix, mix, 3)
                dve.wait_ge(xn_done, 2 * NT)
                for c in range(NC):
                    dve.wait_ge(h_read, MF * (c + 1))
                    for a in range(2):
                        i = 2 * c + a
                        V.tensor_tensor(done[:, i, :, :], ps[:, a, :].rearrange("p (t d) -> p t d", t=2),
                                        x_row[:, 2 * i:2 * i + 2, :], ALU.add).then_inc(out_sum, 1)
                        dve.wait_ge(out_sum, i + 1)
                        dve.sem_inc(acc_read, 1)

            with dve.Fori(0, B) as b:
                V.memset(raw[:, :, 0:NCONV - 1], 0.0).then_inc(pad_zero, 1)
                for c in range(NC):
                    layer0(c)
                finish_layer0()
                layer1()
                end_round(dve, b + 2)

        @block.gpsimd
        def _(pool):
            G = nc.gpsimd
            end_round(pool, 1)

            def layer0(c):
                plan = ROW_PLAN
                w = c * (NS + 1)
                pool.wait_ge(silu_done, MI * (c + 1))
                if c:
                    pool.wait_ge(state_read, w - 2)
                for d in range(MI):
                    last = G.tensor_scalar(state[:, w % 3, d, :], xm[:, d, :], param("dskip")[:, d:d + 1], None,
                                           ALU.mult)
                last.then_inc(skip_done, 1)
                pool.wait_ge(du_done, MI * (c + 1))
                for n in range(NS):
                    j, w = c * NS + n, c * (NS + 1) + n + 1
                    drained(pool, plan, ("B", c, n), "a")
                    if w >= 3:
                        pool.wait_ge(state_read, w - 2)
                    G.tensor_tensor(state[:, w % 3, :, :], du[:, :, :], wide(b_wide[:, j % 3, :], MI), ALU.mult)\
                        .then_inc(driven, 1)

            def layer1():
                plan = ROW_PLAN
                pool.wait_ge(xn_done, 1)
                link("p", G.memset(k_odd[0:64, :, :].bitcast(F32), 0.0))
                G.memset(k_odd[64:128, :, :].bitcast(F32), 1.0).then_inc(k_odd_clear, 1)
                pool.wait_ge(k_odd_clear, 1)
                G.memset(odd_hi, 0.0)
                G.memset(even, 0.0).then_inc(l1_clear, 1)
                G.memset(vals_by_head[:, :, :, 0, DH].bitcast(F32), 1.0)
                G.memset(vals_by_head[:, :, :, 1, DH].bitcast(F32), 0.0)
                G.memset(vals_pad.bitcast(F32), 0.0)
                for t in range(NT):
                    drained(pool, plan, ("pb", t), "a")
                    if t >= 2:
                        pool.wait_ge(lines_read, t - 1)
                    a = pt1[:, t, :].rearrange("p (l i) -> p l i", i=4)
                    b = pt2[:, t, :].rearrange("p (l i) -> p l i", i=4)
                    G.tensor_tensor(outer[:, t % 2], a.unsqueeze(3).broadcast_to([P, 2 * H, 4, 4]),
                                    b.unsqueeze(2).broadcast_to([P, 2 * H, 4, 4]), ALU.mult)\
                        .then_inc(outer_done, 1)
                by_head = v_sum.rearrange("p t (h d) -> p t h d", h=H)
                pool.wait_ge(v_summed, NT)
                G.tensor_copy(vals_by_head[:, :, :, 0, 0:DH], by_head).then_inc(vals_hi, 1)
                pool.wait_ge(vals_hi, 1)
                G.tensor_tensor(vals_by_head[:, :, :, 1, 0:DH], by_head,
                                vals_by_head[:, :, :, 0, 0:DH].bitcast(F32), ALU.subtract).then_inc(vals_done, 1)
                pool.wait_ge(vals_done, 1)
                pool.wait_ge(lines_done, 1)
                products(G, feat_r, lines[:, :, H:2 * H, :]).then_inc(feat_r_done, 1)
                pool.wait_ge(feat_r_done, 1)
                pool.wait_ge(feat_w_done, 1)
                pool.wait_ge(rows_in, 160)
                link("p", G.memset(qs[:, :, :].bitcast(F32), 0.0))
                link("p", G.memset(k_even[64:128, :, :].bitcast(F32), 0.0))
                G.memset(k_even[32:64, :, :].bitcast(F32), 1.0).then_inc(stacks_clear, 1)
                pool.wait_ge(stacks_clear, 1)
                for u, (_, _, jt) in enumerate(EXPS):
                    if jt in LO_POOL:
                        pool.wait_ge(exps_hi_done, u + 1)
                        at, width, _ = EXPS_AT[u]
                        G.tensor_tensor(exps_lo[:, at:at + width], exps[:, at:at + width],
                                        exps_hi[:, at:at + width].bitcast(F32), ALU.subtract)\
                            .then_inc(exps_lo_p, 1)

            with pool.Fori(0, B) as b:
                for c in range(NC):
                    layer0(c)
                layer1()
                end_round(pool, b + 2)


def _slices(w):
    k = w.shape[0] // P
    return w.reshape(k, P, -1).transpose(1, 0, 2).reshape(P, -1)


def _cols(v):
    return v.reshape(-1, P).T


def kernel(**inputs):
    import numpy as np
    import concourse.bacc as bacc
    from concourse.bass_utils import run_bass_kernel_spmd

    a = {k: np.asarray(v) for k, v in inputs.items()}
    f32 = np.float32

    def everywhere(v):
        return np.broadcast_to(v.reshape(1, -1), (P, v.size))

    def padded(m):
        out = np.zeros((P, m.shape[1]), f32)
        out[:m.shape[0]] = m
        return out

    qkv, in_w = a["L1_attn_qkv_w"], a["L0_attn_in_proj_w"]
    w = {
        "in": _slices(in_w.T), "xproj": _slices(a["L0_attn_x_proj_w"].T), "dt": padded(a["L0_attn_dt_proj_w"].T),
        "oproj": _slices(a["L0_attn_out_proj_w"].T), "f1": _slices(a["L0_attn_ffn_w1"].T),
        "f2": _slices(a["L0_attn_ffn_w2"].T), "qk": _slices(qkv[:, 0:2 * D]),
        "ta": _slices(np.concatenate([qkv[:, 2 * D:], a["L1_attn_w1_read"], a["L1_attn_w2_write"],
                                      a["L1_attn_w2_read"], a["L1_attn_memg_w"]], 1)),
        "tb": _slices(np.concatenate([a["L1_attn_memv_w"], a["L1_attn_w1_write"]], 1)),
        "out": _slices(a["L1_attn_out_w"]), "g1": _slices(a["L1_ffn_W1"].T), "g2": _slices(a["L1_ffn_W2"].T),
    }
    jdiag = np.zeros((P, 6 * H), f32)
    for h in range(H):
        jdiag[6 * h:6 * h + 6, 6 * h:6 * h + 6] = a["L1_attn_J"]
    sumpq = np.zeros((P, FCH, H), f32)
    pairs = [(i, j) for i in range(6) for j in range(i, 6)]
    for n, (i, j) in enumerate(pairs):
        for h in range(H):
            sumpq[(n % 7) * H + h, n // 7, h] = 1.0 if i == j else 2.0
    pick = np.zeros((P, 2 * NS), f32)
    for n in range(2 * NS):
        pick[n, n] = pick[2 * NS + n, n] = 1.0
    sel = np.zeros((P, VC), f32)
    for h in range(2):
        for i in range(2):
            for d in range(DH + 1):
                sel[VW * h + i * (DH + 1) + d, h * (DH + 1) + d] = 1.0
    above = np.triu(np.full((P, P), -1e30, f32), 1)
    rate = np.zeros((P, 1), f32)
    for n in range(7):
        rate[n * H:(n + 1) * H, 0] = a["L1_attn_decays"]
    qkv_b = a["L1_attn_qkv_b"]
    p = {
        "convw": a["L0_attn_conv_w"].reshape(MI, P, NCONV).transpose(1, 0, 2).reshape(P, -1),
        "convb": _cols(a["L0_attn_conv_b"]), "dtb": _cols(a["L0_attn_dt_proj_b"]), "alog": _slices(a["L0_attn_A_log"]),
        "dskip": _cols(a["L0_attn_D"]), "fb1": _cols(a["L0_attn_ffn_b1"]), "qkb": _cols(qkv_b[0:2 * D]),
        "gb1": _cols(a["L1_ffn_b1"]), "scale": everywhere(a["L1_ffn_scale"]), "decay": rate,
        "fb2": everywhere(a["L0_attn_ffn_b2"]), "vb": everywhere(qkv_b[2 * D:]),
        "mvb": everywhere(a["L1_attn_memv_b"]), "mgb": everywhere(a["L1_attn_memg_b"]),
        "mscale": everywhere(a["L1_attn_mem_scale"]), "outb": everywhere(a["L1_attn_out_b"]),
        "gb2": everywhere(a["L1_ffn_b2"]), "jdiag": jdiag, "ident": np.eye(P, dtype=f32), "mask": above,
        "sel": sel, "maskt": above.T, "sumpq": sumpq.reshape(P, -1), "pick": pick, "mean": np.full((P, P), 1.0 / P, f32),
        "ew": a["L0_ffn_expert_weights"].reshape(NT, P, 2).transpose(1, 0, 2).reshape(P, -1),
    }
    arrays = {
        "x": a["L0_attn_seq_embeddings"],
        "weights": np.concatenate([w[n] for n, _ in WEIGHTS], 1),
        "params": np.concatenate([p[n] for n, _ in PARAMS], 1),
        "expert1": a["L0_ffn_w1"].reshape(KD, P, ME * P).transpose(1, 0, 2),
        "expert2": a["L0_ffn_w2"].reshape(ME, P, D).transpose(1, 0, 2),
    }
    arrays = {f"in_{k}": np.ascontiguousarray(v) for k, v in arrays.items()}
    nc = bacc.Bacc("TRN2", target_bir_lowering=False, num_devices=1)
    args = [nc.dram_tensor(k, v.shape, mybir.dt.from_np(v.dtype), kind="ExternalInput").ap()
            for k, v in arrays.items()]
    resid = nc.dram_tensor("resid", (B + 1, S, D), F32, kind="Internal").ap()
    out = nc.dram_tensor("out", (B, S, D), F32, kind="ExternalOutput").ap()
    build(nc, *args, resid, out)
    return run_bass_kernel_spmd(nc, [arrays], core_ids=[0]).results[0]["out"]
```
